# Optimizing a Trainium2 kernel written in Bass

```python
import numpy as np
import jax
import jax.numpy as jnp

def _softmax(x, axis=-1):
    return jax.nn.softmax(x, axis=axis)

def _gelu(x):
    return jax.nn.gelu(x, approximate=True)

def _silu(x):
    return jax.nn.silu(x)

def _sigmoid(x):
    return jax.nn.sigmoid(x)

def _layernorm(x, axis=-1, eps=1e-05):
    m = jnp.mean(x, axis=axis, keepdims=True)
    v = jnp.var(x, axis=axis, keepdims=True)
    return (x - m) / jnp.sqrt(v + eps)

def _scatter_add(tgt, idx, src, axis=0):
    return tgt.at[idx].add(src)

def _segment_sum(src, seg, n):
    return jax.ops.segment_sum(src, seg, n)
kernel_name = 'mk_gnn_ffn_d2_gnn_r32_ee9ba3'

def setup_inputs(seed: int=0):
    np.random.seed(seed)
    _w = jnp.asarray

    def _rec_inputs():
        import jax
        import jax.numpy as jnp
        _gk = jax.random.key(seed)
        x = -0.0002117 + 1 * jax.random.normal(jax.random.fold_in(_gk, 1), (3125, 256), jnp.float32)
        src = jax.random.randint(jax.random.fold_in(_gk, 2), (50000,), 0, 3125, jnp.int32)
        dst = jax.random.randint(jax.random.fold_in(_gk, 3), (50000,), 0, 3125, jnp.int32)
        _o = jnp.argsort(dst, stable=True)
        src = src[_o]
        dst = dst[_o]
        edge_type_32 = jax.random.randint(jax.random.fold_in(_gk, 12), (50000,), 0, 32, jnp.int32)
        edge_weight1 = jax.random.uniform(jax.random.fold_in(_gk, 13), (50000, 1), jnp.float32, 0.0, 0.999998)
        return (x, src, dst, edge_type_32, edge_weight1)
    x, src, dst, edge_type_32, edge_weight1 = _rec_inputs()

    def _L0_gnn_setup():
        import jax, jax.numpy as jnp
        import numpy as np
        N_NODES = 3125
        N_EDGES = 100000
        IN_CH = 256
        OUT_CH = 256
        key = jax.random.key(seed)
        k1, k2, k3, k4, k5 = jax.random.split(key, 5)
        x = jax.random.normal(k1, (N_NODES, IN_CH), dtype=jnp.float32)
        src = jax.random.randint(k2, (N_EDGES,), 0, N_NODES, dtype=jnp.int64)
        dst = jax.random.randint(k3, (N_EDGES,), 0, N_NODES, dtype=jnp.int64)
        bound = 1.0 / np.sqrt(IN_CH)
        weight = jax.random.uniform(k4, (IN_CH, OUT_CH), minval=-bound, maxval=bound, dtype=jnp.float32)
        bias = jax.random.uniform(k5, (OUT_CH,), minval=-bound, maxval=bound, dtype=jnp.float32)
        return {'x': x, 'src': src, 'dst': dst, 'weight': weight, 'bias': bias}
    _L0_gnn_all = _L0_gnn_setup()
    _L0_gnn_in = {k: v for k, v in _L0_gnn_all.items() if k in ('weight', 'bias')}
    del _L0_gnn_all

    def _L0_ffn_setup():
        import jax, jax.numpy as jnp
        import numpy as np
        B, N, D = (16, 128, 256)
        NUM_EXPERTS, TOP_K, HEADS = (4, 2, 4)
        N_EDGES = 32768
        LN_EPS = 1e-05

        def _layernorm(x, g, b):
            mu = x.mean(-1, keepdims=True)
            var = ((x - mu) ** 2).mean(-1, keepdims=True)
            return (x - mu) * jax.lax.rsqrt(var + LN_EPS) * g + b

        def _forward(x, edge_index, W_gat, att_src, att_dst, b_gat, ln_gamma, ln_beta, W1, b1, W2, b2):
            Bc, Nc, Dc = x.shape
            M = Bc * Nc
            x_flat = x.reshape(M, Dc)
            h = (x_flat @ W_gat).reshape(M, HEADS, NUM_EXPERTS)
            loops = jnp.arange(M, dtype=edge_index.dtype)
            src = jnp.concatenate([edge_index[0], loops])
            dst = jnp.concatenate([edge_index[1], loops])
            a_src = (h * att_src).sum(-1)
            a_dst = (h * att_dst).sum(-1)
            e = jax.nn.leaky_relu(a_src[src] + a_dst[dst], negative_slope=0.2)
            e_max = jax.ops.segment_max(e, dst, num_segments=M)
            ee = jnp.exp(e - e_max[dst])
            denom = jax.ops.segment_sum(ee, dst, num_segments=M)
            alpha = ee / (denom[dst] + 1e-16)
            msg = h[src] * alpha[:, :, None]
            agg = jax.ops.segment_sum(msg, dst, num_segments=M).reshape(M, HEADS * NUM_EXPERTS) + b_gat
            scores = _layernorm(agg, ln_gamma, ln_beta).reshape(M, HEADS, NUM_EXPERTS).mean(1)
            scores = scores.reshape(Bc, Nc, NUM_EXPERTS)
            topk_s, topk_i = jax.lax.top_k(scores, TOP_K)
            w = jax.nn.softmax(topk_s, axis=-1)
            out = jnp.zeros_like(x)
            for ei in range(NUM_EXPERTS):
                g = jnp.where(topk_i == ei, w, 0.0).sum(-1)
                hh = jax.nn.gelu(x @ W1[ei] + b1[ei], approximate=False)
                out = out + g[..., None] * (hh @ W2[ei] + b2[ei])
            return out
        key = jax.random.key(seed)
        ks = jax.random.split(key, 8)
        s = 0.05
        return {'x': jax.random.normal(ks[0], (B, N, D), jnp.float32), 'W_gat': jax.random.normal(ks[1], (D, HEADS * NUM_EXPERTS), jnp.float32) * s, 'att_src': jax.random.normal(ks[2], (HEADS, NUM_EXPERTS), jnp.float32) * s, 'att_dst': jax.random.normal(ks[3], (HEADS, NUM_EXPERTS), jnp.float32) * s, 'b_gat': jnp.zeros((HEADS * NUM_EXPERTS,), jnp.float32), 'ln_gamma': jnp.ones((HEADS * NUM_EXPERTS,), jnp.float32), 'ln_beta': jnp.zeros((HEADS * NUM_EXPERTS,), jnp.float32), 'W1': jax.random.normal(ks[4], (NUM_EXPERTS, D, 2 * D), jnp.float32) * s, 'b1': jnp.zeros((NUM_EXPERTS, 2 * D), jnp.float32), 'W2': jax.random.normal(ks[5], (NUM_EXPERTS, 2 * D, D), jnp.float32) * s, 'b2': jnp.zeros((NUM_EXPERTS, D), jnp.float32), 'edge_index': jax.random.randint(ks[6], (2, N_EDGES), 0, B * N, jnp.int32)}
    _L0_ffn_all = _L0_ffn_setup()
    _L0_ffn_in = {k: v for k, v in _L0_ffn_all.items() if k in ('W_gat', 'att_src', 'att_dst', 'b_gat', 'ln_gamma', 'ln_beta', 'W1', 'b1', 'W2', 'b2', 'edge_index')}
    del _L0_ffn_all

    def _L1_gnn_setup():
        import jax, jax.numpy as jnp
        import numpy as np
        N_NODES = 625
        N_EDGES = 10000
        IN_DIM = 256
        OUT_DIM = 256
        NUM_RELS = 32
        NUM_BASES = 8
        key = jax.random.key(seed)
        k1, k2, k3, k4, k5, k6, k7 = jax.random.split(key, 7)
        h = jax.random.normal(k1, (N_NODES, IN_DIM), dtype=jnp.float32)
        src = jax.random.randint(k2, (N_EDGES,), 0, N_NODES, dtype=jnp.int32)
        dst = jax.random.randint(k3, (N_EDGES,), 0, N_NODES, dtype=jnp.int32)
        rel_type = jax.random.randint(k4, (N_EDGES,), 0, NUM_RELS, dtype=jnp.int32)
        norm = jax.random.uniform(k5, (N_EDGES, 1), dtype=jnp.float32)
        scale_w = np.sqrt(2.0) * np.sqrt(6.0 / (IN_DIM + OUT_DIM))
        bases = jax.random.uniform(k6, (NUM_BASES, IN_DIM, OUT_DIM), dtype=jnp.float32, minval=-scale_w, maxval=scale_w)
        scale_c = np.sqrt(2.0) * np.sqrt(6.0 / (NUM_RELS + NUM_BASES))
        w_comp = jax.random.uniform(k7, (NUM_RELS, NUM_BASES), dtype=jnp.float32, minval=-scale_c, maxval=scale_c)
        return {'h': h, 'src': src, 'dst': dst, 'rel_type': rel_type, 'norm': norm, 'bases': bases, 'w_comp': w_comp}
    _L1_gnn_all = _L1_gnn_setup()
    _L1_gnn_in = {k: v for k, v in _L1_gnn_all.items() if k in ('bases', 'w_comp')}
    del _L1_gnn_all

    def _L1_ffn_setup():
        import math
        import jax, jax.numpy as jnp
        import numpy as np
        CAPACITY_FACTOR = 1.25
        TOP_K = 2
        LN_EPS = 1e-05

        def _layer_norm(x, gamma, beta):
            mu = jnp.mean(x, axis=-1, keepdims=True)
            var = jnp.var(x, axis=-1, keepdims=True)
            return (x - mu) * jax.lax.rsqrt(var + LN_EPS) * gamma + beta
        key = jax.random.key(seed)
        ks = jax.random.split(key, 4)
        B, S, D, F, E = (8, 128, 256, 512, 8)
        x = jax.random.normal(ks[0], (B, S, D), dtype=jnp.float32)
        Wr = jax.random.normal(ks[1], (D, E), dtype=jnp.float32) / np.sqrt(D)
        br = jnp.zeros((E,), jnp.float32)
        W1 = jax.random.normal(ks[2], (E, D, F), dtype=jnp.float32) / np.sqrt(D)
        b1 = jnp.zeros((E, F), jnp.float32)
        W2 = jax.random.normal(ks[3], (E, F, D), dtype=jnp.float32) / np.sqrt(F)
        b2 = jnp.zeros((E, D), jnp.float32)
        gamma = jnp.ones((D,), jnp.float32)
        beta = jnp.zeros((D,), jnp.float32)
        return {'x': x, 'Wr': Wr, 'br': br, 'W1': W1, 'b1': b1, 'W2': W2, 'b2': b2, 'gamma': gamma, 'beta': beta}
    _L1_ffn_all = _L1_ffn_setup()
    _L1_ffn_in = {k: v for k, v in _L1_ffn_all.items() if k in ('Wr', 'br', 'W1', 'b1', 'W2', 'b2', 'gamma', 'beta')}
    del _L1_ffn_all
    return {'x': x, 'src': src, 'dst': dst, 'edge_type_32': edge_type_32, 'edge_weight1': edge_weight1, 'L0_gnn_weight': _L0_gnn_in['weight'], 'L0_gnn_bias': _L0_gnn_in['bias'], 'L0_ffn_W_gat': _L0_ffn_in['W_gat'], 'L0_ffn_att_src': _L0_ffn_in['att_src'], 'L0_ffn_att_dst': _L0_ffn_in['att_dst'], 'L0_ffn_b_gat': _L0_ffn_in['b_gat'], 'L0_ffn_ln_gamma': _L0_ffn_in['ln_gamma'], 'L0_ffn_ln_beta': _L0_ffn_in['ln_beta'], 'L0_ffn_W1': _L0_ffn_in['W1'], 'L0_ffn_b1': _L0_ffn_in['b1'], 'L0_ffn_W2': _L0_ffn_in['W2'], 'L0_ffn_b2': _L0_ffn_in['b2'], 'L0_ffn_edge_index': _L0_ffn_in['edge_index'], 'L1_gnn_bases': _L1_gnn_in['bases'], 'L1_gnn_w_comp': _L1_gnn_in['w_comp'], 'L1_ffn_Wr': _L1_ffn_in['Wr'], 'L1_ffn_br': _L1_ffn_in['br'], 'L1_ffn_W1': _L1_ffn_in['W1'], 'L1_ffn_b1': _L1_ffn_in['b1'], 'L1_ffn_W2': _L1_ffn_in['W2'], 'L1_ffn_b2': _L1_ffn_in['b2'], 'L1_ffn_gamma': _L1_ffn_in['gamma'], 'L1_ffn_beta': _L1_ffn_in['beta']}

def reference(x, src, dst, edge_type_32, edge_weight1, L0_gnn_weight, L0_gnn_bias, L0_ffn_W_gat, L0_ffn_att_src, L0_ffn_att_dst, L0_ffn_b_gat, L0_ffn_ln_gamma, L0_ffn_ln_beta, L0_ffn_W1, L0_ffn_b1, L0_ffn_W2, L0_ffn_b2, L0_ffn_edge_index, L1_gnn_bases, L1_gnn_w_comp, L1_ffn_Wr, L1_ffn_br, L1_ffn_W1, L1_ffn_b1, L1_ffn_W2, L1_ffn_b2, L1_ffn_gamma, L1_ffn_beta):
    import jax
    import jax.numpy as jnp

    def _L0_gnn_ref(x, src, dst, weight, bias):
        import jax, jax.numpy as jnp
        import numpy as np
        N_NODES = 3125
        N_EDGES = 100000
        IN_CH = 256
        OUT_CH = 256
        h = jnp.matmul(x, weight) + bias
        agg = jax.ops.segment_sum(h[src], dst, num_segments=N_NODES)
        deg = jax.ops.segment_sum(jnp.ones((src.shape[0],), dtype=h.dtype), dst, num_segments=N_NODES)
        deg = jnp.maximum(deg, 1.0)[:, None]
        return agg / deg

    def _L0_ffn_ref(x, W_gat, att_src, att_dst, b_gat, ln_gamma, ln_beta, W1, b1, W2, b2, edge_index):
        import jax, jax.numpy as jnp
        import numpy as np
        B, N, D = (16, 128, 256)
        NUM_EXPERTS, TOP_K, HEADS = (4, 2, 4)
        N_EDGES = 32768
        LN_EPS = 1e-05

        def _layernorm(x, g, b):
            mu = x.mean(-1, keepdims=True)
            var = ((x - mu) ** 2).mean(-1, keepdims=True)
            return (x - mu) * jax.lax.rsqrt(var + LN_EPS) * g + b

        def _forward(x, edge_index, W_gat, att_src, att_dst, b_gat, ln_gamma, ln_beta, W1, b1, W2, b2):
            Bc, Nc, Dc = x.shape
            M = Bc * Nc
            x_flat = x.reshape(M, Dc)
            h = (x_flat @ W_gat).reshape(M, HEADS, NUM_EXPERTS)
            loops = jnp.arange(M, dtype=edge_index.dtype)
            src = jnp.concatenate([edge_index[0], loops])
            dst = jnp.concatenate([edge_index[1], loops])
            a_src = (h * att_src).sum(-1)
            a_dst = (h * att_dst).sum(-1)
            e = jax.nn.leaky_relu(a_src[src] + a_dst[dst], negative_slope=0.2)
            e_max = jax.ops.segment_max(e, dst, num_segments=M)
            ee = jnp.exp(e - e_max[dst])
            denom = jax.ops.segment_sum(ee, dst, num_segments=M)
            alpha = ee / (denom[dst] + 1e-16)
            msg = h[src] * alpha[:, :, None]
            agg = jax.ops.segment_sum(msg, dst, num_segments=M).reshape(M, HEADS * NUM_EXPERTS) + b_gat
            scores = _layernorm(agg, ln_gamma, ln_beta).reshape(M, HEADS, NUM_EXPERTS).mean(1)
            scores = scores.reshape(Bc, Nc, NUM_EXPERTS)
            topk_s, topk_i = jax.lax.top_k(scores, TOP_K)
            w = jax.nn.softmax(topk_s, axis=-1)
            out = jnp.zeros_like(x)
            for ei in range(NUM_EXPERTS):
                g = jnp.where(topk_i == ei, w, 0.0).sum(-1)
                hh = jax.nn.gelu(x @ W1[ei] + b1[ei], approximate=False)
                out = out + g[..., None] * (hh @ W2[ei] + b2[ei])
            return out
        return _forward(x, edge_index, W_gat, att_src, att_dst, b_gat, ln_gamma, ln_beta, W1, b1, W2, b2)

    def _L1_gnn_ref(h, src, dst, rel_type, norm, bases, w_comp):
        import jax, jax.numpy as jnp
        import numpy as np
        N_NODES = 625
        N_EDGES = 10000
        IN_DIM = 256
        OUT_DIM = 256
        NUM_RELS = 32
        NUM_BASES = 8
        weight = jnp.einsum('rb,bio->rio', w_comp, bases)
        xw = jnp.einsum('ni,rio->nro', h, weight)
        msg = xw[src, rel_type] * norm
        out = jax.ops.segment_sum(msg, dst, num_segments=h.shape[0])
        return jax.nn.relu(out)

    def _L1_ffn_ref(x, Wr, br, W1, b1, W2, b2, gamma, beta):
        import math
        import jax, jax.numpy as jnp
        import numpy as np
        CAPACITY_FACTOR = 1.25
        TOP_K = 2
        LN_EPS = 1e-05

        def _layer_norm(x, gamma, beta):
            mu = jnp.mean(x, axis=-1, keepdims=True)
            var = jnp.var(x, axis=-1, keepdims=True)
            return (x - mu) * jax.lax.rsqrt(var + LN_EPS) * gamma + beta
        B, S, D = x.shape
        E = Wr.shape[1]
        N = B * S
        K = TOP_K
        logits = jnp.mean(x, axis=1) @ Wr + br
        routing_weights = jax.nn.softmax(logits, axis=-1)
        capacity = float(math.ceil(N * CAPACITY_FACTOR / E))
        expected_loads = routing_weights.sum(axis=0) * (N / B)
        scale = jnp.where(expected_loads > capacity, capacity / expected_loads, 1.0)
        routing_weights = jax.nn.softmax(routing_weights * scale, axis=-1)
        rw_tok = jnp.broadcast_to(routing_weights[:, None, :], (B, S, E)).reshape(N, E)
        top_w, top_i = jax.lax.top_k(rw_tok, K)
        top_w = jax.nn.softmax(top_w, axis=-1)
        xf = x.reshape(N, D)
        h = jax.nn.gelu(jnp.einsum('nd,edf->enf', xf, W1) + b1[:, None, :], approximate=False)
        y = jnp.einsum('enf,efd->end', h, W2) + b2[:, None, :]
        w_dense = jnp.zeros((N, E), x.dtype).at[jnp.arange(N)[:, None], top_i].add(top_w)
        out = jnp.einsum('ne,end->nd', w_dense, y).reshape(B, S, D)
        out = _layer_norm(out + x, gamma, beta)
        return out
    x = x + _L0_gnn_ref(_layernorm(x, axis=-1), src, dst, L0_gnn_weight, L0_gnn_bias)
    x = x + _L0_ffn_ref(_layernorm(x, axis=-1)[None], L0_ffn_W_gat, L0_ffn_att_src, L0_ffn_att_dst, L0_ffn_b_gat, L0_ffn_ln_gamma, L0_ffn_ln_beta, L0_ffn_W1, L0_ffn_b1, L0_ffn_W2, L0_ffn_b2, L0_ffn_edge_index)[0]
    x = x + _L1_gnn_ref(_layernorm(x, axis=-1), src, dst, edge_type_32, edge_weight1, L1_gnn_bases, L1_gnn_w_comp)
    x = x + _L1_ffn_ref(_layernorm(x, axis=-1)[None], L1_ffn_Wr, L1_ffn_br, L1_ffn_W1, L1_ffn_b1, L1_ffn_W2, L1_ffn_b2, L1_ffn_gamma, L1_ffn_beta)[0]
    return x

_drawn_inputs = setup_inputs


def setup_inputs(seed=0):
    import zlib

    import numpy as np

    out = dict(_drawn_inputs(seed))
    spreads = {'L0_ffn_b_gat': (0.0, 0.1),
     'L0_ffn_ln_gamma': (1.0, 0.2),
     'L0_ffn_ln_beta': (0.0, 0.1),
     'L0_ffn_b1': (0.0, 0.1),
     'L0_ffn_b2': (0.0, 0.1),
     'L1_ffn_br': (0.0, 0.1),
     'L1_ffn_b1': (0.0, 0.553),
     'L1_ffn_b2': (0.0, 0.408),
     'L1_ffn_gamma': (1.0, 0.2),
     'L1_ffn_beta': (0.0, 0.272)}
    factors = {}
    for name, (base, spread) in spreads.items():
        noise = np.random.default_rng([zlib.crc32(name.encode()), seed]).standard_normal(out[name].shape)
        drawn = base * np.exp(spread * noise) if base else spread * noise
        out[name] = jnp.asarray(drawn.astype(out[name].dtype))
    for name, factor in factors.items():
        out[name] = (out[name] * factor).astype(out[name].dtype)
    return out
```

```python
import concourse.bass as bass
from concourse import mybir
from contextlib import ExitStack

F32, BF16, I32, U32, U8 = (mybir.dt.float32, mybir.dt.bfloat16, mybir.dt.int32, mybir.dt.uint32, mybir.dt.uint8)
ALU = mybir.AluOpType
ACT = mybir.ActivationFunctionType
AX = mybir.AxisListType

P = 128
N = 3125
D = 256
DC = D // P
NT = -(-N // P)
NFULL = N // P
NTAIL = N - NFULL * P
NPAD = NT * P
EPS = 1e-5

E = 50000
WIN = 32
NW = -(-N // WIN)
ET = 392
EROWS = E // ET
EREST = E - EROWS * ET
STAGE = 14
KT = 488
TRASH = -(-(P * ET - E) // P)
KTP = KT + TRASH
PAYW = 12
RELS, BASES = 32, 8
QT = 4
assert (E + P * NW) // P <= KT and ET % STAGE == 0 and EROWS == P - 1

GE = 32768
GT = GE // P
GKT = 280
GSTAGE = 16
assert (GE + (P - 1) * NT) // P <= GKT
HEADS, EXPERTS = 4, 4
GW = HEADS * EXPERTS + HEADS


class Link:

    def __init__(self, eng, sem):
        self.eng, self.sem, self.count, self.base = eng, sem, 0, 0

    def __call__(self, ins):
        self.note(ins)
        self.eng.wait_ge(self.sem, self.base + self.count)

    def note(self, ins):
        self.count += 1
        ins.then_inc(self.sem, 1)

    def wait(self):
        self.eng.wait_ge(self.sem, self.base + self.count)

    def enter(self, i, per_step):
        self.kept, self.per_step = self.count, per_step
        self.base, self.count = i * per_step + self.kept, 0

    def leave(self, steps):
        assert self.count == self.per_step, (self.count, self.per_step)
        self.base, self.count = 0, self.kept + steps * self.per_step


def ds(start, size):
    return bass.ds(start, size)


def gnn_ffn(nc, a, out, stop=99):
    scratch = lambda name, shape, dt: nc.dram_tensor(name, shape, dt, kind="Internal").ap()
    xn_dram = scratch("xn_table", (NPAD, D), F32)
    pay_dram = scratch("edge_records", (P * KTP, PAYW), F32)
    gpay_dram = scratch("attention_records", (P * GKT, 2), F32)
    with ExitStack() as whole:
        paused = whole.enter_context(nc.semaphore("paused"))
        sb = lambda name, shape, dt=F32: whole.enter_context(nc.sbuf_tensor(name, shape, dt))
        X = sb("X", [P, NT, D])
        iota = sb("iota", [P, P])
        ident = sb("ident", [P, P])
        before = sb("before", [P, P])
        ones = sb("ones", [P, P])
        slot_win = sb("slot_win", [1, KT], I32)
        slot_last = sb("slot_last", [1, KT], I32)
        slot_keep = sb("slot_keep", [P, KT])
        grow = sb("grow", [P, GT], I32)
        gpay = sb("gpay", [P, GT, 2])
        gslot = sb("gslot", [1, GKT], I32)
        gkeep = sb("gkeep", [P, GKT])
        glast = sb("glast", [1, NT], I32)
        kept = dict(X=X, iota=iota, ident=ident, before=before, ones=ones, slot_win=slot_win, slot_last=slot_last,
                    slot_keep=slot_keep, grow=grow, gpay=gpay, gslot=gslot, gkeep=gkeep, glast=glast,
                    xn_dram=xn_dram, pay_dram=pay_dram, gpay_dram=gpay_dram)
        sort_edges(nc, paused, a, **kept)
        if stop <= 1:
            return
        with ExitStack() as early:
            recs = early.enter_context(nc.sbuf_tensor("recs", [P, KTP, PAYW], F32))
            agg = early.enter_context(nc.sbuf_tensor("agg", [P, 3, NW * WIN], F32))
            sum_neighbours(nc, paused, a, X, iota, ones, slot_win, recs, agg, xn_dram, pay_dram)
            table_dram = scratch("attention_table", (NPAD, GW), F32)
            xnt_dram = scratch("xn1_transposed", (P, DC, NPAD), F32)
            adst_dram = scratch("a_dst", (P, NT, HEADS), F32)
            htab_dram = scratch("h_table", (P, NT, GW), F32)
            first_update(nc, paused, a, X, ident, agg, grow, gpay, gpay_dram, table_dram, xnt_dram, adst_dram, htab_dram)
        if stop <= 2:
            return
        y_dram = scratch("expert_rows", (EXPERTS * CHUNKS, P, CT, D), F32)
        with ExitStack() as late:
            sl = lambda name, shape, dt=F32: late.enter_context(nc.sbuf_tensor(name, shape, dt))
            grecs = sl("grecs", [P, GKT + GSET * GSETS, 2])
            gall = sl("gall", [P, GKT, GW])
            tmax = sl("tmax", [P, HEADS, GKT + 2])
            attention_maxima(nc, paused, a, iota, ident, grecs, gall, tmax, gpay_dram, table_dram, xnt_dram, y_dram)
            if stop <= 3:
                return
            second_update(nc, paused, a, X, iota, ident, gslot, gkeep, glast, grecs, gall, tmax, adst_dram, htab_dram, y_dram, xn_dram)
        if stop <= 4:
            return
        z_dram = scratch("basis_sums", (NT * P // WIN, P, DC * BASES * WIN), F32)
        sum_relations(nc, paused, iota, slot_win, slot_last, slot_keep, xn_dram, pay_dram, z_dram)
        if stop <= 5:
            return
        third_update(nc, a, X, iota, ident, ones, z_dram, out)


def count_windows(dve, link, windows, unroll, T, win, iota, hot, count):
    with dve.Fori(0, windows // unroll) as i:
        link.enter(i, unroll)
        for u in range(unroll):
            w = i * unroll + u
            link.note(dve.tensor_scalar(hot[:, ds(w, 1), 0:T].rearrange("p o t -> p (o t)"), win[:, 0:T],
                                                   iota[:, ds(w, 1)], None, ALU.is_equal, ALU.add,
                                                   accum_out=count[:, ds(w, 1)]))
        link.leave(windows // unroll)
    link.wait()


def rank_edges(dve, link, windows, unroll, T, hot, start, rank, pos):
    with dve.Fori(0, windows // unroll) as i:
        link.enter(i, 3 * unroll)
        for u in range(unroll):
            w = i * unroll + u
            row = hot[:, ds(w, 1), 0:T].rearrange("p o t -> p (o t)")
            link(dve.tensor_tensor_scan(rank[:, 0:T], row, row, start[:, ds(w, 1)], ALU.add, ALU.max))
            link(dve.tensor_tensor(rank[:, 0:T], rank[:, 0:T], row, ALU.mult))
            link(dve.tensor_tensor(pos[:, 0:T], pos[:, 0:T], rank[:, 0:T], ALU.add))
        link.leave(windows // unroll)


def rows_of(dve, link, T, columns, pos, pos_i, rank, row_i):
    link(dve.tensor_scalar(pos_i[:, 0:T], pos[:, 0:T], -1.0, None, ALU.add))
    link(dve.tensor_scalar(row_i[:, 0:T], pos_i[:, 0:T], P - 1, None, ALU.bitwise_and))
    link(dve.tensor_copy(rank[:, 0:T], row_i[:, 0:T]))
    link(dve.tensor_scalar(row_i[:, 0:T], pos_i[:, 0:T], 7, None, ALU.arith_shift_right))
    link(dve.tensor_copy(pos[:, 0:T], row_i[:, 0:T]))
    link(dve.scalar_tensor_tensor(row_i[:, 0:T], rank[:, 0:T], float(columns), pos[:, 0:T], ALU.mult, ALU.add))


def inverse_root(dve, link, var, root, tmp, var_ready, std_ready, n):
    link(dve.tensor_scalar(var, var, EPS, None, ALU.add))
    dve.sem_inc(var_ready, 1)
    dve.wait_ge(std_ready, n)
    link(dve.reciprocal(root, root))
    link(dve.tensor_tensor(tmp, root, root, ALU.mult))
    link(dve.tensor_tensor(tmp, tmp, var, ALU.mult))
    link(dve.tensor_scalar(tmp, tmp, -0.5, 1.5, ALU.mult, ALU.add))
    link(dve.tensor_tensor(root, root, tmp, ALU.mult))


def normalise(dve, link, X, XN, stats, aggr, var, root, tmp, var_ready, std_ready, n, xn_ready):
    for t in range(NT):
        link.note(dve.bn_stats(stats[:, t, :], X[:, t, :]))
    link.wait()
    for t in range(NT):
        link.note(dve.bn_aggr(aggr[:, t, :], stats[:, t, :]))
    link.wait()
    link(dve.tensor_copy(var, aggr[:, :, 1]))
    inverse_root(dve, link, var, root, tmp, var_ready, std_ready, n)
    for t in range(NT):
        dve.tensor_scalar(XN[:, t, :], X[:, t, :], aggr[:, t, 0:1], root[:, t:t + 1],
                          ALU.subtract, ALU.mult).then_inc(xn_ready, 1)


def sort_edges(nc, paused, a, X, iota, ident, before, ones, slot_win, slot_last, slot_keep, grow, gpay, gslot, gkeep, glast,
               xn_dram, pay_dram, gpay_dram):
    with ExitStack() as ctx:
        sb = lambda name, shape, dt=F32: ctx.enter_context(nc.sbuf_tensor(name, shape, dt))
        pb = lambda name, shape, dt=F32: ctx.enter_context(nc.psum_tensor(name, shape, dt))
        sem = lambda name: ctx.enter_context(nc.semaphore(name))
        W1 = NW + 1
        XN = sb("XN0", [P, NT, D])
        stats, aggr, rstd = sb("stats0", [P, NT, 6]), sb("aggr0", [P, NT, 2]), sb("rstd0", [P, NT])
        var, tmp = sb("var0", [P, NT]), sb("tmp0", [P, NT])
        dst, src, rel = (sb(n, [P, ET], I32) for n in ("dst", "src", "rel"))
        norm = sb("norm", [P, ET])
        win_i, low_i = sb("win_i", [P, ET], I32), sb("low_i", [P, ET], I32)
        win, relf = sb("win", [P, ET]), sb("relf", [P, ET])
        hot = sb("hot", [P, W1, ET], U8)
        count, start = sb("count", [P, W1]), sb("start", [P, W1])
        total_i, tiles, tile_end = sb("total_i", [P, W1], I32), sb("tiles", [P, W1]), sb("tile_end", [P, W1])
        rank, pos = sb("rank", [P, ET]), sb("pos", [P, ET])
        pos_i, row_i = sb("pos_i", [P, ET], I32), sb("row_i", [P, ET], I32)
        pay = sb("pay", [P, ET, PAYW])
        pad = sb("pad", [P, KTP * PAYW])
        relhot = sb("relhot", [P, STAGE * 2, RELS])
        relhot_t = sb("relhot_t", [P, STAGE * 2 // QT, P])
        wcomp = sb("wcomp", [P, QT, BASES])
        gdst, gsrc, gtmp, glow = (sb(n, [P, GT], I32) for n in ("gdst", "gsrc", "gtmp", "glow"))
        gpad = sb("gpad", [P, GKT * 2])
        glist_in, gpads_out = sem("glist_in"), sem("gpads_out")
        idx_stage = [sb(f"idx_stage{k}", [P, STAGE], I32) for k in range(2)]
        pay_stage = [sb(f"pay_stage{k}", [P, STAGE, PAYW]) for k in range(2)]
        tile_col = sb("tile_col", [P, 1])
        slot_iota = sb("slot_iota", [P, KT])
        slot_full = sb("slot_full", [P, KT])
        slot_ge = sb("slot_ge", [P, KT])
        cnt_ps = pb("cnt_ps", [P, 2, 512])
        relt_ps = pb("relt_ps", [P, 2, 512])
        coef_ps = pb("coef_ps", [P, 512])
        end_ps = pb("end_ps", [P, 512])

        consts, x_in, list_in = sem("consts"), sem("x_in"), sem("list_in")
        iota_ready = sem("iota_ready")
        v = sem("vector_steps")
        var_ready, std_ready, xn_ready, xn_out = sem("var_ready"), sem("std_ready"), sem("xn_ready"), sem("xn_out")
        lists_clear, pad_ready, pads_out = sem("lists_clear"), sem("pad_ready"), sem("pads_out")
        count_ready, prefix_ready = sem("count_ready"), sem("prefix_ready")
        relhot_ready, relt_ready, relt_copied, coef_ready, coef_used = (
            sem(n) for n in ("relhot_ready", "relt_ready", "relt_copied", "coef_ready", "coef_used"))
        wc_in = sem("wc_in")
        rows_ready, staged = sem("rows_ready"), sem("staged")
        scattered = [sem("scattered0"), sem("scattered1")]
        end_ready, end_done = sem("end_ready"), sem("end_done")
        RSTEPS = ET // (STAGE * 2)
        QN = STAGE * 2 // QT
        block = ctx.enter_context(nc.Block())

        @block.sync
        def _(sp):
            sp.dma_start(X[:, 0:NFULL, :], a["x"][0:NFULL * P, :].rearrange("(t p) d -> p t d", p=P)).then_inc(x_in, 16)
            sp.wait_ge(lists_clear, 5)
            sp.dma_start(X[0:NTAIL, NFULL, :], a["x"][NFULL * P:N, :]).then_inc(x_in, 16)
            for tile, name in ((dst, "dst"), (src, "src"), (rel, "edge_type_32"), (norm, "edge_weight1")):
                flat = a[name].rearrange("e o -> (e o)") if name == "edge_weight1" else a[name]
                sp.dma_start(tile[0:EROWS, :], flat[0:EROWS * ET].rearrange("(p t) -> p t", t=ET)).then_inc(list_in, 16)
                sp.dma_start(tile[EROWS:P, 0:EREST], flat[EROWS * ET:E].rearrange("(p t) -> p t", p=1)).then_inc(list_in, 16)
            for tile, row in ((gsrc, 0), (gdst, 1)):
                sp.dma_start(tile[:, :], a["L0_ffn_edge_index"][row, :].rearrange("(p t) -> p t", t=GT)).then_inc(glist_in, 16)
            sp.wait_ge(pad_ready, 2)
            sp.dma_start(pay_dram.rearrange("(p k) w -> p (k w)", p=P), pad[:, :]).then_inc(pads_out, 16)
            sp.wait_ge(pad_ready, 4)
            sp.dma_start(gpay_dram.rearrange("(p k) w -> p (k w)", p=P), gpad[:, :]).then_inc(gpads_out, 16)
            sp.wait_ge(gpads_out, 16)
            sp.wait_ge(xn_ready, NT)
            sp.dma_start(xn_dram.rearrange("(t p) d -> p t d", p=P), XN[:, :, :]).then_inc(xn_out, 16)
            sp.wait_ge(xn_out, 16)

        @block.gpsimd
        def _(pool):
            nc.gpsimd.iota(iota[:, :], [[1, P]], base=0, channel_multiplier=0, allow_small_or_imprecise_dtypes=True).then_inc(iota_ready, 1)
            nc.gpsimd.iota(slot_iota[:, :], [[1, KT]], base=0, channel_multiplier=0, allow_small_or_imprecise_dtypes=True).then_inc(iota_ready, 1)
            nc.gpsimd.memset(ones[:, :], 1.0).then_inc(consts, 1)
            nc.gpsimd.memset(wcomp[:, :, :], 0.0).then_inc(consts, 1)
            pool.wait_ge(consts, 2)
            nc.gpsimd.affine_select(out=ident[:, :], in_=ones[:, :], compare_op=ALU.is_equal, fill=0.0, base=0,
                                    pattern=[[-1, P]], channel_multiplier=1).then_inc(consts, 1)
            nc.gpsimd.affine_select(out=before[:, :], in_=ones[:, :], compare_op=ALU.is_gt, fill=0.0, base=0,
                                    pattern=[[1, P]], channel_multiplier=-1).then_inc(consts, 1)
            for q in range(QT):
                pool.dma_start(wcomp[q * RELS:(q + 1) * RELS, q, :], a["L1_gnn_w_comp"]).then_inc(wc_in, 16)
            pool.wait_ge(pads_out, 16)
            with pool.Fori(0, ET // (2 * STAGE)) as i:
                for k in range(2):
                    pool.wait_ge(staged, i * 4 + 2 * k + 2)
                    pool.sem_inc(paused, 1)
                    for t in range(STAGE):
                        pool.indirect_dma_start(
                            pay_dram, bass.IndirectOffsetOnAxis(ap=idx_stage[k][:, t:t + 1].bitcast(U32), axis=0),
                            pay_stage[k][:, t, :], None).then_inc(scattered[k], 16)
            for k in range(2):
                pool.wait_ge(scattered[k], 16 * (ET // 2))

        @block.scalar
        def _(act):
            act.wait_ge(var_ready, 1)
            nc.scalar.activation(rstd[:, :], var[:, :], ACT.Sqrt).then_inc(std_ready, 1)
            with act.Fori(0, RSTEPS) as i:
                act.wait_ge(relt_ready, i + 2)
                nc.scalar.activation(relhot_t[:, :, :].rearrange("p (a q) e -> p a (q e)", a=1)[:, 0, 0:4 * P],
                                     relt_ps[:, 0, 0:4 * P], ACT.Copy).then_inc(relt_copied, 1)
                nc.scalar.activation(relhot_t[:, 4:QN, :].rearrange("p q e -> p (q e)"),
                                     relt_ps[:, 1, 0:(QN - 4) * P], ACT.Copy).then_inc(relt_copied, 1)
            act.wait_ge(rows_ready, 1)
            act.wait_ge(coef_used, RSTEPS + 1)

            def stage(i, k):
                cols = ds(i * (2 * STAGE) + k * STAGE, STAGE)
                nc.scalar.activation(pay_stage[k][:, :, :], pay[:, cols, :], ACT.Copy).then_inc(staged, 1)
                nc.scalar.activation(idx_stage[k][:, :], row_i[:, cols], ACT.Copy).then_inc(staged, 1)

            for k in range(2):
                stage(0, k)
            with act.Fori(1, ET // (2 * STAGE)) as i:
                for k in range(2):
                    act.wait_ge(scattered[k], i * (16 * STAGE))
                    stage(i, k)

        @block.tensor
        def _(pe):
            pe.wait_ge(consts, 4)
            with pe.Fori(0, RSTEPS) as i:
                pe.wait_ge(relhot_ready, i + 1)
                for q in range(QN):
                    mm = nc.tensor.transpose(relt_ps[:, q // 4, (q % 4) * P:(q % 4 + 1) * P],
                                             relhot[:, q * QT:(q + 1) * QT, :].rearrange("p q r -> p (q r)"), ident[:, :])
                mm.then_inc(relt_ready, 1)
                pe.wait_ge(relt_copied, i * 2 + 2)
                pe.wait_ge(wc_in, 16 * QT)
                pe.wait_ge(coef_used, i + 1)
                for q in range(QN):
                    mm = nc.tensor.matmul(coef_ps[:, q * QT * BASES:(q + 1) * QT * BASES], relhot_t[:, q, :],
                                          wcomp[:, :, :].rearrange("p q b -> p (q b)"), start=True, stop=True)
                mm.then_inc(coef_ready, 1)
            pe.wait_ge(count_ready, 1)
            nc.tensor.matmul(cnt_ps[:, 0, 0:W1], before[:, :], count[:, :], start=True, stop=True)
            nc.tensor.matmul(cnt_ps[:, 1, 0:W1], ones[:, :], count[:, :], start=True, stop=True).then_inc(prefix_ready, 1)
            pe.wait_ge(end_ready, 1)
            nc.tensor.matmul(end_ps[:, 0:KT], ones[0:NW, :], slot_ge[0:NW, :], start=True, stop=True).then_inc(end_done, 1)
            pe.wait_ge(count_ready, 2)
            nc.tensor.matmul(cnt_ps[:, 0, 0:NT], before[:, :], count[:, 0:NT], start=True, stop=True)
            nc.tensor.matmul(cnt_ps[:, 1, 0:NT], ones[:, :], count[:, 0:NT], start=True, stop=True).then_inc(prefix_ready, 1)
            pe.wait_ge(end_ready, 2)
            nc.tensor.matmul(end_ps[:, 0:GKT], ones[0:NT, :], slot_ge[0:NT, 0:GKT], start=True, stop=True).then_inc(end_done, 1)

        @block.vector
        def _(dve):
            link = Link(dve, v)
            dve.sem_inc(coef_used, 1)
            dve.sem_inc(relt_ready, 1)
            nc.vector.memset(dst[:, :], NW * WIN).then_inc(lists_clear, 1)
            nc.vector.memset(src[:, :], 0).then_inc(lists_clear, 1)
            nc.vector.memset(rel[:, :], 0).then_inc(lists_clear, 1)
            nc.vector.memset(norm[:, :], 0.0).then_inc(lists_clear, 1)
            nc.vector.memset(X[:, NFULL, :], 0.0).then_inc(lists_clear, 1)
            nc.vector.memset(pad[:, :], 0.0).then_inc(pad_ready, 1)
            dve.wait_ge(pad_ready, 1)
            nc.vector.memset(pad[:, :].rearrange("p (k w) -> p k w", w=PAYW)[:, :, 1:2], -1.0).then_inc(pad_ready, 1)
            nc.vector.memset(gpad[:, :], 0.0).then_inc(pad_ready, 1)
            dve.wait_ge(pad_ready, 3)
            nc.vector.memset(gpad[:, :].rearrange("p (k w) -> p k w", w=2)[:, :, 1:2], -1.0).then_inc(pad_ready, 1)
            link(nc.vector.memset(pay[:, :, :], 0.0))
            link(nc.vector.memset(pos[:, :], 0.0))
            dve.wait_ge(x_in, 32)
            normalise(dve, link, X, XN, stats, aggr, var[:, :], rstd[:, :], tmp[:, :], var_ready, std_ready, 1, xn_ready)
            dve.wait_ge(list_in, 16 * 8)
            dve.wait_ge(iota_ready, 2)
            link.note(nc.vector.tensor_scalar(win_i[:, :], dst[:, :], 5, None, ALU.arith_shift_right))
            link.note(nc.vector.tensor_scalar(low_i[:, :], dst[:, :], WIN - 1, None, ALU.bitwise_and))
            link.note(nc.vector.tensor_copy(relf[:, :], rel[:, :]))
            link.note(nc.vector.tensor_copy(pay[:, :, 0:1].bitcast(I32), src[:, :].unsqueeze(2)))
            link.wait()
            link.note(nc.vector.tensor_copy(win[:, :], win_i[:, :]))
            link.note(nc.vector.tensor_copy(pay[:, :, 1:2], low_i[:, :].unsqueeze(2)))
            link.wait()
            rounds = 2
            with dve.Fori(0, RSTEPS) as i:
                link.enter(i, rounds)
                cols = ds(i * (2 * STAGE), 2 * STAGE)
                dve.wait_ge(relt_ready, i + 1)
                link.note(nc.vector.tensor_tensor(relhot[:, :, :],
                                                  relf[:, cols].unsqueeze(2).to_broadcast([P, 2 * STAGE, RELS]),
                                                  iota[:, 0:RELS].unsqueeze(1).to_broadcast([P, 2 * STAGE, RELS]),
                                                  ALU.is_equal))
                link.wait()
                dve.sem_inc(relhot_ready, 1)
                dve.wait_ge(coef_ready, i + 1)
                link.note(nc.vector.tensor_tensor(pay[:, cols, 2:2 + BASES],
                                                  coef_ps[:, 0:2 * STAGE * BASES].rearrange("p (t b) -> p t b", b=BASES),
                                                  norm[:, cols].unsqueeze(2).to_broadcast([P, 2 * STAGE, BASES]),
                                                  ALU.mult))
                link.wait()
                dve.sem_inc(coef_used, 1)
                link.leave(RSTEPS)
            UN = 3
            count_windows(dve, link, W1, UN, ET, win, iota, hot, count)
            dve.sem_inc(count_ready, 1)
            dve.wait_ge(prefix_ready, 1)
            link(nc.vector.tensor_scalar(total_i[:, :], cnt_ps[:, 1, 0:W1], float(P - 1), None, ALU.add))
            link(nc.vector.tensor_scalar(total_i[:, :], total_i[:, :], 7, None, ALU.arith_shift_right))
            link(nc.vector.tensor_copy(tiles[:, :], total_i[:, :]))
            link(nc.vector.tensor_scalar(tiles[:, :], tiles[:, :], 1.0, None, ALU.max))
            link(nc.vector.memset(tiles[:, NW:W1], float(TRASH)))
            link(nc.vector.tensor_tensor_scan(tile_end[:, :], tiles[:, :], tiles[:, :], 0.0, ALU.add, ALU.max))
            link(nc.vector.tensor_tensor(start[:, :], tile_end[:, :], tiles[:, :], ALU.subtract))
            link(nc.vector.memset(start[:, NW:W1], float(KT)))
            link(nc.vector.tensor_scalar(start[:, :], start[:, :], float(P), None, ALU.mult))
            link(nc.vector.tensor_tensor(start[:, :], start[:, :], cnt_ps[:, 0, 0:W1], ALU.add))
            rank_edges(dve, link, W1, UN, ET, hot, start, rank, pos)
            rows_of(dve, link, ET, KTP, pos, pos_i, rank, row_i)
            dve.sem_inc(rows_ready, 1)
            link(nc.vector.tensor_tensor(slot_full[:, 0:NW], ident[:, 0:NW], tile_end[:, 0:NW], ALU.mult))
            link(nc.vector.tensor_reduce(tile_col[:, :], slot_full[:, 0:NW], AX.X, ALU.add))
            link(nc.vector.tensor_scalar(slot_ge[:, :], slot_iota[:, :], tile_col[:, :], None, ALU.is_ge))
            dve.sem_inc(end_ready, 1)
            dve.wait_ge(end_done, 1)
            link(nc.vector.tensor_scalar(slot_full[:, :], end_ps[:, 0:KT], float(NW - 1), None, ALU.min))
            link.note(nc.vector.tensor_copy(slot_win[:, :], slot_full[0:1, :]))
            link.note(nc.vector.memset(slot_keep[:, 0:1], 0.0))
            link.note(nc.vector.memset(slot_last[:, KT - 1:KT], 1))
            link.note(nc.vector.tensor_tensor(slot_keep[:, 1:KT], slot_full[:, 1:KT], slot_full[:, 0:KT - 1], ALU.is_equal))
            link.note(nc.vector.tensor_tensor(slot_last[:, 0:KT - 1], slot_full[0:1, 1:KT], slot_full[0:1, 0:KT - 1], ALU.not_equal))
            link(nc.vector.memset(pos[:, :], 0.0))
            dve.wait_ge(glist_in, 32)
            link.note(nc.vector.tensor_scalar(gtmp[:, :], gdst[:, :], 7, None, ALU.arith_shift_right))
            link(nc.vector.tensor_scalar(glow[:, :], gdst[:, :], P - 1, None, ALU.bitwise_and))
            link.note(nc.vector.tensor_copy(win[:, 0:GT], gtmp[:, :]))
            link.note(nc.vector.tensor_copy(gpay[:, :, 0:1].bitcast(I32), gsrc[:, :].unsqueeze(2)))
            link(nc.vector.tensor_copy(gpay[:, :, 1:2], glow[:, :].unsqueeze(2)))
            count_windows(dve, link, NT, 5, GT, win, iota, hot, count)
            dve.sem_inc(count_ready, 1)
            dve.wait_ge(prefix_ready, 2)
            link(nc.vector.tensor_scalar(total_i[:, 0:NT], cnt_ps[:, 1, 0:NT], float(P - 1), None, ALU.add))
            link(nc.vector.tensor_scalar(total_i[:, 0:NT], total_i[:, 0:NT], 7, None, ALU.arith_shift_right))
            link(nc.vector.tensor_copy(tiles[:, 0:NT], total_i[:, 0:NT]))
            link(nc.vector.tensor_tensor_scan(tile_end[:, 0:NT], tiles[:, 0:NT], tiles[:, 0:NT], 0.0, ALU.add, ALU.max))
            link(nc.vector.tensor_tensor(start[:, 0:NT], tile_end[:, 0:NT], tiles[:, 0:NT], ALU.subtract))
            link(nc.vector.tensor_scalar(start[:, 0:NT], start[:, 0:NT], float(P), None, ALU.mult))
            link(nc.vector.tensor_tensor(start[:, 0:NT], start[:, 0:NT], cnt_ps[:, 0, 0:NT], ALU.add))
            rank_edges(dve, link, NT, 5, GT, hot, start, rank, pos)
            rows_of(dve, link, GT, GKT, pos, pos_i, rank, grow)
            link(nc.vector.tensor_scalar(rank[:, 0:NT], tiles[:, 0:NT], 0.5, float(GKT + 1), ALU.is_lt, ALU.mult))
            link(nc.vector.tensor_tensor(rank[:, 0:NT], rank[:, 0:NT], tile_end[:, 0:NT], ALU.max))
            link(nc.vector.tensor_scalar(glast[:, :], rank[0:1, 0:NT], -1.0, None, ALU.add))
            link(nc.vector.tensor_tensor(slot_full[:, 0:NT], ident[:, 0:NT], tile_end[:, 0:NT], ALU.mult))
            link(nc.vector.tensor_reduce(tile_col[:, :], slot_full[:, 0:NT], AX.X, ALU.add))
            link(nc.vector.tensor_scalar(slot_ge[:, 0:GKT], slot_iota[:, 0:GKT], tile_col[:, :], None, ALU.is_ge))
            dve.sem_inc(end_ready, 1)
            dve.wait_ge(end_done, 2)
            link(nc.vector.tensor_scalar(slot_full[:, 0:GKT], end_ps[:, 0:GKT], float(NT - 1), None, ALU.min))
            link.note(nc.vector.tensor_copy(gslot[:, :], slot_full[0:1, 0:GKT]))
            link.note(nc.vector.memset(gkeep[:, 0:1], 0.0))
            link.note(nc.vector.tensor_tensor(gkeep[:, 1:GKT], slot_full[:, 1:GKT], slot_full[:, 0:GKT - 1], ALU.is_equal))


SET = 2
SETS = 4


def sum_neighbours(nc, paused, a, X, iota, ones, slot_win, recs, agg, table, pay_dram):
    with ExitStack() as ctx:
        sb = lambda name, shape, dt=F32: ctx.enter_context(nc.sbuf_tensor(name, shape, dt))
        pb = lambda name, shape, dt=F32: ctx.enter_context(nc.psum_tensor(name, shape, dt))
        sem = lambda name: ctx.enter_context(nc.semaphore(name))
        rows = [sb(f"rows{k}", [P, SET, D]) for k in range(SETS)]
        idx = [sb(f"idx{k}", [P, SET], I32) for k in range(SETS)]
        hot = [sb(f"target{k}", [P, SET, WIN]) for k in range(SETS)]
        part = [pb(f"part{k}", [P, 512]) for k in range(SETS)]
        recs_in, idx_ready, hot_ready, added, agg_clear = (
            sem(n) for n in ("recs_in", "idx_ready", "hot_ready", "added", "agg_clear"))
        gathered = [sem(f"gathered{k}") for k in range(SETS)]
        summed = [sem(f"summed{k}") for k in range(SETS)]
        PER = SET * SETS
        STEPS = KT // PER
        block = ctx.enter_context(nc.Block())

        @block.sync
        def _(sp):
            sp.dma_start(recs[:, :, :], pay_dram.rearrange("(p k) w -> p k w", p=P)).then_inc(recs_in, 16)

        @block.scalar
        def _(act):
            act.wait_ge(recs_in, 16)
            with act.Fori(0, STEPS) as i:
                for k in range(SETS):
                    act.wait_ge(summed[k], i + 1)
                    nc.scalar.activation(idx[k][:, :].unsqueeze(2), recs[:, ds(i * PER + k * SET, SET), 0:1].bitcast(I32),
                                         ACT.Copy).then_inc(idx_ready, 1)

        @block.gpsimd
        def _(pool):
            with pool.Fori(0, STEPS) as i:
                for k in range(SETS):
                    pool.wait_ge(idx_ready, i * SETS + k + 1)
                    pool.sem_inc(paused, 1)
                    for u in range(SET):
                        pool.indirect_dma_start(rows[k][:, u, :], None, table,
                                                bass.IndirectOffsetOnAxis(ap=idx[k][:, u:u + 1].bitcast(U32), axis=0)
                                                ).then_inc(gathered[k], 16)

        @block.tensor
        def _(pe):
            with pe.Fori(0, STEPS) as i:
                for k in range(SETS):
                    pe.wait_ge(hot_ready, i * SETS + k + 1)
                    pe.wait_ge(added, i * PER + (k + 1) * SET)
                    pe.wait_ge(gathered[k], (i + 1) * (16 * SET))
                    for u in range(SET):
                        for c in range(DC):
                            nc.tensor.matmul(part[k][:, u * 3 * WIN + c * WIN:u * 3 * WIN + (c + 1) * WIN],
                                             rows[k][:, u, c * P:(c + 1) * P], hot[k][:, u, :], start=True, stop=True)
                        mm = nc.tensor.matmul(part[k][:, u * 3 * WIN + 2 * WIN:(u + 1) * 3 * WIN],
                                              ones[:, :], hot[k][:, u, :], start=True, stop=True)
                    mm.then_inc(summed[k], 1)

        @block.vector
        def _(dve):
            for k in range(SETS):
                dve.sem_inc(summed[k], 1)
            nc.vector.memset(agg[:, :, :], 0.0).then_inc(agg_clear, 1)
            dve.wait_ge(agg_clear, 1)
            dve.wait_ge(recs_in, 16)
            dve.sem_inc(added, PER)

            def targets(i, k):
                nc.vector.tensor_tensor(hot[k][:, :, :], recs[:, ds(i * PER + k * SET, SET), 1:2].to_broadcast([P, SET, WIN]),
                                        iota[:, 0:WIN].unsqueeze(1).to_broadcast([P, SET, WIN]),
                                        ALU.is_equal).then_inc(hot_ready, 1)

            def step(i, more):
                _, wins = nc.values_load_multi_w_load_instructions(
                    slot_win[0:1, ds(i * PER, PER)], engines=[dve.engine], min_val=0, max_val=NW - 1)
                for k in range(SETS):
                    dve.wait_ge(summed[k], i + 2)
                    for u in range(SET):
                        to = agg[:, :, ds(wins[k * SET + u] * WIN, WIN)]
                        dve.wait_ge(added, (i + 1) * PER + k * SET + u)
                        nc.vector.tensor_tensor(to, to, part[k][:, u * 3 * WIN:(u + 1) * 3 * WIN].rearrange("p (c w) -> p c w", w=WIN),
                                                ALU.add).then_inc(added, 1)
                    if more:
                        targets(i + 1, k)

            for k in range(SETS):
                targets(0, k)
            with dve.Fori(0, STEPS - 1) as i:
                step(i, True)
            step(STEPS - 1, False)


def transpose_nodes(pe, ident, XN, xnt_ps, psum_free, xnt_ready, first=0):
    for n, (t, c) in enumerate((t, c) for t in range(NT) for c in range(DC)):
        g, q = divmod(n, 4)
        if q == 0 and g >= 2:
            pe.wait_ge(psum_free, first + g - 1)
        mm = pe.transpose(xnt_ps[:, g % 2, q * P:(q + 1) * P], XN[:, t, c * P:(c + 1) * P], ident[:, :])
        if q == 3 or n == NT * DC - 1:
            mm.then_inc(xnt_ready, 1)


def copy_transposed(act, XNT, xnt_ps, psum_free, xnt_ready, first=0):
    groups = -(-NT * DC // 4)
    for g in range(groups):
        act.wait_ge(xnt_ready, first + g + 1)
        tiles = min(4, NT * DC - 4 * g) // DC
        act.activation(XNT[:, :, g * 2 * P:(g * 2 + tiles) * P].rearrange("p c (t n) -> p t c n", n=P),
                       xnt_ps[:, g % 2, 0:tiles * DC * P].rearrange("p (t c n) -> p t c n", c=DC, n=P),
                       ACT.Copy).then_inc(psum_free, 1)


def first_update(nc, paused, a, X, ident, agg, grow, gpay, gpay_dram, table_dram, xnt_dram, adst_dram, htab_dram):
    with ExitStack() as ctx:
        sb = lambda name, shape, dt=F32: ctx.enter_context(nc.sbuf_tensor(name, shape, dt))
        pb = lambda name, shape, dt=F32: ctx.enter_context(nc.psum_tensor(name, shape, dt))
        sem = lambda name: ctx.enter_context(nc.semaphore(name))
        W, b = sb("W_gnn", [P, DC, D]), sb("b_gnn", [1, D])
        wgat = sb("wgat", [P, DC, HEADS * EXPERTS])
        att = sb("att", [P, 2, HEADS * EXPERTS])
        inv, some = sb("inv", [P, NW * WIN]), sb("some", [1, NW * WIN])
        XN, XNT = sb("XN1", [P, NT, D]), sb("XNT1", [P, DC, NPAD])
        stats, aggr = sb("stats1", [P, NT, 6]), sb("aggr1", [P, NT, 2])
        var, root, tmp = sb("var1", [P, NT]), sb("root1", [P, NT]), sb("tmp1", [P, NT])
        htab, ha, adst = sb("htab", [P, NT, GW]), sb("ha", [P, NT, HEADS * EXPERTS]), sb("adst", [P, NT, HEADS])
        gidx = [sb(f"gidx{k}", [P, GSTAGE], I32) for k in range(2)]
        grec = [sb(f"grec{k}", [P, GSTAGE, 2]) for k in range(2)]
        upd = [pb(f"upd{k}", [P, 512]) for k in range(2)]
        xnt_ps = pb("xnt_ps", [P, 2, 512])
        h_ps = pb("h_ps", [P, 512])
        w_in, v, scaled, updated, upd_used = (sem(n) for n in ("w_in", "vector_steps1", "scaled", "updated", "upd_used"))
        var_ready, std_ready, xn_ready = sem("var_ready1"), sem("std_ready1"), sem("xn_ready1")
        psum_free, xnt_ready, h_ready, tables_ready, out_done = (
            sem(n) for n in ("psum_free", "xnt_ready", "h_ready", "tables_ready", "out_done"))
        staged = sem("gstaged")
        scattered = [sem("gscattered0"), sem("gscattered1")]
        block = ctx.enter_context(nc.Block())
        GROUPS = -(-NT * DC // 4)

        @block.sync
        def _(sp):
            sp.dma_start(W[:, :, :], a["L0_gnn_weight"].rearrange("(c p) d -> p c d", p=P)).then_inc(w_in, 16)
            sp.dma_start(b[:, :], a["L0_gnn_bias"].rearrange("(o d) -> o d", o=1)).then_inc(w_in, 16)
            sp.dma_start(wgat[:, :, :], a["L0_ffn_W_gat"].rearrange("(c p) d -> p c d", p=P)).then_inc(w_in, 16)
            for n, name in enumerate(("L0_ffn_att_src", "L0_ffn_att_dst")):
                sp.dma_start(att[:, n, :], a[name].rearrange("h e -> (h e)").partition_broadcast(P)).then_inc(w_in, 16)
            sp.wait_ge(psum_free, GROUPS)
            sp.dma_start(xnt_dram, XNT[:, :, :]).then_inc(out_done, 16)
            sp.wait_ge(tables_ready, 1)
            sp.dma_start(table_dram.rearrange("(t p) w -> p t w", p=P), htab[:, :, :]).then_inc(out_done, 16)
            sp.dma_start(htab_dram, htab[:, :, :]).then_inc(out_done, 16)
            sp.dma_start(adst_dram, adst[:, :, :]).then_inc(out_done, 16)
            sp.wait_ge(out_done, 64)

        @block.gpsimd
        def _(pool):
            with pool.Fori(0, GT // (2 * GSTAGE)) as i:
                for k in range(2):
                    pool.wait_ge(staged, i * 4 + 2 * k + 2)
                    pool.sem_inc(paused, 1)
                    for t in range(GSTAGE):
                        pool.indirect_dma_start(
                            gpay_dram, bass.IndirectOffsetOnAxis(ap=gidx[k][:, t:t + 1].bitcast(U32), axis=0),
                            grec[k][:, t, :], None).then_inc(scattered[k], 16)
            for k in range(2):
                pool.wait_ge(scattered[k], 16 * (GT // 2))

        @block.scalar
        def _(act):
            first = 0

            def stage(i):
                for k in range(2):
                    if i is not first:
                        act.wait_ge(scattered[k], i * (16 * GSTAGE))
                    cols = ds(i * (2 * GSTAGE) + k * GSTAGE, GSTAGE)
                    nc.scalar.activation(grec[k][:, :, :], gpay[:, cols, :], ACT.Copy).then_inc(staged, 1)
                    nc.scalar.activation(gidx[k][:, :], grow[:, cols], ACT.Copy).then_inc(staged, 1)

            stage(first)
            act.wait_ge(var_ready, 1)
            nc.scalar.activation(root[:, :], var[:, :], ACT.Sqrt).then_inc(std_ready, 1)
            copy_transposed(nc.scalar, XNT, xnt_ps, psum_free, xnt_ready)
            with act.Fori(1, GT // (2 * GSTAGE)) as i:
                stage(i)

        @block.tensor
        def _(pe):
            pe.wait_ge(w_in, 80)
            pe.wait_ge(scaled, 1)
            for t in range(NT):
                n = min(P, NW * WIN - t * P)
                if t >= 2:
                    pe.wait_ge(upd_used, t - 1)
                for c in range(DC):
                    nc.tensor.matmul(upd[t % 2][0:n, 0:D], agg[:, c, t * P:t * P + n], W[:, c, :], start=(c == 0), stop=False)
                nc.tensor.matmul(upd[t % 2][0:n, 0:D], some[0:1, t * P:t * P + n], b[:, :], start=False, stop=True).then_inc(updated, 1)
            pe.wait_ge(xn_ready, NT)
            transpose_nodes(nc.tensor, ident, XN, xnt_ps, psum_free, xnt_ready)
            pe.wait_ge(psum_free, GROUPS)
            for t in range(NT):
                for c in range(DC):
                    mm = nc.tensor.matmul(h_ps[:, t * 16:(t + 1) * 16], XNT[:, c, t * P:(t + 1) * P], wgat[:, c, :],
                                          start=(c == 0), stop=(c == DC - 1))
            mm.then_inc(h_ready, 1)

        @block.vector
        def _(dve):
            link = Link(dve, v)
            link.note(nc.vector.tensor_scalar(some[:, :], agg[0:1, 2, :], 1.0, None, ALU.min))
            link(nc.vector.tensor_scalar(inv[:, :], agg[:, 2, :], 1.0, None, ALU.max))
            link(nc.vector.reciprocal(inv[:, :], inv[:, :]))
            for c in range(DC):
                link.note(nc.vector.tensor_tensor(agg[:, c, :], agg[:, c, :], inv[:, :], ALU.mult))
            link.wait()
            dve.sem_inc(scaled, 1)
            for t in range(NT):
                n = min(P, NW * WIN - t * P)
                dve.wait_ge(updated, t + 1)
                nc.vector.tensor_tensor(X[0:n, t, :], X[0:n, t, :], upd[t % 2][0:n, 0:D], ALU.add).then_inc(upd_used, 1)
            dve.wait_ge(upd_used, NT)
            normalise(dve, link, X, XN, stats, aggr, var[:, :], root[:, :], tmp[:, :], var_ready, std_ready, 1, xn_ready)
            dve.wait_ge(h_ready, 1)
            hv = h_ps[:, 0:NT * 16].rearrange("p (t k) -> p t k", k=16)
            link.note(nc.vector.tensor_copy(htab[:, :, 0:16], hv))
            for n, to in ((0, htab[:, :, 16:20]), (1, adst[:, :, :])):
                link(nc.vector.tensor_tensor(ha[:, :, :], hv, att[:, n, :].unsqueeze(1).to_broadcast([P, NT, 16]), ALU.mult))
                link(nc.vector.tensor_reduce(to, ha[:, :, :].rearrange("p t (h e) -> p t h e", e=EXPERTS), AX.X, ALU.add))
            dve.sem_inc(tables_ready, 1)


CT = 5
CHUNKS = NT // CT
HALF = CT * P // 2
FE = 2 * D
FC = FE // P
GSET = 7
GSETS = 2
GSTEPS = GKT // (GSET * GSETS)
BIG = 1e30
assert NT % CT == 0 and GSTEPS == EXPERTS * CHUNKS


def attention_maxima(nc, paused, a, iota, ident, grecs, gall, tmax, gpay_dram, table_dram, xnt_dram, y_dram):
    with ExitStack() as ctx:
        sb = lambda name, shape, dt=F32: ctx.enter_context(nc.sbuf_tensor(name, shape, dt))
        pb = lambda name, shape, dt=F32: ctx.enter_context(nc.psum_tensor(name, shape, dt))
        sem = lambda name: ctx.enter_context(nc.semaphore(name))
        PER = GSET * GSETS
        M = GSET * HEADS
        XNT = sb("XNT", [P, DC, NPAD])
        W1 = [sb(f"W1_{j}", [P, DC, FE]) for j in range(2)]
        W2 = sb("W2", [P, EXPERTS, FC, D])
        b1 = sb("b1", [P, EXPERTS, FC])
        hid = sb("hid", [P, FC, 2 * HALF])
        ys = sb("ys", [P, CT, D])
        rows = [sb(f"grows{k}", [P, GSET, GW]) for k in range(GSETS)]
        idx = [sb(f"gix{k}", [P, GSET], I32) for k in range(GSETS)]
        hot = [sb(f"ghot{k}", [P, GSET, P], BF16) for k in range(GSETS)]
        pen = [sb(f"pen{k}", [P, GSET, P], BF16) for k in range(GSETS)]
        rest = sb("rest", [P, M])
        split = [sb(f"split{k}", [P, 3, 32], BF16) for k in range(GSETS)]
        splt = [sb(f"splt{k}", [96, P], BF16) for k in range(GSETS)]
        identb = sb("identb", [P, P], BF16)
        pick = sb("pick", [96, M, P], BF16)
        hot_ps = pb("hot_ps", [P, GSET, P], BF16)
        splt_ps = pb("splt_ps", [96, P], BF16)
        val_ps = pb("val_ps", [P, 2, HEADS, P])
        h_ps, y_ps = pb("h_ps2", [P, 2, 512]), pb("y_ps", [P, 2, 512])

        w_in, clear, pick_ready = sem("w_in2"), sem("clear2"), sem("pick_ready")
        v = sem("vector_steps2")
        idx_ready = sem("gix_ready")
        gathered = [sem(f"ggathered{k}") for k in range(GSETS)]
        kept, hot_ready, hott_ready, pen_ready = (sem(n) for n in ("kept", "ghot_ready", "ghott_ready", "pen_ready"))
        split_ready, splt_ready, splt_copied = sem("split_ready"), sem("splt_ready"), sem("splt_copied")
        val_ready, val_used = sem("val_ready"), sem("val_used")
        h_ready, h_used, y_ready, y_used = (sem(n) for n in ("h_ready2", "h_used", "y_ready", "y_used"))
        stored, up_in = sem("y_stored"), [sem("up_in0"), sem("up_in1")]
        block = ctx.enter_context(nc.Block())

        @block.sync
        def _(sp):
            sp.dma_start(grecs[:, 0:GKT, :], gpay_dram.rearrange("(p k) w -> p k w", p=P)).then_inc(w_in, 16)
            sp.dma_start(XNT[:, :, :], xnt_dram).then_inc(w_in, 16)
            for e in range(EXPERTS):
                sp.dma_start(W2[:, e, :, :], a["L0_ffn_W2"][e].rearrange("(c p) f -> p c f", p=P)).then_inc(w_in, 16)
                sp.dma_start(b1[:, e, :], a["L0_ffn_b1"][e].rearrange("(c p) -> p c", p=P),
                             allow_slow_non_contiguous=True).then_inc(w_in, 16)
            def load_up(i, j):
                sp.dma_start(W1[j][:, :, :], a["L0_ffn_W1"][ds(i % EXPERTS, 1)].rearrange("o (c p) f -> p (o c) f", p=P)
                             ).then_inc(up_in[j], 16)

            for j in range(2):
                load_up(j, j)
            with sp.Fori(0, GSTEPS // 2) as ii:
                for j in range(2):
                    i = ii * 2 + j
                    sp.wait_ge(h_ready, (i + 1) * (2 * FC))
                    load_up(i + 2, j)
                    sp.wait_ge(y_used, (i + 1) * CT + 2)
                    sp.dma_start(y_dram[ds(i, 1)].rearrange("o p t d -> (o p) t d"), ys[:, :, :]).then_inc(stored, 16)
            for j in range(2):
                sp.wait_ge(up_in[j], 16 * (GSTEPS // 2 + 1))
            sp.wait_ge(stored, 16 * GSTEPS + 1)

        @block.gpsimd
        def _(pool):
            nc.gpsimd.memset(pick[:, :, :], 0.0).then_inc(pick_ready, 1)
            for j in range(3):
                pool.wait_ge(pick_ready, j + 1)
                view = pick[32 * j:32 * j + M, :, :]
                nc.gpsimd.affine_select(out=view, in_=view, compare_op=ALU.not_equal, fill=1.0, base=0,
                                        pattern=[[-1, M], [0, P]], channel_multiplier=1).then_inc(pick_ready, 1)
            pool.wait_ge(pick_ready, 4)
            with pool.Fori(0, GSTEPS // 2) as ii:
                for j in range(2):
                    i = ii * 2 + j
                    for k in range(GSETS):
                        pool.wait_ge(idx_ready, i * GSETS + k + 1)
                        pool.sem_inc(paused, 1)
                        pool.wait_ge(split_ready, i * GSETS + k + 1)
                        pool.sem_inc(paused, 1)
                        for u in range(GSET):
                            pool.indirect_dma_start(rows[k][:, u, :], None, table_dram,
                                                    bass.IndirectOffsetOnAxis(ap=idx[k][:, u:u + 1].bitcast(U32), axis=0)
                                                    ).then_inc(gathered[k], 16)

        @block.scalar
        def _(act):
            def stage(i, k):
                nc.scalar.activation(idx[k][:, :].unsqueeze(2), grecs[:, ds(i * PER + k * GSET, GSET), 0:1].bitcast(I32),
                                     ACT.Copy).then_inc(idx_ready, 1)

            act.wait_ge(w_in, 16 * 10)
            act.wait_ge(clear, 2)
            for k in range(GSETS):
                stage(0, k)
            with act.Fori(0, GSTEPS // 2) as ii:
                for j in range(2):
                    i = ii * 2 + j
                    for k in range(GSETS):
                        act.wait_ge(gathered[k], (i + 1) * (16 * GSET))
                        act.sem_inc(paused, 1)
                        nc.scalar.activation(gall[:, ds(i * PER + k * GSET, GSET), :], rows[k][:, :, :], ACT.Copy).then_inc(kept, 1)
                        act.wait_ge(kept, i * GSETS + k + 1)
                        stage(i + 1, k)
                        act.wait_ge(hott_ready, i * GSETS + k + 2)
                        act.wait_ge(val_ready, i * PER + k * GSET + 1)
                        nc.scalar.activation(pen[k][:, :, :], hot_ps[:, :, :], ACT.Copy, bias=-BIG, scale=BIG).then_inc(pen_ready, 1)
                        act.wait_ge(splt_ready, i * GSETS + k + 2)
                        nc.scalar.activation(splt[k][:, :], splt_ps[:, :], ACT.Copy).then_inc(splt_copied, 1)
                        for f in range(FC):
                            n = k * FC + f
                            act.wait_ge(h_ready, i * (2 * FC) + n + 1)
                            if n == 0:
                                act.wait_ge(y_ready, i * CT + 1)
                            act.sem_inc(paused, 1)
                            nc.scalar.activation(hid[:, f, k * HALF:(k + 1) * HALF], h_ps[:, n % 2, 0:HALF], ACT.Gelu,
                                                 bias=b1[:, ds(i % EXPERTS, 1), f:f + 1].rearrange("p a b -> p (a b)")
                                                 ).then_inc(h_used, 1)
                    act.wait_ge(stored, i * 16 + 1)
                    for t in range(CT):
                        act.wait_ge(y_ready, i * CT + t + 2)
                        nc.scalar.activation(ys[:, t, :], y_ps[:, t % 2, 0:D], ACT.Copy).then_inc(y_used, 1)

        @block.tensor
        def _(pe):
            pe.wait_ge(w_in, 16 * 10)
            pe.wait_ge(pick_ready, 4)
            pe.sem_inc(h_used, 2)
            pe.sem_inc(y_used, 2)
            pe.wait_ge(clear, 2)

            def transposes(i, k):
                pe.wait_ge(hot_ready, i * GSETS + k + 1)
                pe.wait_ge(pen_ready, i * GSETS + k + 1)
                for u in range(GSET):
                    mm = nc.tensor.transpose(hot_ps[:, u, :], hot[k][:, u, :], identb[:, :])
                mm.then_inc(hott_ready, 1)
                pe.wait_ge(split_ready, (i + 1) * GSETS + k + 1)
                pe.wait_ge(splt_copied, i * GSETS + k + 1)
                nc.tensor.transpose(splt_ps[:, :], split[k][:, :, :].rearrange("p j m -> p (j m)"), identb[:, :]).then_inc(splt_ready, 1)

            def values(i, k):
                pe.wait_ge(pen_ready, i * GSETS + k + 2)
                pe.wait_ge(splt_copied, i * GSETS + k + 2)
                for u in range(GSET):
                    n = k * GSET + u
                    pe.wait_ge(val_used, i * PER + n + 1)
                    nc.tensor.matmul(val_ps[:, n % 2, :, :], identb[:, :],
                                     pen[k][:, u, :].unsqueeze(1).to_broadcast([P, HEADS, P]), start=True, stop=False)
                    for h in range(HEADS):
                        mm = nc.tensor.matmul(val_ps[:, n % 2, h, :], pick[:, u * HEADS + h, :], splt[k][:, :],
                                              start=False, stop=(h == HEADS - 1))
                    mm.then_inc(val_ready, 1)

            with pe.Fori(0, GSTEPS // 2) as ii:
                for j in range(2):
                    i = ii * 2 + j
                    e, chunk = i % EXPERTS, i // EXPERTS
                    pe.wait_ge(up_in[j], (ii + 1) * 16)
                    for k in range(GSETS):
                        transposes(i, k)
                        for f in range(FC):
                            n = k * FC + f
                            pe.wait_ge(h_used, i * (2 * FC) + n + 1)
                            for c in range(DC):
                                mm = nc.tensor.matmul(h_ps[:, n % 2, 0:HALF],
                                                      W1[j][:, c, f * P:(f + 1) * P],
                                                      XNT[:, c, ds(chunk * (2 * HALF) + k * HALF, HALF)],
                                                      start=(c == 0), stop=(c == DC - 1))
                            mm.then_inc(h_ready, 1)
                        values(i, k)
                    pe.wait_ge(h_used, i * (2 * FC) + 2 * FC + 2)
                    for t in range(CT):
                        pe.wait_ge(y_used, i * CT + t + 1)
                        for f in range(FC):
                            mm = nc.tensor.matmul(y_ps[:, t % 2, 0:D], hid[:, f, t * P:(t + 1) * P],
                                                  W2[:, ds(e, 1), f, :].rearrange("p o d -> p (o d)"), start=(f == 0), stop=(f == FC - 1))
                        mm.then_inc(y_ready, 1)

        @block.vector
        def _(dve):
            link = Link(dve, v)
            dve.sem_inc(hott_ready, 1)
            dve.sem_inc(val_ready, 1)
            dve.sem_inc(y_ready, 1)
            dve.sem_inc(pen_ready, 1)
            dve.sem_inc(splt_copied, 1)
            dve.sem_inc(splt_ready, 1)
            dve.sem_inc(stored, 1)
            nc.vector.memset(grecs[:, GKT:GKT + PER, :], 0.0).then_inc(clear, 1)
            nc.vector.tensor_copy(identb[:, :], ident[:, :]).then_inc(clear, 1)
            for k in range(GSETS):
                link(nc.vector.memset(split[k][:, :, :], 0.0))
            link(nc.vector.memset(tmax[:, :, GKT:GKT + 2], -BIG))
            dve.sem_inc(val_used, 2)
            dve.sem_inc(split_ready, GSETS)
            dve.wait_ge(w_in, 16 * 10)
            with dve.Fori(0, GSTEPS // 2) as ii:
                link.enter(ii, 2 * 4 * GSETS)
                for j in range(2):
                    i = ii * 2 + j
                    for k in range(GSETS):
                        dve.wait_ge(hott_ready, i * GSETS + k + 1) if k else dve.wait_ge(hott_ready, i * GSETS + 1)
                        nc.vector.tensor_tensor(hot[k][:, :, :], grecs[:, ds(i * PER + k * GSET, GSET), 1:2].to_broadcast([P, GSET, P]),
                                                iota[:, :].unsqueeze(1).to_broadcast([P, GSET, P]), ALU.is_equal).then_inc(hot_ready, 1)
                        dve.wait_ge(gathered[k], (i + 1) * (16 * GSET))
                        dve.wait_ge(splt_ready, i * GSETS + k + 1) if k else dve.wait_ge(splt_ready, i * GSETS + 1)
                        value = rows[k][:, :, 16:20]
                        part = lambda q: split[k][:, q, 0:M].rearrange("p (u h) -> p u h", h=HEADS)
                        left = rest[:, :].rearrange("p (u h) -> p u h", h=HEADS)
                        link(nc.vector.tensor_copy(part(0), value))
                        link(nc.vector.tensor_tensor(left, value, part(0), ALU.subtract))
                        link(nc.vector.tensor_copy(part(1), left))
                        link(nc.vector.tensor_tensor(left, left, part(1), ALU.subtract))
                        nc.vector.tensor_copy(part(2), left).then_inc(split_ready, 1)
                        for u in range(GSET):
                            n = k * GSET + u
                            dve.wait_ge(val_ready, i * PER + n + 2)
                            nc.vector.tensor_reduce(tmax[:, :, ds(i * PER + n, 1)].rearrange("p h o -> p (h o)"),
                                                    val_ps[:, n % 2, :, :], AX.X, ALU.max).then_inc(val_used, 1)
                link.leave(GSTEPS // 2)


def block_ends(nc, dve, link, glast, to, values, step):
    with dve.Fori(0, NT // step) as i:
        link.enter(i, step)
        _, ends = nc.values_load_multi_w_load_instructions(glast[0:1, ds(i * step, step)], engines=[dve.engine],
                                                           min_val=0, max_val=GKT)
        for u in range(step):
            link.note(nc.vector.tensor_copy(to[:, ds(i * step + u, 1), :].rearrange("p o c -> p c o"),
                                            values[:, :, ds(ends[u], 1)]))
        link.leave(NT // step)
    link.wait()


def second_update(nc, paused, a, X, iota, ident, gslot, gkeep, glast, grecs, gall, tmax, adst_dram, htab_dram, y_dram, xn_dram):
    with ExitStack() as ctx:
        sb = lambda name, shape, dt=F32: ctx.enter_context(nc.sbuf_tensor(name, shape, dt))
        pb = lambda name, shape, dt=F32: ctx.enter_context(nc.psum_tensor(name, shape, dt))
        sem = lambda name: ctx.enter_context(nc.semaphore(name))
        H, C16 = HEADS, HEADS * EXPERTS
        PER = GSET * GSETS
        adst, htab = sb("adst2", [P, NT, H]), sb("htab2", [P, NT, GW])
        reset = sb("reset", [P, GKT])
        own = sb("own", [P, NT, 2 * H])
        rest, own3 = sb("rest2", [P, NT, 2 * H]), sb("own3", [P, NT, 3, 2 * H], BF16)
        selfw = sb("selfw", [P, NT, H])
        identb = sb("identb2", [P, P], BF16)
        hotb = [sb(f"hotb{k}", [P, GSET, P], BF16) for k in range(GSETS)]
        hott = [sb(f"hott{k}", [P, GSET, P], BF16) for k in range(GSETS)]
        look = sb("look", [P, GKT, 2 * H])
        weight = sb("weight", [P, GKT, H])
        hotf = [sb(f"hotf{k}", [P, GSET, P]) for k in range(GSETS)]
        sums = sb("sums", [P, GW, GKT + 2])
        acc = sb("acc", [P, NT, GW])
        sq, mean, var, root, tmp = (sb("sq", [P, NT, C16]), *(sb(f"{n}3", [P, NT]) for n in ("mean", "var", "root", "tmp")))
        bg = sb("bg", [P, 3, C16])
        den = sb("den", [P, NT, H])
        score, gate, rank, cmp = (sb(n, [P, NT, EXPERTS]) for n in ("score", "gate", "rank2", "cmp"))
        gatet, b2 = sb("gatet", [EXPERTS, NPAD]), sb("b2", [EXPERTS, D])
        yt = [sb(f"yt{k}", [P, EXPERTS, D]) for k in range(3)]
        XN = sb("XN2", [P, NT, D])
        stats, aggr = sb("stats2", [P, NT, 6]), sb("aggr2", [P, NT, 2])
        hot_ps = pb("hot_ps2", [P, 2, 1024], BF16)
        look_ps = pb("look_ps", [P, 2, 512])
        gt_ps, b_ps = pb("gt_ps", [EXPERTS, 2, 512]), pb("b_ps", [P, 2, 512])

        w_in, v = sem("w_in3"), sem("vector_steps3")
        hot_ready, hott_ready, hott_copied, look_ready, look_used = (
            sem(n) for n in ("hotb_ready", "hott_ready2", "hott_copied", "look_ready", "look_used"))
        hotf_ready, sum_ready, sum_used, own_ready, arg_ready, exp_done = (
            sem(n) for n in ("hotf_ready", "sum_ready", "sum_used", "own_ready", "arg_ready", "exp_done"))
        var_ready, std_ready, xn_ready, xn_out = sem("var_ready3"), sem("std_ready3"), sem("xn_ready3"), sem("xn_out3")
        gate_ready, gt_ready, gt_copied, b_ready, x_added = (
            sem(n) for n in ("gate_ready", "gt_ready", "gt_copied", "b_ready", "x_added"))
        y_in = [sem(f"y_in{k}") for k in range(3)]
        msg_ready = sem("msg_ready")
        block = ctx.enter_context(nc.Block())
        GG = -(-NT // 4)

        @block.sync
        def _(sp):
            sp.dma_start(adst[:, :, :], adst_dram).then_inc(w_in, 16)
            sp.dma_start(htab[:, :, :], htab_dram).then_inc(w_in, 16)
            for n, name in enumerate(("L0_ffn_b_gat", "L0_ffn_ln_gamma", "L0_ffn_ln_beta")):
                sp.dma_start(bg[:, n, :], a[name].partition_broadcast(P)).then_inc(w_in, 16)
            sp.dma_start(b2[:, :], a["L0_ffn_b2"]).then_inc(w_in, 16)
            for t in range(NT):
                if t >= 3:
                    sp.wait_ge(x_added, t - 2)
                chunk, tt = divmod(t, CT)
                sp.dma_start(yt[t % 3][:, :, :], y_dram[chunk * EXPERTS:(chunk + 1) * EXPERTS, :, tt, :]
                             .rearrange("e p d -> p e d")).then_inc(y_in[t % 3], 16)
            sp.wait_ge(xn_ready, NT)
            sp.dma_start(xn_dram.rearrange("(t p) d -> p t d", p=P), XN[:, :, :]).then_inc(xn_out, 16)
            sp.wait_ge(xn_out, 16)

        @block.scalar
        def _(act):
            act.wait_ge(own_ready, 1)
            with act.Fori(0, GSTEPS) as i:
                for k in range(GSETS):
                    act.wait_ge(hott_ready, i * GSETS + k + 2)
                    act.wait_ge(look_ready, i * GSETS + 1)
                    nc.scalar.activation(hott[k][:, :, :].rearrange("p u d -> p (u d)"), hot_ps[:, k, 0:GSET * P],
                                         ACT.Copy).then_inc(hott_copied, 1)
            act.wait_ge(arg_ready, 1)
            nc.scalar.activation(weight[:, :, :], weight[:, :, :], ACT.Exp).then_inc(exp_done, 1)
            nc.scalar.activation(selfw[:, :, :], selfw[:, :, :], ACT.Exp).then_inc(exp_done, 1)
            with act.Fori(0, GSTEPS) as i:
                for k in range(GSETS):
                    act.wait_ge(sum_ready, i * GSETS + k + 2)
                    act.sem_inc(paused, 1)
                    nc.scalar.activation(sums[:, :, ds(i * PER + k * GSET, GSET)].rearrange("p c u -> p u c"),
                                         look_ps[:, k, 0:GSET * GW].rearrange("p (u c) -> p u c", c=GW), ACT.Copy).then_inc(sum_used, 1)
            act.wait_ge(var_ready, 1)
            nc.scalar.activation(root[:, :], var[:, :], ACT.Sqrt).then_inc(std_ready, 1)
            act.wait_ge(gate_ready, 1)
            nc.scalar.activation(gate[:, :, :], gate[:, :, :], ACT.Exp).then_inc(exp_done, 1)
            for g in range(GG):
                act.wait_ge(gt_ready, g + 1)
                n = min(4, NT - 4 * g) * P
                nc.scalar.activation(gatet[:, g * 4 * P:g * 4 * P + n], gt_ps[:, g % 2, 0:n], ACT.Copy).then_inc(gt_copied, 1)
            act.wait_ge(var_ready, 2)
            nc.scalar.activation(root[:, :], var[:, :], ACT.Sqrt).then_inc(std_ready, 1)

        @block.tensor
        def _(pe):
            pe.wait_ge(own_ready, 1)
            with pe.Fori(0, GSTEPS) as i:
                _, blocks = nc.values_load_multi_w_load_instructions(gslot[0:1, ds(i * PER, PER)], engines=[pe.engine],
                                                                     min_val=0, max_val=NT - 1)
                for k in range(GSETS):
                    pe.wait_ge(hot_ready, i * GSETS + k + 1)
                    pe.wait_ge(hott_copied, i * GSETS + 1)
                    for u in range(GSET):
                        mm = nc.tensor.transpose(hot_ps[:, k, u * P:(u + 1) * P], hotb[k][:, u, :], identb[:, :])
                    mm.then_inc(hott_ready, 1)
                for k in range(GSETS):
                    pe.wait_ge(hott_copied, i * GSETS + k + 2)
                    pe.wait_ge(look_used, i * GSETS + 1)
                    for u in range(GSET):
                        mm = nc.tensor.matmul(look_ps[:, k, u * 24:(u + 1) * 24], hott[k][:, u, :],
                                              own3[:, ds(blocks[k * GSET + u], 1), :, :].rearrange("p o j c -> p (o j c)"),
                                              start=True, stop=True)
                    mm.then_inc(look_ready, 1)
            pe.wait_ge(msg_ready, 1)
            with pe.Fori(0, GSTEPS) as i:
                for k in range(GSETS):
                    pe.wait_ge(hotf_ready, i * GSETS + k + 1)
                    pe.wait_ge(sum_used, i * GSETS + 1)
                    for u in range(GSET):
                        mm = nc.tensor.matmul(look_ps[:, k, u * GW:(u + 1) * GW], hotf[k][:, u, :],
                                              gall[:, ds(i * PER + k * GSET + u, 1), :].rearrange("p o c -> p (o c)"),
                                              start=True, stop=True)
                    mm.then_inc(sum_ready, 1)
            pe.wait_ge(gate_ready, 2)
            for g in range(GG):
                if g >= 2:
                    pe.wait_ge(gt_copied, g - 1)
                for t in range(4 * g, min(4 * g + 4, NT)):
                    mm = nc.tensor.transpose(gt_ps[:, g % 2, (t % 4) * P:(t % 4 + 1) * P], gate[:, t, :], ident[:, :])
                mm.then_inc(gt_ready, 1)
            pe.wait_ge(gt_copied, GG)
            for t in range(NT):
                if t >= 2:
                    pe.wait_ge(x_added, t - 1)
                nc.tensor.matmul(b_ps[:, t % 2, 0:D], gatet[:, t * P:(t + 1) * P], b2[:, :], start=True, stop=True).then_inc(b_ready, 1)

        @block.vector
        def _(dve):
            link = Link(dve, v)
            dve.sem_inc(hott_ready, 1)
            dve.sem_inc(look_ready, 1)
            dve.sem_inc(hott_copied, 1)
            dve.sem_inc(look_used, 1)
            dve.sem_inc(sum_ready, 1)
            dve.sem_inc(sum_used, 1)
            V = nc.vector

            def leaky(x):
                link(V.scalar_tensor_tensor(x, x, 0.2, x, ALU.mult, ALU.max))

            link.note(V.tensor_copy(identb[:, :], ident[:, :]))
            link.note(V.memset(sums[:, :, GKT:GKT + 2], 0.0))
            link(V.tensor_scalar(reset[:, :], gkeep[:, :], -1.0, BIG, ALU.add, ALU.mult))
            for h in range(H):
                link.note(V.tensor_tensor_scan(tmax[:, h, 0:GKT], reset[:, :], tmax[:, h, 0:GKT], -BIG, ALU.add, ALU.max))
            link.wait()
            block_ends(nc, dve, link, glast, den, tmax, 5)
            dve.wait_ge(w_in, 96)
            asrc, hown = htab[:, :, 16:20], htab[:, :, 0:16]
            link(V.tensor_tensor(den[:, :, :], den[:, :, :], asrc, ALU.max))
            link(V.tensor_tensor(own[:, :, H:2 * H], den[:, :, :], adst[:, :, :], ALU.add))
            leaky(own[:, :, H:2 * H])
            link(V.tensor_copy(own[:, :, 0:H], adst[:, :, :]))
            link(V.tensor_tensor(selfw[:, :, :], asrc, adst[:, :, :], ALU.add))
            leaky(selfw[:, :, :])
            link(V.tensor_tensor(selfw[:, :, :], selfw[:, :, :], own[:, :, H:2 * H], ALU.subtract))
            link(V.tensor_copy(own3[:, :, 0, :], own[:, :, :]))
            link(V.tensor_tensor(rest[:, :, :], own[:, :, :], own3[:, :, 0, :], ALU.subtract))
            link(V.tensor_copy(own3[:, :, 1, :], rest[:, :, :]))
            link(V.tensor_tensor(rest[:, :, :], rest[:, :, :], own3[:, :, 1, :], ALU.subtract))
            link(V.tensor_copy(own3[:, :, 2, :], rest[:, :, :]))
            dve.sem_inc(own_ready, 1)
            with dve.Fori(0, GSTEPS) as i:
                for k in range(GSETS):
                    dve.wait_ge(hott_ready, i * GSETS + 1)
                    V.tensor_tensor(hotb[k][:, :, :], grecs[:, ds(i * PER + k * GSET, GSET), 1:2].to_broadcast([P, GSET, P]),
                                    iota[:, :].unsqueeze(1).to_broadcast([P, GSET, P]), ALU.is_equal).then_inc(hot_ready, 1)
                for k in range(GSETS):
                    dve.wait_ge(look_ready, i * GSETS + k + 2)
                    V.tensor_reduce(look[:, ds(i * PER + k * GSET, GSET), :],
                                    look_ps[:, k, 0:GSET * 24].rearrange("p (u j c) -> p u c j", j=3, c=2 * H),
                                    AX.X, ALU.add).then_inc(look_used, 1)
            dve.wait_ge(look_used, GSTEPS * GSETS + 1)
            link(V.tensor_tensor(weight[:, :, :], gall[:, :, 16:20], look[:, :, 0:H], ALU.add))
            leaky(weight[:, :, :])
            link(V.tensor_tensor(weight[:, :, :], weight[:, :, :], look[:, :, H:2 * H], ALU.subtract))
            link(V.tensor_scalar(weight[:, :, :], weight[:, :, :], 0.0, None, ALU.min))
            dve.sem_inc(arg_ready, 1)
            dve.wait_ge(exp_done, 2)
            g4 = gall[:, :, 0:16].rearrange("p k (h e) -> p k h e", e=EXPERTS)
            for h in range(H):
                link.note(V.tensor_tensor(gall[:, :, h * EXPERTS:(h + 1) * EXPERTS], gall[:, :, h * EXPERTS:(h + 1) * EXPERTS],
                                          weight[:, :, h:h + 1].to_broadcast([P, GKT, EXPERTS]), ALU.mult))
            link.note(V.tensor_copy(gall[:, :, 16:20], weight[:, :, :]))
            link.wait()
            dve.sem_inc(msg_ready, 1)
            with dve.Fori(0, GSTEPS) as i:
                for k in range(GSETS):
                    dve.wait_ge(sum_ready, i * GSETS + 1)
                    V.tensor_tensor(hotf[k][:, :, :], grecs[:, ds(i * PER + k * GSET, GSET), 1:2].to_broadcast([P, GSET, P]),
                                    iota[:, :].unsqueeze(1).to_broadcast([P, GSET, P]), ALU.is_equal).then_inc(hotf_ready, 1)
            dve.wait_ge(sum_used, GSTEPS * GSETS + 1)
            for c in range(GW):
                link.note(V.tensor_tensor_scan(sums[:, c, 0:GKT], gkeep[:, :], sums[:, c, 0:GKT], 0.0, ALU.mult, ALU.add))
            link.wait()
            block_ends(nc, dve, link, glast, acc, sums, 5)
            a3 = lambda x: x.rearrange("p t (h e) -> p t h e", e=EXPERTS)
            for h in range(H):
                part = slice(h * EXPERTS, (h + 1) * EXPERTS)
                link.note(V.tensor_tensor(sq[:, :, part], hown[:, :, part], selfw[:, :, h:h + 1].to_broadcast([P, NT, EXPERTS]), ALU.mult))
            link.wait()
            link(V.tensor_tensor(acc[:, :, 0:16], acc[:, :, 0:16], sq[:, :, :], ALU.add))
            link(V.tensor_tensor(den[:, :, :], acc[:, :, 16:20], selfw[:, :, :], ALU.add))
            link(V.tensor_scalar(den[:, :, :], den[:, :, :], 1e-16, None, ALU.add))
            link(V.reciprocal(den[:, :, :], den[:, :, :]))
            for h in range(H):
                part = slice(h * EXPERTS, (h + 1) * EXPERTS)
                link.note(V.tensor_tensor(acc[:, :, part], acc[:, :, part], den[:, :, h:h + 1].to_broadcast([P, NT, EXPERTS]), ALU.mult))
            link.wait()
            agg = acc[:, :, 0:16]
            spread = lambda n: bg[:, n, :].unsqueeze(1).to_broadcast([P, NT, C16])
            over = lambda x: x.unsqueeze(2).to_broadcast([P, NT, C16])
            link(V.tensor_tensor(agg, agg, spread(0), ALU.add))
            link(V.tensor_reduce(mean[:, :], agg, AX.X, ALU.add))
            link(V.tensor_scalar(mean[:, :], mean[:, :], 1.0 / C16, None, ALU.mult))
            link(V.tensor_tensor(agg, agg, over(mean[:, :]), ALU.subtract))
            link(V.tensor_tensor(sq[:, :, :], agg, agg, ALU.mult))
            link(V.tensor_reduce(var[:, :], sq[:, :, :], AX.X, ALU.add))
            link(V.tensor_scalar(var[:, :], var[:, :], 1.0 / C16, None, ALU.mult))
            inverse_root(dve, link, var[:, :], root[:, :], tmp[:, :], var_ready, std_ready, 1)
            link(V.tensor_tensor(agg, agg, over(root[:, :]), ALU.mult))
            link(V.tensor_tensor(agg, agg, spread(1), ALU.mult))
            link(V.tensor_tensor(agg, agg, spread(2), ALU.add))
            link(V.tensor_reduce(score[:, :, :], agg.rearrange("p t (h e) -> p t e h", e=EXPERTS), AX.X, ALU.add))
            link(V.tensor_scalar(score[:, :, :], score[:, :, :], 1.0 / H, None, ALU.mult))
            link(V.memset(rank[:, :, :], 0.0))
            for e in range(EXPERTS):
                for o in range(EXPERTS):
                    if o != e:
                        link(V.tensor_tensor(cmp[:, :, e], score[:, :, o], score[:, :, e], ALU.is_ge if o < e else ALU.is_gt))
                        link(V.tensor_tensor(rank[:, :, e], rank[:, :, e], cmp[:, :, e], ALU.add))
            link(V.tensor_scalar(rank[:, :, :], rank[:, :, :], 1.5, None, ALU.is_lt))
            link(V.tensor_reduce(tmp[:, :], score[:, :, :], AX.X, ALU.max))
            link(V.tensor_tensor(gate[:, :, :], score[:, :, :], tmp[:, :].unsqueeze(2).to_broadcast([P, NT, EXPERTS]), ALU.subtract))
            dve.sem_inc(gate_ready, 1)
            dve.wait_ge(exp_done, 3)
            link(V.tensor_tensor(gate[:, :, :], gate[:, :, :], rank[:, :, :], ALU.mult))
            link(V.tensor_reduce(tmp[:, :], gate[:, :, :], AX.X, ALU.add))
            link(V.reciprocal(tmp[:, :], tmp[:, :]))
            link(V.tensor_tensor(gate[:, :, :], gate[:, :, :], tmp[:, :].unsqueeze(2).to_broadcast([P, NT, EXPERTS]), ALU.mult))
            dve.sem_inc(gate_ready, 1)
            for t in range(NT):
                dve.wait_ge(y_in[t % 3], 16 * (t // 3 + 1))
                for e in range(EXPERTS):
                    link(V.scalar_tensor_tensor(X[:, t, :], yt[t % 3][:, e, :], gate[:, t, e:e + 1], X[:, t, :], ALU.mult, ALU.add))
                dve.wait_ge(b_ready, t + 1)
                V.tensor_tensor(X[:, t, :], X[:, t, :], b_ps[:, t % 2, 0:D], ALU.add).then_inc(x_added, 1)
            dve.wait_ge(x_added, NT)
            normalise(dve, link, X, XN, stats, aggr, var[:, :], root[:, :], tmp[:, :], var_ready, std_ready, 2, xn_ready)


def sum_relations(nc, paused, iota, slot_win, slot_last, slot_keep, table, pay_dram, z_dram):
    with ExitStack() as ctx:
        sb = lambda name, shape, dt=F32: ctx.enter_context(nc.sbuf_tensor(name, shape, dt))
        pb = lambda name, shape, dt=F32: ctx.enter_context(nc.psum_tensor(name, shape, dt))
        sem = lambda name: ctx.enter_context(nc.semaphore(name))
        PER = SET * SETS
        STEPS = KT // PER
        BW = BASES * WIN
        recs = sb("recs5", [P, KTP, PAYW])
        rows = [sb(f"rrows{k}", [P, SET, D]) for k in range(SETS)]
        idx = [sb(f"ridx{k}", [P, SET], I32) for k in range(SETS)]
        hot = [sb(f"rhot{k}", [P, SET, WIN]) for k in range(SETS)]
        coef = [sb(f"coef{k}", [P, SET, BASES, WIN]) for k in range(SETS)]
        acc = [sb(f"acc{n}", [P, DC * BW]) for n in range(PER)]
        zero = sb("zero", [P, DC * BW])
        part = pb("part5", [P, PER, 512])
        recs_in, idx_ready, v, coef_ready, added = (
            sem(n) for n in ("recs_in5", "ridx_ready", "vector_steps5", "coef_ready5", "added5"))
        gathered = [sem(f"rgathered{k}") for k in range(SETS)]
        summed = [sem(f"rsummed{k}") for k in range(SETS)]
        flushed = [sem(f"flushed{n}") for n in range(PER)]
        zero_ready, zero_out = sem("zero_ready"), sem("zero_out")
        block = ctx.enter_context(nc.Block())

        @block.sync
        def _(sp):
            sp.dma_start(recs[:, :, :], pay_dram.rearrange("(p k) w -> p k w", p=P)).then_inc(recs_in, 16)
            sp.wait_ge(zero_ready, 1)
            for w in range(NW, NT * P // WIN):
                sp.dma_start(z_dram[w], zero[:, :]).then_inc(zero_out, 16)
            with sp.Fori(0, STEPS) as i:
                _, wins = nc.values_load_multi_w_load_instructions(slot_win[0:1, ds(i * PER, PER)], engines=[sp.engine],
                                                                   min_val=0, max_val=NW - 1)
                _, lasts = nc.values_load_multi_w_load_instructions(slot_last[0:1, ds(i * PER, PER)], engines=[sp.engine],
                                                                    min_val=0, max_val=1)
                for n in range(PER):
                    sp.wait_ge(added, (i + 1) * PER + n + 1)
                    sp.dma_start(z_dram[ds(wins[n], 1)].rearrange("o p w -> (o p) w"), acc[n][:, :],
                                 cond=lasts[n] > 0).then_inc(flushed[n], 16)
            sp.wait_ge(zero_out, 16 * (NT * P // WIN - NW))
            for n in range(PER):
                sp.wait_ge(flushed[n], 16 * STEPS + 1)

        @block.scalar
        def _(act):
            act.wait_ge(recs_in, 16)
            with act.Fori(0, STEPS) as i:
                for k in range(SETS):
                    act.wait_ge(summed[k], i + 1)
                    nc.scalar.activation(idx[k][:, :].unsqueeze(2), recs[:, ds(i * PER + k * SET, SET), 0:1].bitcast(I32),
                                         ACT.Copy).then_inc(idx_ready, 1)

        @block.gpsimd
        def _(pool):
            with pool.Fori(0, STEPS) as i:
                for k in range(SETS):
                    pool.wait_ge(idx_ready, i * SETS + k + 1)
                    pool.sem_inc(paused, 1)
                    for u in range(SET):
                        pool.indirect_dma_start(rows[k][:, u, :], None, table,
                                                bass.IndirectOffsetOnAxis(ap=idx[k][:, u:u + 1].bitcast(U32), axis=0)
                                                ).then_inc(gathered[k], 16)

        @block.tensor
        def _(pe):
            with pe.Fori(0, STEPS) as i:
                for k in range(SETS):
                    pe.wait_ge(coef_ready, i * SETS + k + 1)
                    pe.wait_ge(added, i * PER + (k + 1) * SET)
                    pe.wait_ge(gathered[k], (i + 1) * (16 * SET))
                    for u in range(SET):
                        for c in range(DC):
                            mm = nc.tensor.matmul(part[:, k * SET + u, c * BW:(c + 1) * BW], rows[k][:, u, c * P:(c + 1) * P],
                                                  coef[k][:, u, :, :].rearrange("p b w -> p (b w)"), start=True, stop=True)
                    mm.then_inc(summed[k], 1)

        @block.vector
        def _(dve):
            link = Link(dve, v)
            for k in range(SETS):
                dve.sem_inc(summed[k], 1)
            for n in range(PER):
                dve.sem_inc(flushed[n], 1)
            V = nc.vector
            V.memset(zero[:, :], 0.0).then_inc(zero_ready, 1)
            link(V.memset(acc[PER - 1][:, :], 0.0))
            dve.wait_ge(recs_in, 16)

            def weights(i, k):
                cols = ds(i * PER + k * SET, SET)
                link(V.tensor_tensor(hot[k][:, :, :], recs[:, cols, 1:2].to_broadcast([P, SET, WIN]),
                                     iota[:, 0:WIN].unsqueeze(1).to_broadcast([P, SET, WIN]), ALU.is_equal))
                V.tensor_tensor(coef[k][:, :, :, :], hot[k][:, :, :].unsqueeze(2).to_broadcast([P, SET, BASES, WIN]),
                                recs[:, cols, 2:2 + BASES].unsqueeze(3).to_broadcast([P, SET, BASES, WIN]),
                                ALU.mult).then_inc(coef_ready, 1)

            def step(i, more):
                for k in range(SETS):
                    dve.wait_ge(summed[k], i + 2)
                    for u in range(SET):
                        n = k * SET + u
                        dve.wait_ge(flushed[n], i * 16 + 1)
                        dve.wait_ge(added, i * PER + n + PER)
                        V.scalar_tensor_tensor(acc[n][:, :], acc[(n - 1) % PER][:, :], slot_keep[:, ds(i * PER + n, 1)],
                                               part[:, n, :], ALU.mult, ALU.add).then_inc(added, 1)
                    if more:
                        weights(i + 1, k)

            dve.sem_inc(added, PER)
            for k in range(SETS):
                weights(0, k)
            with dve.Fori(0, STEPS - 1) as i:
                link.enter(i, SETS)
                step(i, True)
                link.leave(STEPS - 1)
            step(STEPS - 1, False)


def third_update(nc, a, X, iota, ident, ones, z_dram, out):
    with ExitStack() as ctx:
        sb = lambda name, shape, dt=F32: ctx.enter_context(nc.sbuf_tensor(name, shape, dt))
        pb = lambda name, shape, dt=F32: ctx.enter_context(nc.psum_tensor(name, shape, dt))
        sem = lambda name: ctx.enter_context(nc.semaphore(name))
        BW, WT = BASES * WIN, P // WIN
        E8, K2 = 8, 2
        CAPACITY = float(-(-N * 5 // (4 * E8)))
        bases = sb("bases", [P, BASES, DC, D])
        z = [sb(f"z{k}", [P, WT, DC * BW]) for k in range(2)]
        zn = [sb(f"zn{k}", [P, DC * BASES, WT, WIN]) for k in range(2)]
        XN, XNT = sb("XN6", [P, NT, D]), sb("XNT6", [P, DC, NPAD])
        stats, aggr = sb("stats6", [P, NT, 6]), sb("aggr6", [P, NT, 2])
        var, root, tmp = sb("var6", [P, NT]), sb("root6", [P, NT]), sb("tmp6", [P, NT])
        wr, br = sb("wr", [P, DC, E8]), sb("br", [P, E8])
        mean = sb("mean6", [P, DC, P])
        lg, r1, r2, top, sm = (sb(n, [P, E8]) for n in ("lg", "r1", "r2", "top", "sm"))
        larger, equal, earlier = (sb(n, [P, E8, E8]) for n in ("larger", "equal", "earlier"))
        which = sb("which", [P, K2], I32)
        wgt = sb("wgt", [P, K2])
        W1 = [sb(f"V1_{k}", [P, DC, FE]) for k in range(K2)]
        W2 = [sb(f"V2_{k}", [P, FC, D]) for k in range(K2)]
        b1, b2 = sb("b1_6", [P, K2, FC]), sb("b2_6", [P, K2, D])
        gam, bet, bias = sb("gam", [P, D]), sb("bet", [P, D]), sb("bias6", [P, D])
        hid = [sb(f"hid6_{k}", [P, FC, 2 * HALF]) for k in range(1)]
        z_ps = pb("z_ps", [P, 2, 512])
        xnt_ps = pb("xnt_ps6", [P, 2, 512])
        h_ps, y_ps = pb("h_ps6", [P, 2, 512]), pb("y_ps6", [P, 2, 512])
        w_in, v, e_in = sem("w_in6"), sem("vector_steps6"), sem("experts_in")
        z_in = [sem("z_in0"), sem("z_in1")]
        z_ready, z_added, z_turned = sem("z_ready"), sem("z_added"), sem("z_turned")
        var_ready, std_ready, xn_ready = sem("var_ready6"), sem("std_ready6"), sem("xn_ready6")
        psum_free, xnt_ready = sem("psum_free6"), sem("xnt_ready6")
        mean_ready, mean_copied, logits_ready, arg_ready, exp_done, picked = (
            sem(n) for n in ("mean_ready", "mean_copied", "logits_ready", "arg_ready6", "exp_done6", "picked"))
        h_ready, h_used, y_ready, y_used = (sem(n) for n in ("h_ready6", "h_used6", "y_ready6", "y_used6"))
        out_ready, out_done = sem("out_ready"), sem("out_done6")
        block = ctx.enter_context(nc.Block())
        GROUPS = -(-NT * DC // 4)

        @block.sync
        def _(sp):
            sp.dma_start(bases[:, :, :, :], a["L1_gnn_bases"].rearrange("b (c p) d -> p b c d", p=P)).then_inc(w_in, 16)
            sp.dma_start(wr[:, :, :], a["L1_ffn_Wr"].rearrange("(c p) e -> p c e", p=P)).then_inc(w_in, 16)
            sp.dma_start(br[:, :], a["L1_ffn_br"].partition_broadcast(P)).then_inc(w_in, 16)
            sp.dma_start(gam[:, :], a["L1_ffn_gamma"].partition_broadcast(P)).then_inc(w_in, 16)
            sp.dma_start(bet[:, :], a["L1_ffn_beta"].partition_broadcast(P)).then_inc(w_in, 16)
            for t in range(NT):
                if t >= 2:
                    sp.wait_ge(z_turned, t - 1)
                sp.dma_start(z[t % 2][:, :, :], z_dram[t * WT:(t + 1) * WT].rearrange("w p x -> p w x")).then_inc(z_in[t % 2], 16)
            sp.wait_ge(picked, 1)
            _, chosen = nc.values_load_multi_w_load_instructions(which[0:1, :], engines=[sp.engine],
                                                                 min_val=0, max_val=E8 - 1, bass_reorder=False)
            for k in range(K2):
                e = ds(chosen[k], 1)
                sp.dma_start(W1[k][:, :, :], a["L1_ffn_W1"][e].rearrange("o (c p) f -> p (o c) f", p=P)).then_inc(e_in, 16)
                sp.dma_start(W2[k][:, :, :], a["L1_ffn_W2"][e].rearrange("o (c p) f -> p (o c) f", p=P)).then_inc(e_in, 16)
                sp.dma_start(b1[:, k, :], a["L1_ffn_b1"][e].rearrange("o (c p) -> p (o c)", p=P),
                             allow_slow_non_contiguous=True).then_inc(e_in, 16)
                sp.dma_start(b2[:, k, :], a["L1_ffn_b2"][e].rearrange("o d -> (o d)").partition_broadcast(P)).then_inc(e_in, 16)
            sp.wait_ge(out_ready, NT)
            sp.dma_start(out[0:NFULL * P, :].rearrange("(t p) d -> p t d", p=P), XN[:, 0:NFULL, :]).then_inc(out_done, 16)
            sp.dma_start(out[NFULL * P:N, :], XN[0:NTAIL, NFULL, :]).then_inc(out_done, 16)
            sp.wait_ge(out_done, 32)

        @block.scalar
        def _(act):
            for t in range(NT):
                act.wait_ge(z_in[t % 2], 16 * (t // 2 + 1))
                if t >= 2:
                    act.wait_ge(z_ready, t - 1)
                nc.scalar.activation(zn[t % 2][:, :, :, :], z[t % 2][:, :, :].rearrange("p w (k d) -> p k w d", d=WIN),
                                     ACT.Copy).then_inc(z_turned, 1)
            act.wait_ge(var_ready, 1)
            nc.scalar.activation(root[:, :], var[:, :], ACT.Sqrt).then_inc(std_ready, 1)
            act.wait_ge(mean_ready, 1)
            for c in range(DC):
                nc.scalar.activation(mean[:, c, :], z_ps[:, c, 0:1].to_broadcast([P, P]), ACT.Copy, scale=1.0 / N).then_inc(mean_copied, 1)
            for n in range(3):
                act.wait_ge(arg_ready, n + 1)
                x = sm[:, 0:1] if n == 2 else sm[:, :]
                nc.scalar.activation(x, x, ACT.Exp).then_inc(exp_done, 1)
            copy_transposed(nc.scalar, XNT, xnt_ps, psum_free, xnt_ready)
            act.wait_ge(e_in, 16 * 4 * K2)
            for unit in range(CHUNKS * K2):
                for n in range(2 * FC):
                    half, f = divmod(n, FC)
                    act.wait_ge(h_ready, unit * 2 * FC + n + 1)
                    if n == 0 and unit:
                        act.wait_ge(y_ready, unit * CT)
                    nc.scalar.activation(hid[0][:, f, half * HALF:(half + 1) * HALF], h_ps[:, n % 2, 0:HALF], ACT.Gelu,
                                         bias=b1[:, unit % K2, f:f + 1]).then_inc(h_used, 1)
            act.wait_ge(var_ready, 2)
            nc.scalar.activation(root[:, :], var[:, :], ACT.Sqrt).then_inc(std_ready, 1)

        @block.tensor
        def _(pe):
            pe.wait_ge(w_in, 16 * 5)
            for t in range(NT):
                pe.wait_ge(z_turned, t + 1)
                if t >= 2:
                    pe.wait_ge(z_added, t - 1)
                for n, (c, b) in enumerate((c, b) for c in range(DC) for b in range(BASES)):
                    mm = nc.tensor.matmul(z_ps[:, t % 2, 0:D], zn[t % 2][:, c * BASES + b, :, :].rearrange("p w d -> p (w d)"), bases[:, b, c, :],
                                          start=(n == 0), stop=(n == DC * BASES - 1))
                mm.then_inc(z_ready, 1)
            pe.wait_ge(xn_ready, NT)
            for c in range(DC):
                for t in range(NT):
                    n = P if t < NFULL else NTAIL
                    mm = nc.tensor.matmul(z_ps[:, c, 0:1], XN[0:n, t, c * P:(c + 1) * P], ones[0:n, 0:1],
                                          start=(t == 0), stop=(t == NT - 1))
            mm.then_inc(mean_ready, 1)
            pe.wait_ge(mean_copied, DC)
            for c in range(DC):
                mm = nc.tensor.matmul(y_ps[:, 0, 0:E8], mean[:, c, :], wr[:, c, :], start=(c == 0), stop=(c == DC - 1))
            mm.then_inc(logits_ready, 1)
            transpose_nodes(nc.tensor, ident, XN, xnt_ps, psum_free, xnt_ready)
            pe.wait_ge(psum_free, GROUPS)
            pe.wait_ge(e_in, 16 * 4 * K2)
            for unit in range(CHUNKS * K2):
                chunk, k = divmod(unit, K2)
                for n in range(2 * FC):
                    half, f = divmod(n, FC)
                    if unit * 2 * FC + n >= 2:
                        pe.wait_ge(h_used, unit * 2 * FC + n - 1)
                    lo = chunk * 2 * HALF + half * HALF
                    for c in range(DC):
                        mm = nc.tensor.matmul(h_ps[:, n % 2, 0:HALF], W1[k][:, c, f * P:(f + 1) * P], XNT[:, c, lo:lo + HALF],
                                              start=(c == 0), stop=(c == DC - 1))
                    mm.then_inc(h_ready, 1)
                pe.wait_ge(h_used, (unit + 1) * 2 * FC)
                for t in range(CT):
                    if unit * CT + t >= 2:
                        pe.wait_ge(y_used, unit * CT + t - 1)
                    for f in range(FC):
                        mm = nc.tensor.matmul(y_ps[:, (unit * CT + t) % 2, 0:D], hid[0][:, f, t * P:(t + 1) * P], W2[k][:, f, :],
                                              start=(f == 0), stop=(f == FC - 1))
                    mm.then_inc(y_ready, 1)

        @block.vector
        def _(dve):
            link = Link(dve, v)
            V = nc.vector
            for t in range(NT):
                dve.wait_ge(z_ready, t + 1)
                V.scalar_tensor_tensor(X[:, t, :], z_ps[:, t % 2, 0:D], 0.0, X[:, t, :], ALU.max, ALU.add).then_inc(z_added, 1)
            dve.wait_ge(z_added, NT)
            normalise(dve, link, X, XN, stats, aggr, var[:, :], root[:, :], tmp[:, :], var_ready, std_ready, 1, xn_ready)

            def softmax(x, n):
                link(V.tensor_reduce(tmp[:, 0:1], x, AX.X, ALU.max))
                link(V.tensor_scalar(sm[:, :], x, tmp[:, 0:1], None, ALU.subtract))
                dve.sem_inc(arg_ready, 1)
                dve.wait_ge(exp_done, n)
                link(V.tensor_reduce(tmp[:, 0:1], sm[:, :], AX.X, ALU.add))
                link(V.reciprocal(tmp[:, 0:1], tmp[:, 0:1]))
                link(V.tensor_scalar(x, sm[:, :], tmp[:, 0:1], None, ALU.mult))

            dve.wait_ge(logits_ready, 1)
            link(V.tensor_tensor(lg[:, :], y_ps[:, 0, 0:E8], br[:, :], ALU.add))
            softmax(lg[:, :], 1)
            link(V.tensor_scalar(r1[:, :], lg[:, :], float(N), None, ALU.mult))
            link(V.tensor_scalar(r2[:, :], r1[:, :], CAPACITY, None, ALU.max))
            link(V.reciprocal(r2[:, :], r2[:, :]))
            link(V.tensor_scalar(r2[:, :], r2[:, :], CAPACITY, None, ALU.mult))
            link(V.tensor_scalar(r1[:, :], r1[:, :], CAPACITY, None, ALU.is_gt))
            link(V.scalar_tensor_tensor(r2[:, :], r2[:, :], -1.0, r1[:, :], ALU.add, ALU.mult))
            link(V.tensor_scalar(r2[:, :], r2[:, :], 1.0, None, ALU.add))
            link(V.tensor_tensor(lg[:, :], lg[:, :], r2[:, :], ALU.mult))
            softmax(lg[:, :], 2)
            e_of = lambda x: x.unsqueeze(2).to_broadcast([P, E8, E8])
            o_of = lambda x: x.unsqueeze(1).to_broadcast([P, E8, E8])
            link.note(V.tensor_tensor(larger[:, :, :], o_of(lg[:, :]), e_of(lg[:, :]), ALU.is_gt))
            link.note(V.tensor_tensor(equal[:, :, :], o_of(lg[:, :]), e_of(lg[:, :]), ALU.is_equal))
            link(V.tensor_tensor(earlier[:, :, :], o_of(iota[:, 0:E8]), e_of(iota[:, 0:E8]), ALU.is_lt))
            link(V.tensor_tensor(equal[:, :, :], equal[:, :, :], earlier[:, :, :], ALU.mult))
            link(V.tensor_tensor(larger[:, :, :], larger[:, :, :], equal[:, :, :], ALU.add))
            link(V.tensor_reduce(r1[:, :], larger[:, :, :], AX.X, ALU.add))
            for k in range(K2):
                link(V.tensor_scalar(r2[:, :], r1[:, :], float(k), None, ALU.is_equal))
                link(V.tensor_tensor(sm[:, :], r2[:, :], iota[:, 0:E8], ALU.mult))
                link(V.tensor_reduce(tmp[:, 0:1], sm[:, :], AX.X, ALU.add))
                link(V.tensor_copy(which[:, k:k + 1], tmp[:, 0:1]))
                link(V.tensor_tensor(sm[:, :], r2[:, :], lg[:, :], ALU.mult))
                link(V.tensor_reduce(top[:, k:k + 1], sm[:, :], AX.X, ALU.add))
            dve.sem_inc(picked, 1)
            link(V.tensor_tensor(sm[:, 0:1], top[:, 1:2], top[:, 0:1], ALU.subtract))
            dve.sem_inc(arg_ready, 1)
            dve.wait_ge(exp_done, 3)
            link(V.tensor_scalar(tmp[:, 0:1], sm[:, 0:1], 1.0, None, ALU.add))
            link(V.reciprocal(wgt[:, 0:1], tmp[:, 0:1]))
            link(V.tensor_tensor(wgt[:, 1:2], wgt[:, 0:1], sm[:, 0:1], ALU.mult))
            dve.wait_ge(e_in, 16 * 4 * K2)
            link(V.tensor_scalar(bias[:, :], b2[:, 0, :], wgt[:, 0:1], None, ALU.mult))
            link(V.scalar_tensor_tensor(bias[:, :], b2[:, 1, :], wgt[:, 1:2], bias[:, :], ALU.mult, ALU.add))
            dve.wait_ge(psum_free, GROUPS)
            for t in range(NT):
                link.note(V.tensor_tensor(XN[:, t, :], XN[:, t, :], bias[:, :], ALU.add))
            link.wait()
            for unit in range(CHUNKS * K2):
                chunk, k = divmod(unit, K2)
                for t in range(CT):
                    node = chunk * CT + t
                    if k:
                        dve.wait_ge(y_used, (unit - 1) * CT + t + 1)
                    dve.wait_ge(y_ready, unit * CT + t + 1)
                    V.scalar_tensor_tensor(XN[:, node, :], y_ps[:, (unit * CT + t) % 2, 0:D], wgt[:, k:k + 1], XN[:, node, :],
                                           ALU.mult, ALU.add).then_inc(y_used, 1)
            dve.wait_ge(y_used, CHUNKS * K2 * CT)
            for t in range(NT):
                link.note(V.bn_stats(stats[:, t, :], XN[:, t, :]))
            link.wait()
            for t in range(NT):
                link.note(V.bn_aggr(aggr[:, t, :], stats[:, t, :]))
            link.wait()
            link(V.tensor_copy(var[:, :], aggr[:, :, 1]))
            inverse_root(dve, link, var[:, :], root[:, :], tmp[:, :], var_ready, std_ready, 2)
            for t in range(NT):
                link.note(V.tensor_scalar(XN[:, t, :], XN[:, t, :], aggr[:, t, 0:1], root[:, t:t + 1], ALU.subtract, ALU.mult))
            link.wait()
            for t in range(NT):
                link.note(V.tensor_tensor(XN[:, t, :], XN[:, t, :], gam[:, :], ALU.mult))
                link.note(V.tensor_tensor(X[:, t, :], X[:, t, :], bet[:, :], ALU.add))
            link.wait()
            for t in range(NT):
                V.tensor_tensor(XN[:, t, :], XN[:, t, :], X[:, t, :], ALU.add).then_inc(out_ready, 1)


_INS = ["x", "src", "dst", "edge_type_32", "edge_weight1", "L0_gnn_weight", "L0_gnn_bias", "L0_ffn_W_gat",
        "L0_ffn_att_src", "L0_ffn_att_dst", "L0_ffn_b_gat", "L0_ffn_ln_gamma", "L0_ffn_ln_beta", "L0_ffn_W1",
        "L0_ffn_b1", "L0_ffn_W2", "L0_ffn_b2", "L0_ffn_edge_index", "L1_gnn_bases", "L1_gnn_w_comp", "L1_ffn_Wr",
        "L1_ffn_br", "L1_ffn_W1", "L1_ffn_b1", "L1_ffn_W2", "L1_ffn_b2", "L1_ffn_gamma", "L1_ffn_beta"]


def kernel(**inputs):
    import numpy as _np
    import concourse.bacc as _bacc
    from concourse import mybir as _mybir
    from concourse.bass_utils import run_bass_kernel_spmd as _run

    nc = _bacc.Bacc("TRN2", target_bir_lowering=False, num_devices=1)
    arrays, aps = {}, {}
    for name in _INS:
        arr = _np.ascontiguousarray(inputs[name])
        arrays[f"in_{name}"] = arr
        aps[name] = nc.dram_tensor(f"in_{name}", arr.shape, _mybir.dt.from_np(arr.dtype), kind="ExternalInput").ap()
    out = nc.dram_tensor("out_0", (N, D), _mybir.dt.float32, kind="ExternalOutput").ap()
    gnn_ffn(nc, aps, out)
    return _run(nc, [arrays], core_ids=[0]).results[0]["out_0"]
```

```python
import concourse.bass as bass
from concourse import mybir
from contextlib import ExitStack

F32, BF16, I32, U32, U8 = (mybir.dt.float32, mybir.dt.bfloat16, mybir.dt.int32, mybir.dt.uint32, mybir.dt.uint8)
ALU = mybir.AluOpType
ACT = mybir.ActivationFunctionType
AX = mybir.AxisListType

P = 128
N = 3125
D = 256
DC = D // P
NT = -(-N // P)
NFULL = N // P
NTAIL = N - NFULL * P
NPAD = NT * P
EPS = 1e-5

E = 50000
WIN = 32
NW = -(-N // WIN)
ET = -(-E // P) + 1
EROWS = E // ET
EREST = E - EROWS * ET
STAGE = 14
BLOCKS = P * ET // P
KT = 488
KG = -(-KT // P)
WORDS = 4
RELS, BASES = 32, 8
QT = 4
KA = 416
RQ = 12
RS = -(-KT // RQ)
assert -(-E // P) + NT - 1 <= KA and -(-E // P) + NW - 1 <= KT <= RQ * RS <= KG * P and ET % (2 * STAGE) == 0 and EROWS == P - 1

GE = 32768
GT = GE // P
GKT = 280
GSTAGE = 8
GSPLIT = (4, 3, 9)
assert (GE + (P - 1) * NT) // P <= GKT
HEADS, EXPERTS = 4, 4
GW = HEADS * EXPERTS + HEADS


class Link:

    def __init__(self, sem):
        self.sem, self.count, self.base = sem, 0, 0

    def on(self, eng):
        self.eng = eng
        return self

    def __call__(self, ins):
        self.note(ins)
        self.eng.wait_ge(self.sem, self.base + self.count)

    def note(self, ins):
        self.count += 1
        ins.then_inc(self.sem, 1)

    def wait(self):
        self.eng.wait_ge(self.sem, self.base + self.count)

    def enter(self, i, per_step):
        self.kept, self.per_step = self.count, per_step
        self.base, self.count = i * per_step + self.kept, 0

    def leave(self, steps):
        assert self.count == self.per_step, (self.count, self.per_step)
        self.base, self.count = 0, self.kept + steps * self.per_step


class Common:

    def __init__(self, sem):
        self.paused = sem("paused")
        self.link = Link(sem("vector_steps"))
        self.var_ready, self.std_ready = sem("var_ready"), sem("std_ready")
        self.gathered = [sem(f"gathered{k}") for k in range(SETS)]
        self.summed = [sem(f"summed{k}") for k in range(SETS)]
        self.flushed = [sem(f"flushed{n}") for n in range(SET * SETS)]


def ds(start, size):
    return bass.ds(start, size)


def gnn_ffn(nc, a, out, stop=99):
    scratch = lambda name, shape, dt: nc.dram_tensor(name, shape, dt, kind="Internal").ap()
    xn_dram = scratch("xn_table", (NPAD, D), F32)
    list_dram = scratch("edge_list", (P * ET, WORDS), F32)
    gpay_dram = scratch("attention_records", (P * GKT, 2), F32)
    with ExitStack() as whole:
        common = Common(lambda name: whole.enter_context(nc.semaphore(name)))
        sb = lambda name, shape, dt=F32: whole.enter_context(nc.sbuf_tensor(name, shape, dt))
        X = sb("X", [P, NT, D])
        iota = sb("iota", [P, P])
        ident = sb("ident", [P, P])
        ones = sb("ones", [P, P])
        fine = Slots(sb, "fine", NW, WIN, KT)
        coefs = sb("coefs", [P, RQ * RS, BASES])
        gslot = sb("gslot", [1, GKT], I32)
        gkeep = sb("gkeep", [P, GKT])
        glast = sb("glast", [1, NT], I32)
        with ExitStack() as early:
            sb = lambda name, shape, dt=F32: early.enter_context(nc.sbuf_tensor(name, shape, dt))
            grow = sb("grow", [P, GT], I32)
            gpay = sb("gpay", [P, GT, 2])
            coarse = Slots(sb, "coarse", NT, P, KA)
            relf, norm = sb("relation", [P, RQ * RS]), sb("norm", [P, RQ * RS])
            sort_edges(nc, common, a, X, iota, ident, ones, fine, coarse, relf, norm,
                       grow, gpay, gslot, gkeep, glast, xn_dram, list_dram, gpay_dram)
            if stop <= 1:
                return
            agg_dram = scratch("neighbour_sums", (NT, P, D + 1), F32)
            sum_neighbours(nc, common, a, iota, ident, coarse, relf, norm, coefs, agg_dram, xn_dram)
            table_dram = scratch("attention_table", (NPAD, GW), F32)
            xnt_dram = scratch("xn1_transposed", (P, DC, NPAD), F32)
            adst_dram = scratch("a_dst", (P, NT, HEADS), F32)
            htab_dram = scratch("h_table", (P, NT, GW), F32)
            first_update(nc, common, a, X, ident, agg_dram, grow, gpay, gpay_dram, table_dram, xnt_dram, adst_dram, htab_dram)
        if stop <= 2:
            return
        y_dram = scratch("expert_rows", (EXPERTS * CHUNKS, P, CT, D), F32)
        with ExitStack() as late:
            sl = lambda name, shape, dt=F32: late.enter_context(nc.sbuf_tensor(name, shape, dt))
            grecs = sl("grecs", [P, GKT + GSET * GSETS, 2])
            gall = sl("gall", [P, GKT, GW])
            tmax = sl("tmax", [P, HEADS, GKT + 2])
            attention_maxima(nc, common, a, iota, ident, grecs, gall, tmax, gpay_dram, table_dram, xnt_dram, y_dram)
            if stop <= 3:
                return
            second_update(nc, common, a, X, iota, ident, gslot, gkeep, glast, grecs, gall, tmax, adst_dram, htab_dram, y_dram, xn_dram)
        if stop <= 4:
            return
        z_dram = scratch("basis_sums", (NT * P // WIN, P, DC * BASES * WIN), F32)
        sum_relations(nc, common, iota, fine, coefs, xn_dram, z_dram)
        if stop <= 5:
            return
        third_update(nc, common, a, X, iota, ident, ones, z_dram, out)


def count_windows(dve, link, windows, unroll, T, win, iota, hot, count):
    with dve.Fori(0, windows // unroll) as i:
        link.enter(i, unroll)
        for u in range(unroll):
            w = i * unroll + u
            link.note(dve.tensor_scalar(hot[:, ds(w, 1), 0:T].rearrange("p o t -> p (o t)"), win[:, 0:T],
                                                   iota[:, ds(w, 1)], None, ALU.is_equal, ALU.add,
                                                   accum_out=count[:, ds(w, 1)]))
        link.leave(windows // unroll)
    link.wait()


def rank_edges(dve, link, windows, unroll, T, hot, start, rank, pos):
    with dve.Fori(0, windows // unroll) as i:
        link.enter(i, 3 * unroll)
        for u in range(unroll):
            w = i * unroll + u
            row = hot[:, ds(w, 1), 0:T].rearrange("p o t -> p (o t)")
            link(dve.tensor_tensor_scan(rank[:, 0:T], row, row, start[:, ds(w, 1)], ALU.add, ALU.max))
            link(dve.tensor_tensor(rank[:, 0:T], rank[:, 0:T], row, ALU.mult))
            link(dve.tensor_tensor(pos[:, 0:T], pos[:, 0:T], rank[:, 0:T], ALU.add))
        link.leave(windows // unroll)


def rows_of(dve, link, T, columns, pos, pos_i, rank, row_i):
    link(dve.tensor_scalar(pos_i[:, 0:T], pos[:, 0:T], -1.0, None, ALU.add))
    link(dve.tensor_scalar(row_i[:, 0:T], pos_i[:, 0:T], P - 1, None, ALU.bitwise_and))
    link(dve.tensor_copy(rank[:, 0:T], row_i[:, 0:T]))
    link(dve.tensor_scalar(row_i[:, 0:T], pos_i[:, 0:T], 7, None, ALU.arith_shift_right))
    link(dve.tensor_copy(pos[:, 0:T], row_i[:, 0:T]))
    link(dve.scalar_tensor_tensor(row_i[:, 0:T], rank[:, 0:T], float(columns), pos[:, 0:T], ALU.mult, ALU.add))


def inverse_root(dve, link, var, root, tmp, var_ready, std_ready, n):
    link(dve.tensor_scalar(var, var, EPS, None, ALU.add))
    dve.sem_inc(var_ready, 1)
    dve.wait_ge(std_ready, n)
    link(dve.reciprocal(root, root))
    link(dve.tensor_tensor(tmp, root, root, ALU.mult))
    link(dve.tensor_tensor(tmp, tmp, var, ALU.mult))
    link(dve.tensor_scalar(tmp, tmp, -0.5, 1.5, ALU.mult, ALU.add))
    link(dve.tensor_tensor(root, root, tmp, ALU.mult))


def normalise(dve, link, X, XN, stats, aggr, var, root, tmp, var_ready, std_ready, n, xn_ready):
    for t in range(NT):
        link.note(dve.bn_stats(stats[:, t, :], X[:, t, :]))
    link.wait()
    for t in range(NT):
        link.note(dve.bn_aggr(aggr[:, t, :], stats[:, t, :]))
    link.wait()
    link(dve.tensor_copy(var, aggr[:, :, 1]))
    inverse_root(dve, link, var, root, tmp, var_ready, std_ready, n)
    for t in range(NT):
        dve.tensor_scalar(XN[:, t, :], X[:, t, :], aggr[:, t, 0:1], root[:, t:t + 1],
                          ALU.subtract, ALU.mult).then_inc(xn_ready, 1)


def stage_columns(act, staged, cols, idx, rec, rows, pay):
    act.activation(rec[:, :, :], pay[:, cols, :], ACT.Copy).then_inc(staged, 1)
    act.activation(idx[:, :], rows[:, cols], ACT.Copy).then_inc(staged, 1)


def stage_first(act, staged, first, width, idx, rec, rows, pay):
    for k in range(2):
        stage_columns(act, staged, ds(first + k * width, width), idx[k], rec[k], rows, pay)


def stage_rest(act, staged, scattered, steps, first, width, idx, rec, rows, pay):
    with act.Fori(1, steps) as i:
        for k in range(2):
            act.wait_ge(scattered[k], i * (16 * width))
            stage_columns(act, staged, ds(i * (2 * width) + (first + k * width), width), idx[k], rec[k], rows, pay)


def scatter_staged(pool, paused, staged, scattered, steps, width, idx, rec, dram):
    with pool.Fori(0, steps) as i:
        for k in range(2):
            pool.wait_ge(staged, i * 4 + 2 * k + 2)
            pool.sem_inc(paused, 1)
            for t in range(width):
                pool.indirect_dma_start(dram, bass.IndirectOffsetOnAxis(ap=idx[k][:, t:t + 1].bitcast(U32), axis=0),
                                        rec[k][:, t, :], None).then_inc(scattered[k], 16)
    for k in range(2):
        pool.wait_ge(scattered[k], 16 * width * steps)


class Slots:

    def __init__(self, sb, name, groups, nodes, count):
        self.groups, self.nodes, self.count, self.wide = groups, nodes, count, -(-count // P)
        self.group = sb(name + "_group", [1, count], I32)
        self.last = sb(name + "_last", [1, count], I32)
        self.keep = sb(name + "_keep", [P, count])
        self.source = sb(name + "_source", [P, count], I32)
        self.target = sb(name + "_target", [P, count])

    def scratch(self, sb, name):
        n = self.groups
        self.start, self.end = sb(name + "_start", [P, n]), sb(name + "_end", [P, n])
        self.first_i, self.last_i = sb(name + "_first_i", [P, n], I32), sb(name + "_last_i", [P, n], I32)
        self.first, self.tiles, self.shift = sb(name + "_first", [P, n]), sb(name + "_tiles", [P, n]), sb(name + "_shift", [P, n])
        self.col, self.pair = sb(name + "_col", [P, 1]), sb(name + "_pair", [P, 2])
        self.full, self.ge = sb(name + "_full", [P, self.wide * P]), sb(name + "_ge", [P, self.wide * P])
        self.base, self.at = sb(name + "_base", [P, self.wide]), sb(name + "_at", [P, self.wide])
        self.block = sb(name + "_block", [P, self.wide], I32)


def place_slots(V, link, ident, slot_iota, z):
    n = z.groups
    link.note(V.tensor_copy(z.first_i[:, :], z.start[:, :]))
    link(V.tensor_scalar(z.last_i[:, :], z.end[:, :], float(P - 1), None, ALU.add))
    link.note(V.tensor_scalar(z.first_i[:, :], z.first_i[:, :], 7, None, ALU.arith_shift_right))
    link(V.tensor_scalar(z.last_i[:, :], z.last_i[:, :], 7, None, ALU.arith_shift_right))
    link.note(V.tensor_copy(z.first[:, :], z.first_i[:, :]))
    link(V.tensor_copy(z.tiles[:, :], z.last_i[:, :]))
    link(V.tensor_tensor(z.tiles[:, :], z.tiles[:, :], z.first[:, :], ALU.subtract))
    link(V.tensor_scalar(z.tiles[:, :], z.tiles[:, :], 1.0, None, ALU.max))
    link(V.tensor_tensor_scan(z.end[:, :], z.tiles[:, :], z.tiles[:, :], 0.0, ALU.add, ALU.max))
    link(V.tensor_tensor(z.shift[:, :], z.first[:, :], z.end[:, :], ALU.subtract))
    link(V.tensor_tensor(z.shift[:, :], z.shift[:, :], z.tiles[:, :], ALU.add))
    link.note(V.memset(z.first[:, n - 1:n], 0.0))
    link(V.tensor_tensor(z.first[:, 0:n - 1], z.shift[:, 1:n], z.shift[:, 0:n - 1], ALU.subtract))
    link(V.tensor_tensor(z.full[:, 0:n], ident[:, 0:n], z.end[:, :], ALU.mult))
    link(V.tensor_reduce(z.col[:, :], z.full[:, 0:n], AX.X, ALU.add))
    link(V.tensor_tensor(z.full[:, 0:n], ident[:, 0:n], z.first[:, :], ALU.mult))
    link.note(V.tensor_reduce(z.pair[:, 1:2], z.full[:, 0:n], AX.X, ALU.add))
    link.note(V.memset(z.pair[:, 0:1], 1.0))
    link(V.tensor_scalar(z.ge[:, :], slot_iota[:, 0:z.wide * P], z.col[:, :], None, ALU.is_ge))


def count_ends(pe, ones, z, end_ps, pair_ps):
    n = z.groups
    for j in range(z.wide):
        pe.matmul(pair_ps[:, j, :], z.ge[0:n, j * P:(j + 1) * P], z.pair[0:n, :], start=True, stop=True)
    return pe.matmul(end_ps[:, 0:z.wide * P], ones[0:n, :], z.ge[0:n, :], start=True, stop=True)


def describe_slots(V, link, slot_at, z, end_ps, pair_ps):
    K = z.count
    link(V.tensor_scalar(z.full[:, :], end_ps[:, 0:z.wide * P], float(z.groups - 1), None, ALU.min))
    link.note(V.tensor_copy(z.group[:, :], z.full[0:1, 0:K]))
    link.note(V.memset(z.keep[:, 0:1], 0.0))
    link.note(V.memset(z.last[:, K - 1:K], 1))
    link.note(V.tensor_tensor(z.keep[:, 1:K], z.full[:, 1:K], z.full[:, 0:K - 1], ALU.is_equal))
    link.note(V.tensor_tensor(z.last[:, 0:K - 1], z.full[0:1, 1:K], z.full[0:1, 0:K - 1], ALU.not_equal))
    link.note(V.tensor_scalar(z.base[:, :], pair_ps[:, :, 0], float(z.groups - 1), float(z.nodes), ALU.min, ALU.mult))
    link(V.tensor_tensor(z.at[:, :], pair_ps[:, :, 1], slot_at[:, 0:z.wide], ALU.add))
    link(V.tensor_scalar(z.block[:, :], z.at[:, :], float(BLOCKS - 1), None, ALU.min))


def sort_edges(nc, common, a, X, iota, ident, ones, fine, coarse, relf, norm,
               grow, gpay, gslot, gkeep, glast, xn_dram, list_dram, gpay_dram):
    paused, var_ready, std_ready = common.paused, common.var_ready, common.std_ready
    with ExitStack() as ctx:
        sb = lambda name, shape, dt=F32: ctx.enter_context(nc.sbuf_tensor(name, shape, dt))
        sem = lambda name: ctx.enter_context(nc.semaphore(name))
        W1 = NW + 1
        GBINS, UN = 5, 3
        XN = sb("XN0", [P, NT, D])
        stats, aggr, rstd = sb("stats0", [P, NT, 6]), sb("aggr0", [P, NT, 2]), sb("rstd0", [P, NT])
        var, tmp = sb("var0", [P, NT]), sb("tmp0", [P, NT])
        before = sb("before", [P, P])
        dst, nxt, src, rel = (sb(n, [P, ET], I32) for n in ("dst", "next_dst", "src", "rel"))
        norm_in = sb("norm_in", [P, ET])
        rec = sb("rec", [P, ET, WORDS])
        hot = sb("hot", [P, W1, ET], U8)
        win = sb("win", [P, ET])
        count, start = sb("count", [P, W1 + 1]), sb("start", [P, W1])
        total, place_end = sb("total", [P, W1]), sb("place_end", [P, W1])
        kinds = (fine, coarse)
        for z, name in zip(kinds, ("fine", "coarse")):
            z.scratch(sb, name)
        rank, pos = sb("rank", [P, ET]), sb("pos", [P, ET])
        pos_i, row_i = sb("pos_i", [P, ET], I32), sb("row_i", [P, ET], I32)
        gdst, gsrc, gtmp, glow = (sb(n, [P, GT], I32) for n in ("gdst", "gsrc", "gtmp", "glow"))
        gwin, ghot, gcount, gstart = sb("gwin", [P, GT]), sb("gonehot", [P, NT, GT], U8), sb("gcount", [P, NT]), sb("gstart", [P, NT])
        gtotal, gtiles, gend = sb("gtotal", [P, NT], I32), sb("gtiles", [P, NT]), sb("gend", [P, NT])
        gpad = sb("gpad", [P, GKT * 2])
        unsorted = sb("unsorted", [1, 1], I32)
        slot_iota, slot_full, slot_ge = (sb(n, [P, KG * P]) for n in ("slot_iota", "slot_full", "slot_ge"))
        slot_at = sb("slot_at", [P, KG])
        tile_col = sb("tile_col", [P, 1])
        slot_rec = [sb(f"slot_rec{n}", [P, z.wide, P, WORDS]) for n, z in enumerate(kinds)]
        gidx = [sb(f"gidx0{k}", [P, GSTAGE], I32) for k in range(2)]
        grec = [sb(f"grec0{k}", [P, GSTAGE, 2]) for k in range(2)]
        idx_stage = [sb(f"idx_stage{k}", [P, STAGE], I32) for k in range(2)]
        rec_stage = [sb(f"rec_stage{k}", [P, STAGE, WORDS]) for k in range(2)]
        consts = sem("consts")
        x_in, list_in, glist_in = sem("x_in"), sem("list_in"), sem("glist_in")
        cleared, pads_out = sem("cleared"), sem("pads_out")
        gcount_ready, gprefix_ready, gend_ready, gend_done, grows_ready = (
            sem(n) for n in ("gcount_ready", "gprefix_ready", "gend_ready", "gend_done", "grows_ready"))
        count_ready, prefix_ready, end_ready, end_done = (sem(n) for n in ("count_ready", "prefix_ready", "end_ready", "end_done"))
        rec_ready, list_out = sem("rec_ready"), sem("list_out")
        gstaged, gscattered = [sem(f"gstaged{n}") for n in range(2)], [[sem(f"gscattered{n}{k}") for k in range(2)] for n in range(2)]
        vs, rows_ready, staged = sem("sort_steps"), sem("rows_ready"), sem("staged")
        scattered = [sem("scattered0"), sem("scattered1")]
        slots_in, offset, turned, slots_made = (sem(n) for n in ("slots_in", "offset", "turned", "slots_made"))
        xn_ready, xn_out = sem("xn_ready"), sem("xn_out")

        with ExitStack() as counting, nc.Block() as block:
            pb = lambda name, shape: counting.enter_context(nc.psum_tensor(name, shape, F32))
            cnt_ps, gcnt_ps = pb("cnt_ps", [P, 2, 256]), pb("gcnt_ps", [P, 2, 256])
            gend_ps = pb("gend_ps", [P, 512])
            end_ps, pair_ps = [pb(f"end_ps{n}", [P, 512]) for n in range(2)], [pb(f"pair_ps{n}", [P, KG, 2]) for n in range(2)]

            @block.sync
            def _(sp):
                for tile, row in ((gsrc, 0), (gdst, 1)):
                    sp.dma_start(tile[:, :], a["L0_ffn_edge_index"][row, :].rearrange("(p t) -> p t", t=GT)).then_inc(glist_in, 16)
                sp.wait_ge(cleared, 8)
                for tile, name in ((dst, "dst"), (src, "src"), (rel, "edge_type_32"), (norm_in, "edge_weight1")):
                    flat = a[name].rearrange("e o -> (e o)") if name == "edge_weight1" else a[name]
                    sp.dma_start(tile[0:EROWS, :], flat[0:EROWS * ET].rearrange("(p t) -> p t", t=ET)).then_inc(list_in, 16)
                    sp.dma_start(tile[EROWS:P, 0:EREST], flat[EROWS * ET:E].rearrange("(p t) -> p t", p=1)).then_inc(list_in, 16)
                sp.dma_start(nxt[0:EROWS, :], a["dst"][1:EROWS * ET + 1].rearrange("(p t) -> p t", t=ET)).then_inc(list_in, 16)
                sp.dma_start(nxt[EROWS:P, 0:EREST - 1], a["dst"][EROWS * ET + 1:E].rearrange("(p t) -> p t", p=1)).then_inc(list_in, 16)
                sp.dma_start(gpay_dram.rearrange("(p k) w -> p (k w)", p=P), gpad[:, :]).then_inc(pads_out, 16)
                sp.dma_start(X[:, 0:NFULL, :], a["x"][0:NFULL * P, :].rearrange("(t p) d -> p t d", p=P)).then_inc(x_in, 16)
                sp.dma_start(X[0:NTAIL, NFULL, :], a["x"][NFULL * P:N, :]).then_inc(x_in, 16)
                sp.wait_ge(rec_ready, WORDS)
                sp.dma_start(list_dram.rearrange("(p t) w -> p t w", p=P), rec[:, :, :]).then_inc(list_out, 16)
                sp.wait_ge(list_out, 16)
                sp.wait_ge(x_in, 32)

            @block.gpsimd
            def _(pool):
                nc.gpsimd.iota(iota[:, :], [[1, P]], base=0, channel_multiplier=0, allow_small_or_imprecise_dtypes=True).then_inc(consts, 1)
                nc.gpsimd.iota(slot_iota[:, :], [[1, KG * P]], base=0, channel_multiplier=0, allow_small_or_imprecise_dtypes=True).then_inc(consts, 1)
                nc.gpsimd.iota(slot_at[:, :], [[P, KG]], base=0, channel_multiplier=1, allow_small_or_imprecise_dtypes=True).then_inc(consts, 1)
                nc.gpsimd.memset(ones[:, :], 1.0).then_inc(consts, 1)
                pool.wait_ge(consts, 4)
                nc.gpsimd.affine_select(out=ident[:, :], in_=ones[:, :], compare_op=ALU.is_equal, fill=0.0, base=0,
                                        pattern=[[-1, P]], channel_multiplier=1).then_inc(consts, 1)
                nc.gpsimd.affine_select(out=before[:, :], in_=ones[:, :], compare_op=ALU.is_gt, fill=0.0, base=0,
                                        pattern=[[1, P]], channel_multiplier=-1).then_inc(consts, 1)
                pool.wait_ge(pads_out, 16)
                scatter_staged(pool, paused, gstaged[0], gscattered[0], GSPLIT[0], GSTAGE, gidx, grec, gpay_dram)

            @block.scalar
            def _(act):
                act.wait_ge(list_in, 16 * 10)
                for w, tile in enumerate((src, dst, rel, norm_in)):
                    nc.scalar.activation(rec[:, :, w:w + 1], tile[:, :].unsqueeze(2), ACT.Copy).then_inc(rec_ready, 1)
                act.wait_ge(grows_ready, 1)
                stage_first(nc.scalar, gstaged[0], 0, GSTAGE, gidx, grec, grow, gpay)
                stage_rest(nc.scalar, gstaged[0], gscattered[0], GSPLIT[0], 0, GSTAGE, gidx, grec, grow, gpay)

            @block.tensor
            def _(pe):
                pe.wait_ge(consts, 6)
                pe.wait_ge(gcount_ready, 1)
                nc.tensor.matmul(gcnt_ps[:, 0, 0:NT], before[:, :], gcount[:, :], start=True, stop=True)
                nc.tensor.matmul(gcnt_ps[:, 1, 0:NT], ones[:, :], gcount[:, :], start=True, stop=True).then_inc(gprefix_ready, 1)
                pe.wait_ge(gend_ready, 1)
                nc.tensor.matmul(gend_ps[:, 0:GKT], ones[0:NT, :], slot_ge[0:NT, 0:GKT], start=True, stop=True).then_inc(gend_done, 1)
                pe.wait_ge(count_ready, 1)
                nc.tensor.matmul(cnt_ps[:, 0, 0:W1], before[:, :], count[:, 0:W1], start=True, stop=True)
                nc.tensor.matmul(cnt_ps[:, 1, 0:W1 + 1], ones[:, :], count[:, :], start=True, stop=True).then_inc(prefix_ready, 1)
                for n, z in enumerate(kinds):
                    pe.wait_ge(end_ready, n + 1)
                    count_ends(nc.tensor, ones, z, end_ps[n], pair_ps[n]).then_inc(end_done, 1)

            @block.vector
            def _(dve):
                link = common.link.on(dve)
                V = nc.vector
                V.memset(gpad[:, :], 0.0).then_inc(cleared, 1)
                dve.wait_ge(cleared, 1)
                V.memset(gpad[:, :].rearrange("p (k w) -> p k w", w=2)[:, :, 1:2], -1.0).then_inc(cleared, 1)
                for tile, fill in ((dst, NW * WIN), (nxt, NW * WIN), (src, 0), (rel, 0), (norm_in, 0.0), (X[:, NFULL, :], 0.0)):
                    V.memset(tile[:, :], fill).then_inc(cleared, 1)
                link(V.memset(pos[:, 0:GT], 0.0))
                dve.wait_ge(glist_in, 32)
                dve.wait_ge(consts, 6)
                link.note(V.tensor_scalar(gtmp[:, :], gdst[:, :], 7, None, ALU.arith_shift_right))
                link(V.tensor_scalar(glow[:, :], gdst[:, :], P - 1, None, ALU.bitwise_and))
                link.note(V.tensor_copy(gwin[:, :], gtmp[:, :]))
                link.note(V.tensor_copy(gpay[:, :, 0:1].bitcast(I32), gsrc[:, :].unsqueeze(2)))
                link(V.tensor_copy(gpay[:, :, 1:2], glow[:, :].unsqueeze(2)))
                count_windows(dve, link, NT, GBINS, GT, gwin, iota, ghot, gcount)
                dve.sem_inc(gcount_ready, 1)
                dve.wait_ge(gprefix_ready, 1)
                link(V.tensor_scalar(gtotal[:, :], gcnt_ps[:, 1, 0:NT], float(P - 1), None, ALU.add))
                link(V.tensor_scalar(gtotal[:, :], gtotal[:, :], 7, None, ALU.arith_shift_right))
                link(V.tensor_copy(gtiles[:, :], gtotal[:, :]))
                link(V.tensor_tensor_scan(gend[:, :], gtiles[:, :], gtiles[:, :], 0.0, ALU.add, ALU.max))
                link(V.tensor_tensor(gstart[:, :], gend[:, :], gtiles[:, :], ALU.subtract))
                link(V.tensor_scalar(gstart[:, :], gstart[:, :], float(P), None, ALU.mult))
                link(V.tensor_tensor(gstart[:, :], gstart[:, :], gcnt_ps[:, 0, 0:NT], ALU.add))
                rank_edges(dve, link, NT, GBINS, GT, ghot, gstart, rank, pos)
                rows_of(dve, link, GT, GKT, pos, pos_i, rank, grow)
                dve.sem_inc(grows_ready, 1)
                link(V.tensor_scalar(rank[:, 0:NT], gtiles[:, :], 0.5, float(GKT + 1), ALU.is_lt, ALU.mult))
                link(V.tensor_tensor(rank[:, 0:NT], rank[:, 0:NT], gend[:, :], ALU.max))
                link(V.tensor_scalar(glast[:, :], rank[0:1, 0:NT], -1.0, None, ALU.add))
                link(V.tensor_tensor(slot_full[:, 0:NT], ident[:, 0:NT], gend[:, :], ALU.mult))
                link(V.tensor_reduce(tile_col[:, :], slot_full[:, 0:NT], AX.X, ALU.add))
                link(V.tensor_scalar(slot_ge[:, 0:GKT], slot_iota[:, 0:GKT], tile_col[:, :], None, ALU.is_ge))
                dve.sem_inc(gend_ready, 1)
                dve.wait_ge(list_in, 16 * 10)
                link.note(V.tensor_scalar(row_i[:, :], dst[:, :], 5, None, ALU.arith_shift_right))
                link(V.tensor_scalar(pos_i[:, :], nxt[:, :], 5, None, ALU.arith_shift_right))
                link.note(V.tensor_copy(win[:, :], row_i[:, :]))
                link(V.tensor_tensor(rank[:, :], row_i[:, :], pos_i[:, :], ALU.is_gt))
                link(V.tensor_reduce(count[:, W1:W1 + 1], rank[:, :], AX.X, ALU.add))
                count_windows(dve, link, W1, UN, ET, win, iota, hot, count)
                dve.sem_inc(count_ready, 1)
                dve.wait_ge(gend_done, 1)
                link(V.tensor_scalar(slot_full[:, 0:GKT], gend_ps[:, 0:GKT], float(NT - 1), None, ALU.min))
                link.note(V.tensor_copy(gslot[:, :], slot_full[0:1, 0:GKT]))
                link.note(V.memset(gkeep[:, 0:1], 0.0))
                link(V.tensor_tensor(gkeep[:, 1:GKT], slot_full[:, 1:GKT], slot_full[:, 0:GKT - 1], ALU.is_equal))
                dve.wait_ge(prefix_ready, 1)
                link.note(V.tensor_scalar(unsorted[:, :], cnt_ps[0:1, 1, W1:W1 + 1], 1.0, None, ALU.min))
                link(V.tensor_copy(total[:, :], cnt_ps[:, 1, 0:W1]))
                link(V.tensor_tensor_scan(place_end[:, :], total[:, :], total[:, :], 0.0, ALU.add, ALU.max))
                link(V.tensor_tensor(start[:, :], place_end[:, :], total[:, :], ALU.subtract))
                link.note(V.tensor_copy(fine.start[:, :], start[:, 0:NW]))
                link.note(V.tensor_copy(fine.end[:, :], place_end[:, 0:NW]))
                ratio = coarse.nodes // fine.nodes
                link.note(V.tensor_copy(coarse.start[:, :], start[:, 0:NW:ratio]))
                link.note(V.tensor_copy(coarse.end[:, 0:NT - 1], start[:, ratio:NW:ratio]))
                link(V.memset(coarse.end[:, NT - 1:NT], float(E)))
                for z in kinds:
                    place_slots(V, link, ident, slot_iota, z)
                    dve.sem_inc(end_ready, 1)
                link(V.tensor_tensor(start[:, :], start[:, :], cnt_ps[:, 0, 0:W1], ALU.add))
                for n, z in enumerate(kinds):
                    dve.wait_ge(end_done, n + 1)
                    describe_slots(V, link, slot_at, z, end_ps[n], pair_ps[n])

        with nc.Block() as block:
            @block.vector
            def _(dve):
                wrong = nc.values_load(unsorted[0:1, 0:1], engines=[dve.engine], min_val=0, max_val=1)
                with dve.If(wrong > 0):
                    link = Link(vs).on(dve)
                    link(nc.vector.memset(pos[:, :], 0.0))
                    rank_edges(dve, link, W1, UN, ET, hot, start, rank, pos)
                    nc.vector.tensor_scalar(row_i[:, :], pos[:, :], -1.0, None, ALU.add).then_inc(rows_ready, 1)

            @block.scalar
            def _(act):
                wrong = nc.values_load(unsorted[0:1, 0:1], engines=[act.engine], min_val=0, max_val=1)
                with act.If(wrong > 0):
                    act.wait_ge(rows_ready, 1)
                    stage_first(nc.scalar, staged, 0, STAGE, idx_stage, rec_stage, row_i, rec)
                    stage_rest(nc.scalar, staged, scattered, ET // (2 * STAGE), 0, STAGE, idx_stage, rec_stage, row_i, rec)

            @block.gpsimd
            def _(pool):
                wrong = nc.values_load(unsorted[0:1, 0:1], engines=[pool.engine], min_val=0, max_val=1)
                with pool.If(wrong > 0):
                    scatter_staged(pool, paused, staged, scattered, ET // (2 * STAGE), STAGE, idx_stage, rec_stage, list_dram)

        with ExitStack() as turn, nc.Block() as block:
            rec_ps = turn.enter_context(nc.psum_tensor("rec_ps", [P, 6, KG * P], F32))
            words = [(0, 0, fine.source), (0, 1, fine.target), (0, 2, relf), (0, 3, norm), (1, 0, coarse.source), (1, 1, coarse.target)]

            @block.sync
            def _(sp):
                sp.wait_ge(xn_ready, NT)
                sp.dma_start(xn_dram.rearrange("(t p) d -> p t d", p=P), XN[:, :, :]).then_inc(xn_out, 16)
                sp.wait_ge(xn_out, 16)

            @block.gpsimd
            def _(pool):
                blocks = list_dram.rearrange("(b e) w -> b (e w)", e=P)
                for n, z in enumerate(kinds):
                    for j in range(z.wide):
                        pool.indirect_dma_start(slot_rec[n][:, j, :, :].rearrange("p e w -> p (e w)"), None, blocks,
                                                bass.IndirectOffsetOnAxis(ap=z.block[:, j:j + 1].bitcast(U32), axis=0)
                                                ).then_inc(slots_in, 16)
                scatter_staged(pool, paused, gstaged[1], gscattered[1], GSPLIT[1], GSTAGE, gidx, grec, gpay_dram)

            @block.scalar
            def _(act):
                first_col = GSPLIT[0] * 2 * GSTAGE
                stage_first(nc.scalar, gstaged[1], first_col, GSTAGE, gidx, grec, grow, gpay)
                for m, (n, w, to) in enumerate(words):
                    act.wait_ge(turned, m + 1)
                    nc.scalar.activation(to[:, :], rec_ps[:, m, 0:to.shape[1]], ACT.Copy).then_inc(slots_made, 1)
                act.wait_ge(var_ready, 1)
                nc.scalar.activation(rstd[:, :], var[:, :], ACT.Sqrt).then_inc(std_ready, 1)
                stage_rest(nc.scalar, gstaged[1], gscattered[1], GSPLIT[1], first_col, GSTAGE, gidx, grec, grow, gpay)

            @block.tensor
            def _(pe):
                pe.wait_ge(offset, 1)
                for m, (n, w, to) in enumerate(words):
                    for j in range(kinds[n].wide):
                        mm = nc.tensor.transpose(rec_ps[:, m, j * P:(j + 1) * P], slot_rec[n][:, j, :, w], ident[:, :])
                    mm.then_inc(turned, 1)

            @block.vector
            def _(dve):
                link = common.link.on(dve)
                dve.wait_ge(slots_in, 16 * sum(z.wide for z in kinds))
                for n, z in enumerate(kinds):
                    for j in range(z.wide):
                        at = slot_rec[n][:, j, :, 1]
                        link.note(nc.vector.tensor_scalar(at, at, z.base[:, j:j + 1], None, ALU.subtract))
                link.wait()
                dve.sem_inc(offset, 1)
                normalise(dve, link, X, XN, stats, aggr, var[:, :], rstd[:, :], tmp[:, :], var_ready, std_ready, 1, xn_ready)


SET = 2
SETS = 4


def sum_neighbours(nc, common, a, iota, ident, coarse, relf, norm, coefs, agg_dram, table):
    paused, gathered, summed, flushed = common.paused, common.gathered, common.summed, common.flushed
    with ExitStack() as ctx:
        sb = lambda name, shape, dt=F32: ctx.enter_context(nc.sbuf_tensor(name, shape, dt))
        pb = lambda name, shape, dt=F32: ctx.enter_context(nc.psum_tensor(name, shape, dt))
        sem = lambda name: ctx.enter_context(nc.semaphore(name))
        PER = SET * SETS
        STEPS = KA // PER
        BANKS = 4
        rows = [sb(f"rows{k}", [P, SET, D + 1]) for k in range(SETS)]
        idx = [sb(f"idx{k}", [P, SET], I32) for k in range(SETS)]
        hot = [sb(f"hot{k}", [P, SET, P]) for k in range(SETS)]
        acc = [sb(f"tile_acc{n}", [P, D + 1]) for n in range(PER)]
        part = pb("part", [P, BANKS, 512])
        relhot = sb("relhot", [P, RQ, RELS])
        relhot_t = sb("relhot_t", [P, RQ // QT, P])
        wcomp = sb("wcomp", [P, QT, BASES])
        relt_ps, coef_ps = pb("relt_ps", [P, 512]), pb("coef_ps", [P, 512])
        idx_ready, hot_ready, added, cleared = (sem(n) for n in ("idx_ready", "hot_ready", "added", "cleared1"))
        wc_in, relhot_ready, relt_ready, relt_copied, coef_ready, coefs_made = (
            sem(n) for n in ("wc_in", "relhot_ready", "relt_ready", "relt_copied", "coef_ready", "coefs_made"))
        block = ctx.enter_context(nc.Block())
        parts = ((0, RS, True), (RS, STEPS, False))

        @block.sync
        def _(sp):
            sp.wait_ge(cleared, 2)
            for q in range(QT):
                sp.dma_start(wcomp[q * RELS:(q + 1) * RELS, q, :], a["L1_gnn_w_comp"]).then_inc(wc_in, 16)
            with sp.Fori(0, STEPS) as i:
                _, tiles = nc.values_load_multi_w_load_instructions(coarse.group[0:1, ds(i * PER, PER)], engines=[sp.engine],
                                                                    min_val=0, max_val=NT - 1)
                _, lasts = nc.values_load_multi_w_load_instructions(coarse.last[0:1, ds(i * PER, PER)], engines=[sp.engine],
                                                                    min_val=0, max_val=1)
                for n in range(PER):
                    sp.wait_ge(added, i * PER + (BANKS + n + 1))
                    sp.dma_start(agg_dram[ds(tiles[n], 1)].rearrange("o p d -> (o p) d"), acc[n][:, :],
                                 cond=lasts[n] > 0).then_inc(flushed[n], 16)
            for n in range(PER):
                sp.wait_ge(flushed[n], 16 * STEPS + 1)

        @block.scalar
        def _(act):
            for lo, hi, coefficients in parts:
                with act.Fori(lo, hi) as i:
                    for k in range(SETS):
                        act.wait_ge(summed[k], i + 1)
                        nc.scalar.activation(idx[k][:, :], coarse.source[:, ds(i * PER + k * SET, SET)], ACT.Copy).then_inc(idx_ready, 1)
                    if coefficients:
                        act.wait_ge(relt_ready, i + 1)
                        nc.scalar.activation(relhot_t[:, :, :].rearrange("p q e -> p (q e)"), relt_ps[:, 0:RQ // QT * P],
                                             ACT.Copy).then_inc(relt_copied, 1)

        @block.gpsimd
        def _(pool):
            pool.wait_ge(cleared, 2 + SETS)
            with pool.Fori(0, STEPS) as i:
                for k in range(SETS):
                    pool.wait_ge(idx_ready, i * SETS + k + 1)
                    pool.sem_inc(paused, 1)
                    for u in range(SET):
                        pool.indirect_dma_start(rows[k][:, u, 0:D], None, table,
                                                bass.IndirectOffsetOnAxis(ap=idx[k][:, u:u + 1].bitcast(U32), axis=0)
                                                ).then_inc(gathered[k], 16)

        @block.tensor
        def _(pe):
            pe.wait_ge(wc_in, 16 * QT)
            for lo, hi, coefficients in parts:
                with pe.Fori(lo, hi) as i:
                    for k in range(SETS):
                        if k == 1 and coefficients:
                            pe.wait_ge(relhot_ready, i + 1)
                            for q in range(RQ // QT):
                                mm = nc.tensor.transpose(relt_ps[:, q * P:(q + 1) * P],
                                                         relhot[:, q * QT:(q + 1) * QT, :].rearrange("p q r -> p (q r)"), ident[:, :])
                            mm.then_inc(relt_ready, 1)
                        pe.wait_ge(hot_ready, i * SETS + k + 1)
                        pe.wait_ge(gathered[k], (i + 1) * (16 * SET))
                        for u in range(SET):
                            n = k * SET + u
                            pe.wait_ge(added, i * PER + n + 1)
                            mm = nc.tensor.matmul(part[:, n % BANKS, 0:D + 1], hot[k][:, u, :], rows[k][:, u, :], start=True, stop=True)
                        mm.then_inc(summed[k], 1)
                    if coefficients:
                        pe.wait_ge(relt_copied, i + 1)
                        pe.wait_ge(coefs_made, i + 1)
                        for q in range(RQ // QT):
                            mm = nc.tensor.matmul(coef_ps[:, q * QT * BASES:(q + 1) * QT * BASES], relhot_t[:, q, :],
                                                  wcomp[:, :, :].rearrange("p q b -> p (q b)"), start=True, stop=True)
                        mm.then_inc(coef_ready, 1)

        @block.vector
        def _(dve):
            V = nc.vector
            dve.sem_inc(coefs_made, 1)
            for k in range(SETS):
                dve.sem_inc(summed[k], 1)
            for n in range(PER):
                dve.sem_inc(flushed[n], 1)
            V.memset(wcomp[:, :, :], 0.0).then_inc(cleared, 1)
            V.memset(acc[PER - 1][:, :], 0.0).then_inc(cleared, 1)
            for k in range(SETS):
                V.memset(rows[k][:, :, D:D + 1], 1.0).then_inc(cleared, 1)
            dve.wait_ge(cleared, 2 + SETS)
            dve.sem_inc(added, BANKS)

            def places(i, k):
                V.tensor_tensor(hot[k][:, :, :], coarse.target[:, ds(i * PER + k * SET, SET)].unsqueeze(2).to_broadcast([P, SET, P]),
                                iota[:, :].unsqueeze(1).to_broadcast([P, SET, P]), ALU.is_equal).then_inc(hot_ready, 1)

            def relations(i):
                V.tensor_tensor(relhot[:, :, :], relf[:, ds(i * RQ, RQ)].unsqueeze(2).to_broadcast([P, RQ, RELS]),
                                iota[:, 0:RELS].unsqueeze(1).to_broadcast([P, RQ, RELS]), ALU.is_equal).then_inc(relhot_ready, 1)

            def step(i, more, coefficients, more_coefficients):
                for k in range(SETS):
                    for u in range(SET):
                        n = k * SET + u
                        if u == 0:
                            dve.wait_ge(summed[k], i + 2)
                        dve.wait_ge(flushed[n], i * 16 + 1)
                        dve.wait_ge(added, i * PER + n + BANKS)
                        V.scalar_tensor_tensor(acc[n][:, :], acc[(n - 1) % PER][:, :], coarse.keep[:, ds(i * PER + n, 1)],
                                               part[:, n % BANKS, 0:D + 1], ALU.mult, ALU.add).then_inc(added, 1)
                        if more and u == 0:
                            places(i + 1, k)
                if coefficients:
                    dve.wait_ge(coef_ready, i + 1)
                    V.tensor_tensor(coefs[:, ds(i * RQ, RQ), :], coef_ps[:, 0:RQ * BASES].rearrange("p (t b) -> p t b", b=BASES),
                                    norm[:, ds(i * RQ, RQ)].unsqueeze(2).to_broadcast([P, RQ, BASES]), ALU.mult).then_inc(coefs_made, 1)
                if more_coefficients:
                    relations(i + 1)

            for k in range(SETS):
                places(0, k)
            relations(0)
            with dve.Fori(0, RS - 1) as i:
                step(i, True, True, True)
            step(RS - 1, True, True, False)
            with dve.Fori(RS, STEPS - 1) as i:
                step(i, True, False, False)
            step(STEPS - 1, False, False, False)


def transpose_nodes(pe, ident, XN, xnt_ps, psum_free, xnt_ready, first=0, loads=None):
    for n, (t, c) in enumerate((t, c) for t in range(NT) for c in range(DC)):
        g, q = divmod(n, 4)
        if loads and c == 0 and t in loads[0]:
            pe.wait_ge(loads[1][loads[0].index(t)], 16)
        if q == 0 and g >= 2:
            pe.wait_ge(psum_free, first + g - 1)
        mm = pe.transpose(xnt_ps[:, g % 2, q * P:(q + 1) * P], XN[:, t, c * P:(c + 1) * P], ident[:, :])
        if q == 3 or n == NT * DC - 1:
            mm.then_inc(xnt_ready, 1)


def copy_transposed(act, XNT, xnt_ps, psum_free, xnt_ready, first=0):
    groups = -(-NT * DC // 4)
    for g in range(groups):
        act.wait_ge(xnt_ready, first + g + 1)
        tiles = min(4, NT * DC - 4 * g) // DC
        act.activation(XNT[:, :, g * 2 * P:(g * 2 + tiles) * P].rearrange("p c (t n) -> p t c n", n=P),
                       xnt_ps[:, g % 2, 0:tiles * DC * P].rearrange("p (t c n) -> p t c n", c=DC, n=P),
                       ACT.Copy).then_inc(psum_free, 1)


def first_update(nc, common, a, X, ident, agg_dram, grow, gpay, gpay_dram, table_dram, xnt_dram, adst_dram, htab_dram):
    paused, var_ready, std_ready = common.paused, common.var_ready, common.std_ready
    with ExitStack() as ctx:
        sb = lambda name, shape, dt=F32: ctx.enter_context(nc.sbuf_tensor(name, shape, dt))
        pb = lambda name, shape, dt=F32: ctx.enter_context(nc.psum_tensor(name, shape, dt))
        sem = lambda name: ctx.enter_context(nc.semaphore(name))
        W, b = sb("W_gnn", [P, DC, D]), sb("b_gnn", [P, D])
        wgat = sb("wgat", [P, DC, HEADS * EXPERTS])
        att = sb("att", [P, 2, HEADS * EXPERTS])
        inv, some = sb("inv", [P, NT]), sb("some", [P, NT])
        agg, aggT = sb("agg", [P, NT, D + 1]), sb("agg_transposed", [P, DC, NPAD])
        thirds = [0, 8, 16, NT]
        agg_in = [sem(f"agg_in{n}") for n in range(3)]
        XN, XNT = sb("XN1", [P, NT, D]), sb("XNT1", [P, DC, NPAD])
        stats, aggr = sb("stats1", [P, NT, 6]), sb("aggr1", [P, NT, 2])
        var, root, tmp = sb("var1", [P, NT]), sb("root1", [P, NT]), sb("tmp1", [P, NT])
        htab, ha, adst = sb("htab", [P, NT, GW]), sb("ha", [P, NT, HEADS * EXPERTS]), sb("adst", [P, NT, HEADS])
        gidx = [sb(f"gidx{k}", [P, GSTAGE], I32) for k in range(2)]
        grec = [sb(f"grec{k}", [P, GSTAGE, 2]) for k in range(2)]
        upd = [pb(f"upd{k}", [P, 512]) for k in range(2)]
        xnt_ps = pb("xnt_ps", [P, 2, 512])
        h_ps = pb("h_ps", [P, 512])
        w_in, updated, upd_used = (sem(n) for n in ("w_in", "updated", "upd_used"))
        xn_ready = sem("xn_ready1")
        psum_free, xnt_ready, h_ready, tables_ready, out_done = (
            sem(n) for n in ("psum_free", "xnt_ready", "h_ready", "tables_ready", "out_done"))
        staged = sem("gstaged")
        scattered = [sem("gscattered0"), sem("gscattered1")]
        block = ctx.enter_context(nc.Block())
        GROUPS = -(-NT * DC // 4)

        @block.sync
        def _(sp):
            for n in range(3):
                tiles = slice(thirds[n], thirds[n + 1])
                sp.dma_start(agg[:, tiles, :], agg_dram[tiles].rearrange("t p d -> p t d")).then_inc(agg_in[n], 16)
            sp.dma_start(W[:, :, :], a["L0_gnn_weight"].rearrange("(c p) d -> p c d", p=P)).then_inc(w_in, 16)
            sp.dma_start(b[:, :], a["L0_gnn_bias"].partition_broadcast(P)).then_inc(w_in, 16)
            sp.dma_start(wgat[:, :, :], a["L0_ffn_W_gat"].rearrange("(c p) d -> p c d", p=P)).then_inc(w_in, 16)
            for n, name in enumerate(("L0_ffn_att_src", "L0_ffn_att_dst")):
                sp.dma_start(att[:, n, :], a[name].rearrange("h e -> (h e)").partition_broadcast(P)).then_inc(w_in, 16)
            sp.wait_ge(psum_free, 2 * GROUPS)
            sp.dma_start(xnt_dram, XNT[:, :, :]).then_inc(out_done, 16)
            sp.wait_ge(tables_ready, 1)
            sp.dma_start(table_dram.rearrange("(t p) w -> p t w", p=P), htab[:, :, :]).then_inc(out_done, 16)
            sp.dma_start(htab_dram, htab[:, :, :]).then_inc(out_done, 16)
            sp.dma_start(adst_dram, adst[:, :, :]).then_inc(out_done, 16)
            sp.wait_ge(out_done, 64)

        @block.gpsimd
        def _(pool):
            scatter_staged(pool, paused, staged, scattered, GSPLIT[2], GSTAGE, gidx, grec, gpay_dram)

        @block.scalar
        def _(act):
            first = sum(GSPLIT[0:2]) * 2 * GSTAGE
            stage_first(nc.scalar, staged, first, GSTAGE, gidx, grec, grow, gpay)
            copy_transposed(nc.scalar, aggT, xnt_ps, psum_free, xnt_ready)
            act.wait_ge(var_ready, 2)
            nc.scalar.activation(root[:, :], var[:, :], ACT.Sqrt).then_inc(std_ready, 1)
            copy_transposed(nc.scalar, XNT, xnt_ps, psum_free, xnt_ready, first=GROUPS)
            stage_rest(nc.scalar, staged, scattered, GSPLIT[2], first, GSTAGE, gidx, grec, grow, gpay)

        @block.tensor
        def _(pe):
            transpose_nodes(nc.tensor, ident, agg, xnt_ps, psum_free, xnt_ready, loads=(thirds, agg_in))
            pe.wait_ge(w_in, 80)
            for t in range(NT):
                pe.wait_ge(psum_free, t // 2 + 1)
                if t >= 2:
                    pe.wait_ge(upd_used, t - 1)
                for c in range(DC):
                    mm = nc.tensor.matmul(upd[t % 2][:, 0:D], aggT[:, c, t * P:(t + 1) * P], W[:, c, :], start=(c == 0), stop=(c == DC - 1))
                mm.then_inc(updated, 1)
            pe.wait_ge(xn_ready, NT)
            transpose_nodes(nc.tensor, ident, XN, xnt_ps, psum_free, xnt_ready, first=GROUPS)
            pe.wait_ge(psum_free, 2 * GROUPS)
            for t in range(NT):
                for c in range(DC):
                    mm = nc.tensor.matmul(h_ps[:, t * 16:(t + 1) * 16], XNT[:, c, t * P:(t + 1) * P], wgat[:, c, :],
                                          start=(c == 0), stop=(c == DC - 1))
            mm.then_inc(h_ready, 1)

        @block.vector
        def _(dve):
            link = common.link.on(dve)
            for n in range(3):
                dve.wait_ge(agg_in[n], 16)
            link.note(nc.vector.tensor_scalar(some[:, :], agg[:, :, D], 1.0, None, ALU.min))
            link(nc.vector.tensor_scalar(inv[:, :], agg[:, :, D], 1.0, None, ALU.max))
            link(nc.vector.reciprocal(inv[:, :], inv[:, :]))
            dve.wait_ge(w_in, 80)
            for t in range(NT):
                link.note(nc.vector.scalar_tensor_tensor(X[:, t, :], b[:, :], some[:, t:t + 1], X[:, t, :], ALU.mult, ALU.add))
            link.wait()
            for t in range(NT):
                dve.wait_ge(updated, t + 1)
                nc.vector.scalar_tensor_tensor(X[:, t, :], upd[t % 2][:, 0:D], inv[:, t:t + 1], X[:, t, :],
                                               ALU.mult, ALU.add).then_inc(upd_used, 1)
            dve.wait_ge(upd_used, NT)
            normalise(dve, link, X, XN, stats, aggr, var[:, :], root[:, :], tmp[:, :], var_ready, std_ready, 2, xn_ready)
            dve.wait_ge(h_ready, 1)
            hv = h_ps[:, 0:NT * 16].rearrange("p (t k) -> p t k", k=16)
            link.note(nc.vector.tensor_copy(htab[:, :, 0:16], hv))
            for n, to in ((0, htab[:, :, 16:20]), (1, adst[:, :, :])):
                link(nc.vector.tensor_tensor(ha[:, :, :], hv, att[:, n, :].unsqueeze(1).to_broadcast([P, NT, 16]), ALU.mult))
                link(nc.vector.tensor_reduce(to, ha[:, :, :].rearrange("p t (h e) -> p t h e", e=EXPERTS), AX.X, ALU.add))
            dve.sem_inc(tables_ready, 1)


CT = 5
CHUNKS = NT // CT
HALF = CT * P // 2
FE = 2 * D
FC = FE // P
GSET = 7
GSETS = 2
GSTEPS = GKT // (GSET * GSETS)
BIG = 1e30
assert NT % CT == 0 and GSTEPS == EXPERTS * CHUNKS


def attention_maxima(nc, common, a, iota, ident, grecs, gall, tmax, gpay_dram, table_dram, xnt_dram, y_dram):
    paused = common.paused
    with ExitStack() as ctx:
        sb = lambda name, shape, dt=F32: ctx.enter_context(nc.sbuf_tensor(name, shape, dt))
        pb = lambda name, shape, dt=F32: ctx.enter_context(nc.psum_tensor(name, shape, dt))
        sem = lambda name: ctx.enter_context(nc.semaphore(name))
        PER = GSET * GSETS
        M = GSET * HEADS
        XNT = sb("XNT", [P, DC, NPAD])
        W1 = [sb(f"W1_{j}", [P, DC, FE]) for j in range(2)]
        W2 = sb("W2", [P, EXPERTS, FC, D])
        b1 = sb("b1", [P, EXPERTS, FC])
        hid = sb("hid", [P, FC, 2 * HALF])
        ys = sb("ys", [P, CT, D])
        rows = [sb(f"grows{k}", [P, GSET, GW]) for k in range(GSETS)]
        idx = [sb(f"gix{k}", [P, GSET], I32) for k in range(GSETS)]
        hot = [sb(f"ghot{k}", [P, GSET, P], BF16) for k in range(GSETS)]
        pen = [sb(f"pen{k}", [P, GSET, P], BF16) for k in range(GSETS)]
        rest = sb("rest", [P, M])
        split = [sb(f"split{k}", [P, 3, 32], BF16) for k in range(GSETS)]
        splt = [sb(f"splt{k}", [96, P], BF16) for k in range(GSETS)]
        identb = sb("identb", [P, P], BF16)
        pick = sb("pick", [96, M, P], BF16)
        hot_ps = pb("hot_ps", [P, GSET, P], BF16)
        splt_ps = pb("splt_ps", [96, P], BF16)
        val_ps = pb("val_ps", [P, 2, HEADS, P])
        h_ps, y_ps = pb("h_ps2", [P, 2, 512]), pb("y_ps", [P, 2, 512])

        w_in, clear, pick_ready = sem("w_in2"), sem("clear2"), sem("pick_ready")
        idx_ready = sem("gix_ready")
        gathered = [sem(f"ggathered{k}") for k in range(GSETS)]
        kept, hot_ready, hott_ready, pen_ready = (sem(n) for n in ("kept", "ghot_ready", "ghott_ready", "pen_ready"))
        split_ready, splt_ready, splt_copied = sem("split_ready"), sem("splt_ready"), sem("splt_copied")
        val_ready, val_used = sem("val_ready"), sem("val_used")
        h_ready, h_used, y_ready, y_used = (sem(n) for n in ("h_ready2", "h_used", "y_ready", "y_used"))
        stored, up_in = sem("y_stored"), [sem("up_in0"), sem("up_in1")]
        block = ctx.enter_context(nc.Block())

        @block.sync
        def _(sp):
            sp.dma_start(grecs[:, 0:GKT, :], gpay_dram.rearrange("(p k) w -> p k w", p=P)).then_inc(w_in, 16)
            sp.dma_start(XNT[:, :, :], xnt_dram).then_inc(w_in, 16)
            for e in range(EXPERTS):
                sp.dma_start(W2[:, e, :, :], a["L0_ffn_W2"][e].rearrange("(c p) f -> p c f", p=P)).then_inc(w_in, 16)
                sp.dma_start(b1[:, e, :], a["L0_ffn_b1"][e].rearrange("(c p) -> p c", p=P),
                             allow_slow_non_contiguous=True).then_inc(w_in, 16)
            def load_up(i, j):
                sp.dma_start(W1[j][:, :, :], a["L0_ffn_W1"][ds(i % EXPERTS, 1)].rearrange("o (c p) f -> p (o c) f", p=P)
                             ).then_inc(up_in[j], 16)

            for j in range(2):
                load_up(j, j)
            with sp.Fori(0, GSTEPS // 2) as ii:
                for j in range(2):
                    i = ii * 2 + j
                    sp.wait_ge(h_ready, (i + 1) * (2 * FC))
                    load_up(i + 2, j)
                    sp.wait_ge(y_used, (i + 1) * CT + 2)
                    sp.dma_start(y_dram[ds(i, 1)].rearrange("o p t d -> (o p) t d"), ys[:, :, :]).then_inc(stored, 16)
            for j in range(2):
                sp.wait_ge(up_in[j], 16 * (GSTEPS // 2 + 1))
            sp.wait_ge(stored, 16 * GSTEPS + 1)

        @block.gpsimd
        def _(pool):
            nc.gpsimd.memset(pick[:, :, :], 0.0).then_inc(pick_ready, 1)
            for j in range(3):
                pool.wait_ge(pick_ready, j + 1)
                view = pick[32 * j:32 * j + M, :, :]
                nc.gpsimd.affine_select(out=view, in_=view, compare_op=ALU.not_equal, fill=1.0, base=0,
                                        pattern=[[-1, M], [0, P]], channel_multiplier=1).then_inc(pick_ready, 1)
            pool.wait_ge(pick_ready, 4)
            with pool.Fori(0, GSTEPS // 2) as ii:
                for j in range(2):
                    i = ii * 2 + j
                    for k in range(GSETS):
                        pool.wait_ge(idx_ready, i * GSETS + k + 1)
                        pool.sem_inc(paused, 1)
                        pool.wait_ge(split_ready, i * GSETS + k + 1)
                        pool.sem_inc(paused, 1)
                        for u in range(GSET):
                            pool.indirect_dma_start(rows[k][:, u, :], None, table_dram,
                                                    bass.IndirectOffsetOnAxis(ap=idx[k][:, u:u + 1].bitcast(U32), axis=0)
                                                    ).then_inc(gathered[k], 16)

        LOOPED = GSTEPS // 2 - 1

        def run(engine, step):
            with engine.Fori(0, LOOPED) as ii:
                for j in range(2):
                    step(ii * 2 + j, ii, j, False)
            for j in range(2):
                step(LOOPED * 2 + j, LOOPED, j, j == 1)

        @block.scalar
        def _(act):
            def stage(i, k):
                nc.scalar.activation(idx[k][:, :].unsqueeze(2), grecs[:, ds(i * PER + k * GSET, GSET), 0:1].bitcast(I32),
                                     ACT.Copy).then_inc(idx_ready, 1)

            def keep_rows(i, k):
                act.wait_ge(gathered[k], (i + 1) * (16 * GSET))
                act.sem_inc(paused, 1)
                nc.scalar.activation(gall[:, ds(i * PER + k * GSET, GSET), :], rows[k][:, :, :], ACT.Copy).then_inc(kept, 1)
                act.wait_ge(kept, i * GSETS + k + 1)
                stage(i + 1, k)

            def turned(i, k, first=False):
                act.wait_ge(hott_ready, i * GSETS + k + 2)
                if not first:
                    act.wait_ge(val_ready, (i * GSETS + k - 1) * GSET + 1)
                nc.scalar.activation(pen[k][:, :, :], hot_ps[:, :, :], ACT.Copy, bias=-BIG, scale=BIG).then_inc(pen_ready, 1)
                act.wait_ge(splt_ready, i * GSETS + k + 2)
                nc.scalar.activation(splt[k][:, :], splt_ps[:, :], ACT.Copy).then_inc(splt_copied, 1)

            def hidden(m, n):
                half, f = divmod(n, FC)
                act.wait_ge(h_ready, m * (2 * FC) + n + 1)
                if n == 0:
                    act.wait_ge(y_ready, m * CT + 1)
                act.sem_inc(paused, 1)
                nc.scalar.activation(hid[:, f, half * HALF:(half + 1) * HALF], h_ps[:, n % 2, 0:HALF], ACT.Gelu,
                                     bias=b1[:, ds(m % EXPERTS, 1), f:f + 1].rearrange("p a b -> p (a b)")
                                     ).then_inc(h_used, 1)

            def rows_out(i, t):
                act.wait_ge(y_ready, i * CT + t + 2)
                nc.scalar.activation(ys[:, t, :], y_ps[:, t % 2, 0:D], ACT.Copy).then_inc(y_used, 1)

            def step(i, ii, j, final):
                keep_rows(i, 1)
                act.wait_ge(stored, i * 16 + 1)
                for t in range(3):
                    rows_out(i, t)
                turned(i, 1)
                for t in range(3, CT):
                    rows_out(i, t)
                if not final:
                    for n in range(2):
                        hidden(i + 1, n)
                    keep_rows(i + 1, 0)
                    for n in range(2, 5):
                        hidden(i + 1, n)
                    turned(i + 1, 0)
                    for n in range(5, 2 * FC):
                        hidden(i + 1, n)

            act.wait_ge(w_in, 16 * 10)
            act.wait_ge(clear, 2)
            for k in range(GSETS):
                stage(0, k)
            for n in range(2 * FC):
                hidden(0, n)
            keep_rows(0, 0)
            turned(0, 0, first=True)
            run(act, step)

        @block.tensor
        def _(pe):
            pe.wait_ge(w_in, 16 * 10)
            pe.wait_ge(pick_ready, 4)
            pe.sem_inc(h_used, 2)
            pe.sem_inc(y_used, 2)
            pe.wait_ge(clear, 2)

            def transposes(i, k):
                pe.wait_ge(hot_ready, i * GSETS + k + 1)
                pe.wait_ge(pen_ready, i * GSETS + k + 1)
                for u in range(GSET):
                    mm = nc.tensor.transpose(hot_ps[:, u, :], hot[k][:, u, :], identb[:, :])
                mm.then_inc(hott_ready, 1)
                pe.wait_ge(split_ready, (i + 1) * GSETS + k + 1)
                pe.wait_ge(splt_copied, i * GSETS + k + 1)
                nc.tensor.transpose(splt_ps[:, :], split[k][:, :, :].rearrange("p j m -> p (j m)"), identb[:, :]).then_inc(splt_ready, 1)

            def values(i, s):
                k, u = divmod(s, GSET)
                if u == 0:
                    pe.wait_ge(pen_ready, i * GSETS + k + 2)
                    pe.wait_ge(splt_copied, i * GSETS + k + 2)
                pe.wait_ge(val_used, i * PER + s + 1)
                nc.tensor.matmul(val_ps[:, s % 2, :, :], identb[:, :],
                                 pen[k][:, u, :].unsqueeze(1).to_broadcast([P, HEADS, P]), start=True, stop=False)
                for h in range(HEADS):
                    mm = nc.tensor.matmul(val_ps[:, s % 2, h, :], pick[:, u * HEADS + h, :], splt[k][:, :],
                                          start=False, stop=(h == HEADS - 1))
                mm.then_inc(val_ready, 1)

            def first_layer(m, W, n):
                half, f = divmod(n, FC)
                pe.wait_ge(h_used, m * (2 * FC) + n + 1)
                for c in range(DC):
                    mm = nc.tensor.matmul(h_ps[:, n % 2, 0:HALF], W[:, c, f * P:(f + 1) * P],
                                          XNT[:, c, ds((m // EXPERTS) * (2 * HALF) + half * HALF, HALF)],
                                          start=(c == 0), stop=(c == DC - 1))
                mm.then_inc(h_ready, 1)

            def second_layer(i, t):
                if t == 0:
                    pe.wait_ge(h_used, i * (2 * FC) + 2 * FC + 2)
                pe.wait_ge(y_used, i * CT + t + 1)
                for f in range(FC):
                    mm = nc.tensor.matmul(y_ps[:, t % 2, 0:D], hid[:, f, t * P:(t + 1) * P],
                                          W2[:, ds(i % EXPERTS, 1), f, :].rearrange("p o d -> p (o d)"), start=(f == 0), stop=(f == FC - 1))
                mm.then_inc(y_ready, 1)

            def step(i, ii, j, final):
                for s in range(PER):
                    if s == 3:
                        transposes(i, 1)
                    if s == 10 and not final:
                        transposes(i + 1, 0)
                    values(i, s)
                    if s < CT:
                        second_layer(i, s)
                    elif s < CT + 2 * FC and not final:
                        if s == CT:
                            pe.wait_ge(up_in[1 - j], (ii + 1 + j) * 16)
                        first_layer(i + 1, W1[1 - j], s - CT)

            pe.wait_ge(up_in[0], 16)
            for n in range(2 * FC):
                first_layer(0, W1[0], n)
            transposes(0, 0)
            run(pe, step)

        @block.vector
        def _(dve):
            link = common.link.on(dve)
            for one in (hott_ready, val_ready, y_ready, pen_ready, splt_copied, splt_ready, stored):
                dve.sem_inc(one, 1)
            nc.vector.memset(grecs[:, GKT:GKT + PER, :], 0.0).then_inc(clear, 1)
            nc.vector.tensor_copy(identb[:, :], ident[:, :]).then_inc(clear, 1)
            for k in range(GSETS):
                link(nc.vector.memset(split[k][:, :, :], 0.0))
            link(nc.vector.memset(tmax[:, :, GKT:GKT + 2], -BIG))
            dve.sem_inc(val_used, 2)
            dve.sem_inc(split_ready, GSETS)
            dve.wait_ge(w_in, 16 * 10)

            def prepare(i, k, first=False):
                if not first:
                    dve.wait_ge(hott_ready, i * GSETS + k)
                nc.vector.tensor_tensor(hot[k][:, :, :], grecs[:, ds(i * PER + k * GSET, GSET), 1:2].to_broadcast([P, GSET, P]),
                                        iota[:, :].unsqueeze(1).to_broadcast([P, GSET, P]), ALU.is_equal).then_inc(hot_ready, 1)
                dve.wait_ge(gathered[k], (i + 1) * (16 * GSET))
                if not first:
                    dve.wait_ge(splt_ready, i * GSETS + k)
                value = rows[k][:, :, 16:20]
                part = lambda q: split[k][:, q, 0:M].rearrange("p (u h) -> p u h", h=HEADS)
                left = rest[:, :].rearrange("p (u h) -> p u h", h=HEADS)
                link(nc.vector.tensor_copy(part(0), value))
                link(nc.vector.tensor_tensor(left, value, part(0), ALU.subtract))
                link(nc.vector.tensor_copy(part(1), left))
                link(nc.vector.tensor_tensor(left, left, part(1), ALU.subtract))
                nc.vector.tensor_copy(part(2), left).then_inc(split_ready, 1)

            def step(i, ii, j, final):
                if j == 0:
                    link.enter(ii, 2 * 4 * GSETS) if not isinstance(ii, int) else None
                for s in range(PER):
                    if s == 1:
                        prepare(i, 1)
                    if s == 8 and not final:
                        prepare(i + 1, 0)
                    dve.wait_ge(val_ready, i * PER + s + 2)
                    nc.vector.tensor_reduce(tmax[:, :, ds(i * PER + s, 1)].rearrange("p h o -> p (h o)"),
                                            val_ps[:, s % 2, :, :], AX.X, ALU.max).then_inc(val_used, 1)
                if j == 1 and not isinstance(ii, int):
                    link.leave(LOOPED)

            prepare(0, 0, first=True)
            run(dve, step)


def block_ends(nc, dve, link, glast, to, values, step):
    with dve.Fori(0, NT // step) as i:
        link.enter(i, step)
        _, ends = nc.values_load_multi_w_load_instructions(glast[0:1, ds(i * step, step)], engines=[dve.engine],
                                                           min_val=0, max_val=GKT)
        for u in range(step):
            link.note(nc.vector.tensor_copy(to[:, ds(i * step + u, 1), :].rearrange("p o c -> p c o"),
                                            values[:, :, ds(ends[u], 1)]))
        link.leave(NT // step)
    link.wait()


def second_update(nc, common, a, X, iota, ident, gslot, gkeep, glast, grecs, gall, tmax, adst_dram, htab_dram, y_dram, xn_dram):
    paused, var_ready, std_ready = common.paused, common.var_ready, common.std_ready
    with ExitStack() as ctx:
        sb = lambda name, shape, dt=F32: ctx.enter_context(nc.sbuf_tensor(name, shape, dt))
        pb = lambda name, shape, dt=F32: ctx.enter_context(nc.psum_tensor(name, shape, dt))
        sem = lambda name: ctx.enter_context(nc.semaphore(name))
        H, C16 = HEADS, HEADS * EXPERTS
        PER = GSET * GSETS
        adst, htab = sb("adst2", [P, NT, H]), sb("htab2", [P, NT, GW])
        reset = sb("reset", [P, GKT])
        own = sb("own", [P, NT, 2 * H])
        rest, own3 = sb("rest2", [P, NT, 2 * H]), sb("own3", [P, NT, 3, 2 * H], BF16)
        selfw = sb("selfw", [P, NT, H])
        identb = sb("identb2", [P, P], BF16)
        hotb = [sb(f"hotb{k}", [P, GSET, P], BF16) for k in range(GSETS)]
        hott = [sb(f"hott{k}", [P, GSET, P], BF16) for k in range(GSETS)]
        look = sb("look", [P, GKT, 2 * H])
        weight = sb("weight", [P, GKT, H])
        hotf = [sb(f"hotf{k}", [P, GSET, P]) for k in range(GSETS)]
        sums = sb("sums", [P, GW, GKT + 2])
        acc = sb("acc", [P, NT, GW])
        sq, mean, var, root, tmp = (sb("sq", [P, NT, C16]), *(sb(f"{n}3", [P, NT]) for n in ("mean", "var", "root", "tmp")))
        bg = sb("bg", [P, 3, C16])
        den = sb("den", [P, NT, H])
        score, gate, rank, cmp = (sb(n, [P, NT, EXPERTS]) for n in ("score", "gate", "rank2", "cmp"))
        gatet, b2 = sb("gatet", [EXPERTS, NPAD]), sb("b2", [EXPERTS, D])
        yt = [sb(f"yt{k}", [P, EXPERTS, D]) for k in range(3)]
        XN = sb("XN2", [P, NT, D])
        stats, aggr = sb("stats2", [P, NT, 6]), sb("aggr2", [P, NT, 2])
        hot_ps = pb("hot_ps2", [P, 2, 1024], BF16)
        look_ps = pb("look_ps", [P, 2, 512])
        gt_ps, b_ps = pb("gt_ps", [EXPERTS, 2, 512]), pb("b_ps", [P, 2, 512])

        w_in = sem("w_in3")
        hot_ready, hott_ready, hott_copied, look_ready, look_used = (
            sem(n) for n in ("hotb_ready", "hott_ready2", "hott_copied", "look_ready", "look_used"))
        hotf_ready, sum_ready, sum_used, own_ready, arg_ready, exp_done = (
            sem(n) for n in ("hotf_ready", "sum_ready", "sum_used", "own_ready", "arg_ready", "exp_done"))
        xn_ready, xn_out = sem("xn_ready3"), sem("xn_out3")
        gt_ready, gt_copied, b_ready, x_added = (
            sem(n) for n in ("gt_ready", "gt_copied", "b_ready", "x_added"))
        y_in = [sem(f"y_in{k}") for k in range(3)]
        msg_ready = sem("msg_ready")
        block = ctx.enter_context(nc.Block())
        GG = -(-NT // 4)

        @block.sync
        def _(sp):
            sp.dma_start(adst[:, :, :], adst_dram).then_inc(w_in, 16)
            sp.dma_start(htab[:, :, :], htab_dram).then_inc(w_in, 16)
            for n, name in enumerate(("L0_ffn_b_gat", "L0_ffn_ln_gamma", "L0_ffn_ln_beta")):
                sp.dma_start(bg[:, n, :], a[name].partition_broadcast(P)).then_inc(w_in, 16)
            sp.dma_start(b2[:, :], a["L0_ffn_b2"]).then_inc(w_in, 16)
            for t in range(NT):
                if t >= 3:
                    sp.wait_ge(x_added, t - 2)
                chunk, tt = divmod(t, CT)
                sp.dma_start(yt[t % 3][:, :, :], y_dram[chunk * EXPERTS:(chunk + 1) * EXPERTS, :, tt, :]
                             .rearrange("e p d -> p e d")).then_inc(y_in[t % 3], 16)
            sp.wait_ge(xn_ready, NT)
            sp.dma_start(xn_dram.rearrange("(t p) d -> p t d", p=P), XN[:, :, :]).then_inc(xn_out, 16)
            sp.wait_ge(xn_out, 16)

        @block.scalar
        def _(act):
            act.wait_ge(own_ready, 1)
            with act.Fori(0, GSTEPS) as i:
                for k in range(GSETS):
                    act.wait_ge(hott_ready, i * GSETS + k + 2)
                    act.wait_ge(look_ready, i * GSETS + 1)
                    nc.scalar.activation(hott[k][:, :, :].rearrange("p u d -> p (u d)"), hot_ps[:, k, 0:GSET * P],
                                         ACT.Copy).then_inc(hott_copied, 1)
            act.wait_ge(arg_ready, 1)
            nc.scalar.activation(weight[:, :, :], weight[:, :, :], ACT.Exp).then_inc(exp_done, 1)
            nc.scalar.activation(selfw[:, :, :], selfw[:, :, :], ACT.Exp).then_inc(exp_done, 1)
            with act.Fori(0, GSTEPS) as i:
                for k in range(GSETS):
                    act.wait_ge(sum_ready, i * GSETS + k + 2)
                    act.sem_inc(paused, 1)
                    nc.scalar.activation(sums[:, :, ds(i * PER + k * GSET, GSET)].rearrange("p c u -> p u c"),
                                         look_ps[:, k, 0:GSET * GW].rearrange("p (u c) -> p u c", c=GW), ACT.Copy).then_inc(sum_used, 1)
            act.wait_ge(var_ready, 3)
            nc.scalar.activation(root[:, :], var[:, :], ACT.Sqrt).then_inc(std_ready, 1)
            act.wait_ge(arg_ready, 2)
            nc.scalar.activation(gate[:, :, :], gate[:, :, :], ACT.Exp).then_inc(exp_done, 1)
            for g in range(GG):
                act.wait_ge(gt_ready, g + 1)
                n = min(4, NT - 4 * g) * P
                nc.scalar.activation(gatet[:, g * 4 * P:g * 4 * P + n], gt_ps[:, g % 2, 0:n], ACT.Copy).then_inc(gt_copied, 1)
            act.wait_ge(var_ready, 4)
            nc.scalar.activation(root[:, :], var[:, :], ACT.Sqrt).then_inc(std_ready, 1)

        @block.tensor
        def _(pe):
            pe.wait_ge(own_ready, 1)
            with pe.Fori(0, GSTEPS) as i:
                _, blocks = nc.values_load_multi_w_load_instructions(gslot[0:1, ds(i * PER, PER)], engines=[pe.engine],
                                                                     min_val=0, max_val=NT - 1)
                for k in range(GSETS):
                    pe.wait_ge(hot_ready, i * GSETS + k + 1)
                    pe.wait_ge(hott_copied, i * GSETS + 1)
                    for u in range(GSET):
                        mm = nc.tensor.transpose(hot_ps[:, k, u * P:(u + 1) * P], hotb[k][:, u, :], identb[:, :])
                    mm.then_inc(hott_ready, 1)
                for k in range(GSETS):
                    pe.wait_ge(hott_copied, i * GSETS + k + 2)
                    pe.wait_ge(look_used, i * GSETS + 1)
                    for u in range(GSET):
                        mm = nc.tensor.matmul(look_ps[:, k, u * 24:(u + 1) * 24], hott[k][:, u, :],
                                              own3[:, ds(blocks[k * GSET + u], 1), :, :].rearrange("p o j c -> p (o j c)"),
                                              start=True, stop=True)
                    mm.then_inc(look_ready, 1)
            pe.wait_ge(msg_ready, 1)
            with pe.Fori(0, GSTEPS) as i:
                for k in range(GSETS):
                    pe.wait_ge(hotf_ready, i * GSETS + k + 1)
                    pe.wait_ge(sum_used, i * GSETS + 1)
                    for u in range(GSET):
                        mm = nc.tensor.matmul(look_ps[:, k, u * GW:(u + 1) * GW], hotf[k][:, u, :],
                                              gall[:, ds(i * PER + k * GSET + u, 1), :].rearrange("p o c -> p (o c)"),
                                              start=True, stop=True)
                    mm.then_inc(sum_ready, 1)
            pe.wait_ge(arg_ready, 3)
            for g in range(GG):
                if g >= 2:
                    pe.wait_ge(gt_copied, g - 1)
                for t in range(4 * g, min(4 * g + 4, NT)):
                    mm = nc.tensor.transpose(gt_ps[:, g % 2, (t % 4) * P:(t % 4 + 1) * P], gate[:, t, :], ident[:, :])
                mm.then_inc(gt_ready, 1)
            pe.wait_ge(gt_copied, GG)
            for t in range(NT):
                if t >= 2:
                    pe.wait_ge(x_added, t - 1)
                nc.tensor.matmul(b_ps[:, t % 2, 0:D], gatet[:, t * P:(t + 1) * P], b2[:, :], start=True, stop=True).then_inc(b_ready, 1)

        @block.vector
        def _(dve):
            link = common.link.on(dve)
            dve.sem_inc(hott_ready, 1)
            dve.sem_inc(look_ready, 1)
            dve.sem_inc(hott_copied, 1)
            dve.sem_inc(look_used, 1)
            dve.sem_inc(sum_ready, 1)
            dve.sem_inc(sum_used, 1)
            V = nc.vector

            def leaky(x):
                link(V.scalar_tensor_tensor(x, x, 0.2, x, ALU.mult, ALU.max))

            link.note(V.tensor_copy(identb[:, :], ident[:, :]))
            link.note(V.memset(sums[:, :, GKT:GKT + 2], 0.0))
            link(V.tensor_scalar(reset[:, :], gkeep[:, :], -1.0, BIG, ALU.add, ALU.mult))
            for h in range(H):
                link.note(V.tensor_tensor_scan(tmax[:, h, 0:GKT], reset[:, :], tmax[:, h, 0:GKT], -BIG, ALU.add, ALU.max))
            link.wait()
            block_ends(nc, dve, link, glast, den, tmax, 5)
            dve.wait_ge(w_in, 96)
            asrc, hown = htab[:, :, 16:20], htab[:, :, 0:16]
            link(V.tensor_tensor(den[:, :, :], den[:, :, :], asrc, ALU.max))
            link(V.tensor_tensor(own[:, :, H:2 * H], den[:, :, :], adst[:, :, :], ALU.add))
            leaky(own[:, :, H:2 * H])
            link(V.tensor_copy(own[:, :, 0:H], adst[:, :, :]))
            link(V.tensor_tensor(selfw[:, :, :], asrc, adst[:, :, :], ALU.add))
            leaky(selfw[:, :, :])
            link(V.tensor_tensor(selfw[:, :, :], selfw[:, :, :], own[:, :, H:2 * H], ALU.subtract))
            link(V.tensor_copy(own3[:, :, 0, :], own[:, :, :]))
            link(V.tensor_tensor(rest[:, :, :], own[:, :, :], own3[:, :, 0, :], ALU.subtract))
            link(V.tensor_copy(own3[:, :, 1, :], rest[:, :, :]))
            link(V.tensor_tensor(rest[:, :, :], rest[:, :, :], own3[:, :, 1, :], ALU.subtract))
            link(V.tensor_copy(own3[:, :, 2, :], rest[:, :, :]))
            dve.sem_inc(own_ready, 1)
            with dve.Fori(0, GSTEPS) as i:
                for k in range(GSETS):
                    dve.wait_ge(hott_ready, i * GSETS + 1)
                    V.tensor_tensor(hotb[k][:, :, :], grecs[:, ds(i * PER + k * GSET, GSET), 1:2].to_broadcast([P, GSET, P]),
                                    iota[:, :].unsqueeze(1).to_broadcast([P, GSET, P]), ALU.is_equal).then_inc(hot_ready, 1)
                for k in range(GSETS):
                    dve.wait_ge(look_ready, i * GSETS + k + 2)
                    V.tensor_reduce(look[:, ds(i * PER + k * GSET, GSET), :],
                                    look_ps[:, k, 0:GSET * 24].rearrange("p (u j c) -> p u c j", j=3, c=2 * H),
                                    AX.X, ALU.add).then_inc(look_used, 1)
            dve.wait_ge(look_used, GSTEPS * GSETS + 1)
            link(V.tensor_tensor(weight[:, :, :], gall[:, :, 16:20], look[:, :, 0:H], ALU.add))
            leaky(weight[:, :, :])
            link(V.tensor_tensor(weight[:, :, :], weight[:, :, :], look[:, :, H:2 * H], ALU.subtract))
            link(V.tensor_scalar(weight[:, :, :], weight[:, :, :], 0.0, None, ALU.min))
            dve.sem_inc(arg_ready, 1)
            dve.wait_ge(exp_done, 2)
            g4 = gall[:, :, 0:16].rearrange("p k (h e) -> p k h e", e=EXPERTS)
            for h in range(H):
                link.note(V.tensor_tensor(gall[:, :, h * EXPERTS:(h + 1) * EXPERTS], gall[:, :, h * EXPERTS:(h + 1) * EXPERTS],
                                          weight[:, :, h:h + 1].to_broadcast([P, GKT, EXPERTS]), ALU.mult))
            link.note(V.tensor_copy(gall[:, :, 16:20], weight[:, :, :]))
            link.wait()
            dve.sem_inc(msg_ready, 1)
            with dve.Fori(0, GSTEPS) as i:
                for k in range(GSETS):
                    dve.wait_ge(sum_ready, i * GSETS + 1)
                    V.tensor_tensor(hotf[k][:, :, :], grecs[:, ds(i * PER + k * GSET, GSET), 1:2].to_broadcast([P, GSET, P]),
                                    iota[:, :].unsqueeze(1).to_broadcast([P, GSET, P]), ALU.is_equal).then_inc(hotf_ready, 1)
            dve.wait_ge(sum_used, GSTEPS * GSETS + 1)
            for c in range(GW):
                link.note(V.tensor_tensor_scan(sums[:, c, 0:GKT], gkeep[:, :], sums[:, c, 0:GKT], 0.0, ALU.mult, ALU.add))
            link.wait()
            block_ends(nc, dve, link, glast, acc, sums, 5)
            a3 = lambda x: x.rearrange("p t (h e) -> p t h e", e=EXPERTS)
            for h in range(H):
                part = slice(h * EXPERTS, (h + 1) * EXPERTS)
                link.note(V.tensor_tensor(sq[:, :, part], hown[:, :, part], selfw[:, :, h:h + 1].to_broadcast([P, NT, EXPERTS]), ALU.mult))
            link.wait()
            link(V.tensor_tensor(acc[:, :, 0:16], acc[:, :, 0:16], sq[:, :, :], ALU.add))
            link(V.tensor_tensor(den[:, :, :], acc[:, :, 16:20], selfw[:, :, :], ALU.add))
            link(V.tensor_scalar(den[:, :, :], den[:, :, :], 1e-16, None, ALU.add))
            link(V.reciprocal(den[:, :, :], den[:, :, :]))
            for h in range(H):
                part = slice(h * EXPERTS, (h + 1) * EXPERTS)
                link.note(V.tensor_tensor(acc[:, :, part], acc[:, :, part], den[:, :, h:h + 1].to_broadcast([P, NT, EXPERTS]), ALU.mult))
            link.wait()
            agg = acc[:, :, 0:16]
            spread = lambda n: bg[:, n, :].unsqueeze(1).to_broadcast([P, NT, C16])
            over = lambda x: x.unsqueeze(2).to_broadcast([P, NT, C16])
            link(V.tensor_tensor(agg, agg, spread(0), ALU.add))
            link(V.tensor_reduce(mean[:, :], agg, AX.X, ALU.add))
            link(V.tensor_scalar(mean[:, :], mean[:, :], 1.0 / C16, None, ALU.mult))
            link(V.tensor_tensor(agg, agg, over(mean[:, :]), ALU.subtract))
            link(V.tensor_tensor(sq[:, :, :], agg, agg, ALU.mult))
            link(V.tensor_reduce(var[:, :], sq[:, :, :], AX.X, ALU.add))
            link(V.tensor_scalar(var[:, :], var[:, :], 1.0 / C16, None, ALU.mult))
            inverse_root(dve, link, var[:, :], root[:, :], tmp[:, :], var_ready, std_ready, 3)
            link(V.tensor_tensor(agg, agg, over(root[:, :]), ALU.mult))
            link(V.tensor_tensor(agg, agg, spread(1), ALU.mult))
            link(V.tensor_tensor(agg, agg, spread(2), ALU.add))
            link(V.tensor_reduce(score[:, :, :], agg.rearrange("p t (h e) -> p t e h", e=EXPERTS), AX.X, ALU.add))
            link(V.tensor_scalar(score[:, :, :], score[:, :, :], 1.0 / H, None, ALU.mult))
            link(V.memset(rank[:, :, :], 0.0))
            for e in range(EXPERTS):
                for o in range(EXPERTS):
                    if o != e:
                        link(V.tensor_tensor(cmp[:, :, e], score[:, :, o], score[:, :, e], ALU.is_ge if o < e else ALU.is_gt))
                        link(V.tensor_tensor(rank[:, :, e], rank[:, :, e], cmp[:, :, e], ALU.add))
            link(V.tensor_scalar(rank[:, :, :], rank[:, :, :], 1.5, None, ALU.is_lt))
            link(V.tensor_reduce(tmp[:, :], score[:, :, :], AX.X, ALU.max))
            link(V.tensor_tensor(gate[:, :, :], score[:, :, :], tmp[:, :].unsqueeze(2).to_broadcast([P, NT, EXPERTS]), ALU.subtract))
            dve.sem_inc(arg_ready, 1)
            dve.wait_ge(exp_done, 3)
            link(V.tensor_tensor(gate[:, :, :], gate[:, :, :], rank[:, :, :], ALU.mult))
            link(V.tensor_reduce(tmp[:, :], gate[:, :, :], AX.X, ALU.add))
            link(V.reciprocal(tmp[:, :], tmp[:, :]))
            link(V.tensor_tensor(gate[:, :, :], gate[:, :, :], tmp[:, :].unsqueeze(2).to_broadcast([P, NT, EXPERTS]), ALU.mult))
            dve.sem_inc(arg_ready, 1)
            for t in range(NT):
                dve.wait_ge(y_in[t % 3], 16 * (t // 3 + 1))
                for e in range(EXPERTS):
                    link(V.scalar_tensor_tensor(X[:, t, :], yt[t % 3][:, e, :], gate[:, t, e:e + 1], X[:, t, :], ALU.mult, ALU.add))
                dve.wait_ge(b_ready, t + 1)
                V.tensor_tensor(X[:, t, :], X[:, t, :], b_ps[:, t % 2, 0:D], ALU.add).then_inc(x_added, 1)
            dve.wait_ge(x_added, NT)
            normalise(dve, link, X, XN, stats, aggr, var[:, :], root[:, :], tmp[:, :], var_ready, std_ready, 4, xn_ready)


def sum_relations(nc, common, iota, fine, coefs, table, z_dram):
    paused = common.paused
    with ExitStack() as ctx:
        sb = lambda name, shape, dt=F32: ctx.enter_context(nc.sbuf_tensor(name, shape, dt))
        pb = lambda name, shape, dt=F32: ctx.enter_context(nc.psum_tensor(name, shape, dt))
        sem = lambda name: ctx.enter_context(nc.semaphore(name))
        PER = SET * SETS
        STEPS = KT // PER
        BW = BASES * WIN
        rows = [sb(f"rrows{k}", [P, SET, D]) for k in range(SETS)]
        idx = [sb(f"ridx{k}", [P, SET], I32) for k in range(SETS)]
        hot = [sb(f"rhot{k}", [P, SET, WIN]) for k in range(SETS)]
        coef = [sb(f"coef{k}", [P, SET, BASES, WIN]) for k in range(SETS)]
        acc = [sb(f"acc{n}", [P, DC * BW]) for n in range(PER)]
        zero = sb("zero", [P, DC * BW])
        part = pb("part5", [P, PER, 512])
        idx_ready, coef_ready, added = (
            sem(n) for n in ("ridx_ready", "coef_ready5", "added5"))
        gathered, summed, flushed = common.gathered, common.summed, common.flushed
        DONE = KA // PER
        GATHERED, SUMMED, FLUSHED = DONE * (16 * SET), DONE + 1, DONE * 16 + 1
        zero_ready, zero_out = sem("zero_ready"), sem("zero_out")
        block = ctx.enter_context(nc.Block())

        @block.sync
        def _(sp):
            sp.wait_ge(zero_ready, 1)
            for w in range(NW, NT * P // WIN):
                sp.dma_start(z_dram[w], zero[:, :]).then_inc(zero_out, 16)
            with sp.Fori(0, STEPS) as i:
                _, wins = nc.values_load_multi_w_load_instructions(fine.group[0:1, ds(i * PER, PER)], engines=[sp.engine],
                                                                   min_val=0, max_val=NW - 1)
                _, lasts = nc.values_load_multi_w_load_instructions(fine.last[0:1, ds(i * PER, PER)], engines=[sp.engine],
                                                                    min_val=0, max_val=1)
                for n in range(PER):
                    sp.wait_ge(added, (i + 1) * PER + n + 1)
                    sp.dma_start(z_dram[ds(wins[n], 1)].rearrange("o p w -> (o p) w"), acc[n][:, :],
                                 cond=lasts[n] > 0).then_inc(flushed[n], 16)
            sp.wait_ge(zero_out, 16 * (NT * P // WIN - NW))
            for n in range(PER):
                sp.wait_ge(flushed[n], FLUSHED + 16 * STEPS)

        @block.scalar
        def _(act):
            with act.Fori(0, STEPS) as i:
                for k in range(SETS):
                    act.wait_ge(summed[k], i + SUMMED)
                    nc.scalar.activation(idx[k][:, :], fine.source[:, ds(i * PER + k * SET, SET)], ACT.Copy).then_inc(idx_ready, 1)

        @block.gpsimd
        def _(pool):
            with pool.Fori(0, STEPS) as i:
                for k in range(SETS):
                    pool.wait_ge(idx_ready, i * SETS + k + 1)
                    pool.sem_inc(paused, 1)
                    for u in range(SET):
                        pool.indirect_dma_start(rows[k][:, u, :], None, table,
                                                bass.IndirectOffsetOnAxis(ap=idx[k][:, u:u + 1].bitcast(U32), axis=0)
                                                ).then_inc(gathered[k], 16)

        @block.tensor
        def _(pe):
            with pe.Fori(0, STEPS) as i:
                for k in range(SETS):
                    pe.wait_ge(coef_ready, i * SETS + k + 1)
                    pe.wait_ge(added, i * PER + (k + 1) * SET)
                    pe.wait_ge(gathered[k], i * (16 * SET) + (GATHERED + 16 * SET))
                    for u in range(SET):
                        for c in range(DC):
                            mm = nc.tensor.matmul(part[:, k * SET + u, c * BW:(c + 1) * BW], rows[k][:, u, c * P:(c + 1) * P],
                                                  coef[k][:, u, :, :].rearrange("p b w -> p (b w)"), start=True, stop=True)
                    mm.then_inc(summed[k], 1)

        @block.vector
        def _(dve):
            link = common.link.on(dve)
            V = nc.vector
            V.memset(zero[:, :], 0.0).then_inc(zero_ready, 1)
            link(V.memset(acc[PER - 1][:, :], 0.0))

            def places(i, k):
                link.note(V.tensor_tensor(hot[k][:, :, :], fine.target[:, ds(i * PER + k * SET, SET)].unsqueeze(2).to_broadcast([P, SET, WIN]),
                                          iota[:, 0:WIN].unsqueeze(1).to_broadcast([P, SET, WIN]), ALU.is_equal))

            def weights(i, k):
                link.wait()
                V.tensor_tensor(coef[k][:, :, :, :], hot[k][:, :, :].unsqueeze(2).to_broadcast([P, SET, BASES, WIN]),
                                coefs[:, ds(i * PER + k * SET, SET), :].unsqueeze(3).to_broadcast([P, SET, BASES, WIN]),
                                ALU.mult).then_inc(coef_ready, 1)

            def step(i, more):
                for k in range(SETS):
                    dve.wait_ge(summed[k], i + (SUMMED + 1))
                    if more:
                        places(i + 1, k)
                    for u in range(SET):
                        n = k * SET + u
                        dve.wait_ge(flushed[n], i * 16 + FLUSHED)
                        dve.wait_ge(added, i * PER + n + PER)
                        V.scalar_tensor_tensor(acc[n][:, :], acc[(n - 1) % PER][:, :], fine.keep[:, ds(i * PER + n, 1)],
                                               part[:, n, :], ALU.mult, ALU.add).then_inc(added, 1)
                        if more and u == 0:
                            weights(i + 1, k)

            dve.sem_inc(added, PER)
            for k in range(SETS):
                places(0, k)
                weights(0, k)
            with dve.Fori(0, STEPS - 1) as i:
                link.enter(i, SETS)
                step(i, True)
                link.leave(STEPS - 1)
            step(STEPS - 1, False)


def third_update(nc, common, a, X, iota, ident, ones, z_dram, out):
    var_ready, std_ready = common.var_ready, common.std_ready
    with ExitStack() as ctx:
        sb = lambda name, shape, dt=F32: ctx.enter_context(nc.sbuf_tensor(name, shape, dt))
        pb = lambda name, shape, dt=F32: ctx.enter_context(nc.psum_tensor(name, shape, dt))
        sem = lambda name: ctx.enter_context(nc.semaphore(name))
        BW, WT = BASES * WIN, P // WIN
        E8, K2 = 8, 2
        CAPACITY = float(-(-N * 5 // (4 * E8)))
        bases = sb("bases", [P, BASES, DC, D])
        z = [sb(f"z{k}", [P, WT, DC * BW]) for k in range(2)]
        zn = [sb(f"zn{k}", [P, DC * BASES, WT, WIN]) for k in range(2)]
        XN, XNT = sb("XN6", [P, NT, D]), sb("XNT6", [P, DC, NPAD])
        stats, aggr = sb("stats6", [P, NT, 6]), sb("aggr6", [P, NT, 2])
        var, root, tmp = sb("var6", [P, NT]), sb("root6", [P, NT]), sb("tmp6", [P, NT])
        wr, br = sb("wr", [P, DC, E8]), sb("br", [P, E8])
        mean = sb("mean6", [P, DC, P])
        lg, r1, r2, top, sm = (sb(n, [P, E8]) for n in ("lg", "r1", "r2", "top", "sm"))
        larger, equal, earlier = (sb(n, [P, E8, E8]) for n in ("larger", "equal", "earlier"))
        which = sb("which", [P, K2], I32)
        wgt = sb("wgt", [P, K2])
        W1 = [sb(f"V1_{k}", [P, DC, FE]) for k in range(K2)]
        W2 = [sb(f"V2_{k}", [P, FC, D]) for k in range(K2)]
        b1, b2 = sb("b1_6", [P, K2, FC]), sb("b2_6", [P, K2, D])
        gam, bet, bias = sb("gam", [P, D]), sb("bet", [P, D]), sb("bias6", [P, D])
        hid = [sb(f"hid6_{k}", [P, FC, 2 * HALF]) for k in range(1)]
        z_ps = pb("z_ps", [P, 2, 512])
        xnt_ps = pb("xnt_ps6", [P, 2, 512])
        h_ps, y_ps = pb("h_ps6", [P, 2, 512]), pb("y_ps6", [P, 2, 512])
        w_in, e_in = sem("w_in6"), sem("experts_in")
        z_in = [sem("z_in0"), sem("z_in1")]
        z_ready, z_added, z_turned = sem("z_ready"), sem("z_added"), sem("z_turned")
        xn_ready = sem("xn_ready6")
        psum_free, xnt_ready = sem("psum_free6"), sem("xnt_ready6")
        mean_ready, mean_copied, logits_ready, arg_ready, exp_done, picked = (
            sem(n) for n in ("mean_ready", "mean_copied", "logits_ready", "arg_ready6", "exp_done6", "picked"))
        h_ready, h_used, y_ready, y_used = (sem(n) for n in ("h_ready6", "h_used6", "y_ready6", "y_used6"))
        out_ready, out_done = sem("out_ready"), sem("out_done6")
        block = ctx.enter_context(nc.Block())
        GROUPS = -(-NT * DC // 4)

        @block.sync
        def _(sp):
            sp.dma_start(bases[:, :, :, :], a["L1_gnn_bases"].rearrange("b (c p) d -> p b c d", p=P)).then_inc(w_in, 16)
            sp.dma_start(wr[:, :, :], a["L1_ffn_Wr"].rearrange("(c p) e -> p c e", p=P)).then_inc(w_in, 16)
            sp.dma_start(br[:, :], a["L1_ffn_br"].partition_broadcast(P)).then_inc(w_in, 16)
            sp.dma_start(gam[:, :], a["L1_ffn_gamma"].partition_broadcast(P)).then_inc(w_in, 16)
            sp.dma_start(bet[:, :], a["L1_ffn_beta"].partition_broadcast(P)).then_inc(w_in, 16)
            for t in range(NT):
                if t >= 2:
                    sp.wait_ge(z_turned, t - 1)
                sp.dma_start(z[t % 2][:, :, :], z_dram[t * WT:(t + 1) * WT].rearrange("w p x -> p w x")).then_inc(z_in[t % 2], 16)
            sp.wait_ge(picked, 1)
            _, chosen = nc.values_load_multi_w_load_instructions(which[0:1, :], engines=[sp.engine],
                                                                 min_val=0, max_val=E8 - 1, bass_reorder=False)
            for k in range(K2):
                e = ds(chosen[k], 1)
                sp.dma_start(W1[k][:, :, :], a["L1_ffn_W1"][e].rearrange("o (c p) f -> p (o c) f", p=P)).then_inc(e_in, 16)
                sp.dma_start(W2[k][:, :, :], a["L1_ffn_W2"][e].rearrange("o (c p) f -> p (o c) f", p=P)).then_inc(e_in, 16)
                sp.dma_start(b1[:, k, :], a["L1_ffn_b1"][e].rearrange("o (c p) -> p (o c)", p=P),
                             allow_slow_non_contiguous=True).then_inc(e_in, 16)
                sp.dma_start(b2[:, k, :], a["L1_ffn_b2"][e].rearrange("o d -> (o d)").partition_broadcast(P)).then_inc(e_in, 16)
            sp.wait_ge(out_ready, NT)
            sp.dma_start(out[0:NFULL * P, :].rearrange("(t p) d -> p t d", p=P), XN[:, 0:NFULL, :]).then_inc(out_done, 16)
            sp.dma_start(out[NFULL * P:N, :], XN[0:NTAIL, NFULL, :]).then_inc(out_done, 16)
            sp.wait_ge(out_done, 32)

        @block.scalar
        def _(act):
            for t in range(NT):
                act.wait_ge(z_in[t % 2], 16 * (t // 2 + 1))
                if t >= 2:
                    act.wait_ge(z_ready, t - 1)
                nc.scalar.activation(zn[t % 2][:, :, :, :], z[t % 2][:, :, :].rearrange("p w (k d) -> p k w d", d=WIN),
                                     ACT.Copy).then_inc(z_turned, 1)
            act.wait_ge(var_ready, 5)
            nc.scalar.activation(root[:, :], var[:, :], ACT.Sqrt).then_inc(std_ready, 1)
            act.wait_ge(mean_ready, 1)
            for c in range(DC):
                nc.scalar.activation(mean[:, c, :], z_ps[:, c, 0:1].to_broadcast([P, P]), ACT.Copy, scale=1.0 / N).then_inc(mean_copied, 1)
            for n in range(3):
                act.wait_ge(arg_ready, n + 1)
                x = sm[:, 0:1] if n == 2 else sm[:, :]
                nc.scalar.activation(x, x, ACT.Exp).then_inc(exp_done, 1)
            copy_transposed(nc.scalar, XNT, xnt_ps, psum_free, xnt_ready)
            act.wait_ge(e_in, 16 * 4 * K2)
            for unit in range(CHUNKS * K2):
                for n in range(2 * FC):
                    half, f = divmod(n, FC)
                    act.wait_ge(h_ready, unit * 2 * FC + n + 1)
                    if n == 0 and unit:
                        act.wait_ge(y_ready, unit * CT)
                    nc.scalar.activation(hid[0][:, f, half * HALF:(half + 1) * HALF], h_ps[:, n % 2, 0:HALF], ACT.Gelu,
                                         bias=b1[:, unit % K2, f:f + 1]).then_inc(h_used, 1)
            act.wait_ge(var_ready, 6)
            nc.scalar.activation(root[:, :], var[:, :], ACT.Sqrt).then_inc(std_ready, 1)

        @block.tensor
        def _(pe):
            pe.wait_ge(w_in, 16 * 5)
            for t in range(NT):
                pe.wait_ge(z_turned, t + 1)
                if t >= 2:
                    pe.wait_ge(z_added, t - 1)
                for n, (c, b) in enumerate((c, b) for c in range(DC) for b in range(BASES)):
                    mm = nc.tensor.matmul(z_ps[:, t % 2, 0:D], zn[t % 2][:, c * BASES + b, :, :].rearrange("p w d -> p (w d)"), bases[:, b, c, :],
                                          start=(n == 0), stop=(n == DC * BASES - 1))
                mm.then_inc(z_ready, 1)
            pe.wait_ge(xn_ready, NT)
            for c in range(DC):
                for t in range(NT):
                    n = P if t < NFULL else NTAIL
                    mm = nc.tensor.matmul(z_ps[:, c, 0:1], XN[0:n, t, c * P:(c + 1) * P], ones[0:n, 0:1],
                                          start=(t == 0), stop=(t == NT - 1))
            mm.then_inc(mean_ready, 1)
            pe.wait_ge(mean_copied, DC)
            for c in range(DC):
                mm = nc.tensor.matmul(y_ps[:, 0, 0:E8], mean[:, c, :], wr[:, c, :], start=(c == 0), stop=(c == DC - 1))
            mm.then_inc(logits_ready, 1)
            transpose_nodes(nc.tensor, ident, XN, xnt_ps, psum_free, xnt_ready)
            pe.wait_ge(psum_free, GROUPS)
            pe.wait_ge(e_in, 16 * 4 * K2)
            for unit in range(CHUNKS * K2):
                chunk, k = divmod(unit, K2)
                for n in range(2 * FC):
                    half, f = divmod(n, FC)
                    if unit * 2 * FC + n >= 2:
                        pe.wait_ge(h_used, unit * 2 * FC + n - 1)
                    lo = chunk * 2 * HALF + half * HALF
                    for c in range(DC):
                        mm = nc.tensor.matmul(h_ps[:, n % 2, 0:HALF], W1[k][:, c, f * P:(f + 1) * P], XNT[:, c, lo:lo + HALF],
                                              start=(c == 0), stop=(c == DC - 1))
                    mm.then_inc(h_ready, 1)
                pe.wait_ge(h_used, (unit + 1) * 2 * FC)
                for t in range(CT):
                    if unit * CT + t >= 2:
                        pe.wait_ge(y_used, unit * CT + t - 1)
                    for f in range(FC):
                        mm = nc.tensor.matmul(y_ps[:, (unit * CT + t) % 2, 0:D], hid[0][:, f, t * P:(t + 1) * P], W2[k][:, f, :],
                                              start=(f == 0), stop=(f == FC - 1))
                    mm.then_inc(y_ready, 1)

        @block.vector
        def _(dve):
            link = common.link.on(dve)
            V = nc.vector
            for t in range(NT):
                dve.wait_ge(z_ready, t + 1)
                V.scalar_tensor_tensor(X[:, t, :], z_ps[:, t % 2, 0:D], 0.0, X[:, t, :], ALU.max, ALU.add).then_inc(z_added, 1)
            dve.wait_ge(z_added, NT)
            normalise(dve, link, X, XN, stats, aggr, var[:, :], root[:, :], tmp[:, :], var_ready, std_ready, 5, xn_ready)

            def softmax(x, n):
                link(V.tensor_reduce(tmp[:, 0:1], x, AX.X, ALU.max))
                link(V.tensor_scalar(sm[:, :], x, tmp[:, 0:1], None, ALU.subtract))
                dve.sem_inc(arg_ready, 1)
                dve.wait_ge(exp_done, n)
                link(V.tensor_reduce(tmp[:, 0:1], sm[:, :], AX.X, ALU.add))
                link(V.reciprocal(tmp[:, 0:1], tmp[:, 0:1]))
                link(V.tensor_scalar(x, sm[:, :], tmp[:, 0:1], None, ALU.mult))

            dve.wait_ge(logits_ready, 1)
            link(V.tensor_tensor(lg[:, :], y_ps[:, 0, 0:E8], br[:, :], ALU.add))
            softmax(lg[:, :], 1)
            link(V.tensor_scalar(r1[:, :], lg[:, :], float(N), None, ALU.mult))
            link(V.tensor_scalar(r2[:, :], r1[:, :], CAPACITY, None, ALU.max))
            link(V.reciprocal(r2[:, :], r2[:, :]))
            link(V.tensor_scalar(r2[:, :], r2[:, :], CAPACITY, None, ALU.mult))
            link(V.tensor_scalar(r1[:, :], r1[:, :], CAPACITY, None, ALU.is_gt))
            link(V.scalar_tensor_tensor(r2[:, :], r2[:, :], -1.0, r1[:, :], ALU.add, ALU.mult))
            link(V.tensor_scalar(r2[:, :], r2[:, :], 1.0, None, ALU.add))
            link(V.tensor_tensor(lg[:, :], lg[:, :], r2[:, :], ALU.mult))
            softmax(lg[:, :], 2)
            e_of = lambda x: x.unsqueeze(2).to_broadcast([P, E8, E8])
            o_of = lambda x: x.unsqueeze(1).to_broadcast([P, E8, E8])
            link.note(V.tensor_tensor(larger[:, :, :], o_of(lg[:, :]), e_of(lg[:, :]), ALU.is_gt))
            link.note(V.tensor_tensor(equal[:, :, :], o_of(lg[:, :]), e_of(lg[:, :]), ALU.is_equal))
            link(V.tensor_tensor(earlier[:, :, :], o_of(iota[:, 0:E8]), e_of(iota[:, 0:E8]), ALU.is_lt))
            link(V.tensor_tensor(equal[:, :, :], equal[:, :, :], earlier[:, :, :], ALU.mult))
            link(V.tensor_tensor(larger[:, :, :], larger[:, :, :], equal[:, :, :], ALU.add))
            link(V.tensor_reduce(r1[:, :], larger[:, :, :], AX.X, ALU.add))
            for k in range(K2):
                link(V.tensor_scalar(r2[:, :], r1[:, :], float(k), None, ALU.is_equal))
                link(V.tensor_tensor(sm[:, :], r2[:, :], iota[:, 0:E8], ALU.mult))
                link(V.tensor_reduce(tmp[:, 0:1], sm[:, :], AX.X, ALU.add))
                link(V.tensor_copy(which[:, k:k + 1], tmp[:, 0:1]))
                link(V.tensor_tensor(sm[:, :], r2[:, :], lg[:, :], ALU.mult))
                link(V.tensor_reduce(top[:, k:k + 1], sm[:, :], AX.X, ALU.add))
            dve.sem_inc(picked, 1)
            link(V.tensor_tensor(sm[:, 0:1], top[:, 1:2], top[:, 0:1], ALU.subtract))
            dve.sem_inc(arg_ready, 1)
            dve.wait_ge(exp_done, 3)
            link(V.tensor_scalar(tmp[:, 0:1], sm[:, 0:1], 1.0, None, ALU.add))
            link(V.reciprocal(wgt[:, 0:1], tmp[:, 0:1]))
            link(V.tensor_tensor(wgt[:, 1:2], wgt[:, 0:1], sm[:, 0:1], ALU.mult))
            dve.wait_ge(e_in, 16 * 4 * K2)
            link(V.tensor_scalar(bias[:, :], b2[:, 0, :], wgt[:, 0:1], None, ALU.mult))
            link(V.scalar_tensor_tensor(bias[:, :], b2[:, 1, :], wgt[:, 1:2], bias[:, :], ALU.mult, ALU.add))
            dve.wait_ge(psum_free, GROUPS)
            for t in range(NT):
                link.note(V.tensor_tensor(XN[:, t, :], XN[:, t, :], bias[:, :], ALU.add))
            link.wait()
            for unit in range(CHUNKS * K2):
                chunk, k = divmod(unit, K2)
                for t in range(CT):
                    node = chunk * CT + t
                    if k:
                        dve.wait_ge(y_used, (unit - 1) * CT + t + 1)
                    dve.wait_ge(y_ready, unit * CT + t + 1)
                    V.scalar_tensor_tensor(XN[:, node, :], y_ps[:, (unit * CT + t) % 2, 0:D], wgt[:, k:k + 1], XN[:, node, :],
                                           ALU.mult, ALU.add).then_inc(y_used, 1)
            dve.wait_ge(y_used, CHUNKS * K2 * CT)
            for t in range(NT):
                link.note(V.bn_stats(stats[:, t, :], XN[:, t, :]))
            link.wait()
            for t in range(NT):
                link.note(V.bn_aggr(aggr[:, t, :], stats[:, t, :]))
            link.wait()
            link(V.tensor_copy(var[:, :], aggr[:, :, 1]))
            inverse_root(dve, link, var[:, :], root[:, :], tmp[:, :], var_ready, std_ready, 6)
            for t in range(NT):
                link.note(V.tensor_scalar(XN[:, t, :], XN[:, t, :], aggr[:, t, 0:1], root[:, t:t + 1], ALU.subtract, ALU.mult))
            link.wait()
            for t in range(NT):
                link.note(V.tensor_tensor(XN[:, t, :], XN[:, t, :], gam[:, :], ALU.mult))
                link.note(V.tensor_tensor(X[:, t, :], X[:, t, :], bet[:, :], ALU.add))
            link.wait()
            for t in range(NT):
                V.tensor_tensor(XN[:, t, :], XN[:, t, :], X[:, t, :], ALU.add).then_inc(out_ready, 1)


_INS = ["x", "src", "dst", "edge_type_32", "edge_weight1", "L0_gnn_weight", "L0_gnn_bias", "L0_ffn_W_gat",
        "L0_ffn_att_src", "L0_ffn_att_dst", "L0_ffn_b_gat", "L0_ffn_ln_gamma", "L0_ffn_ln_beta", "L0_ffn_W1",
        "L0_ffn_b1", "L0_ffn_W2", "L0_ffn_b2", "L0_ffn_edge_index", "L1_gnn_bases", "L1_gnn_w_comp", "L1_ffn_Wr",
        "L1_ffn_br", "L1_ffn_W1", "L1_ffn_b1", "L1_ffn_W2", "L1_ffn_b2", "L1_ffn_gamma", "L1_ffn_beta"]


def kernel(**inputs):
    import numpy as _np
    import concourse.bacc as _bacc
    from concourse import mybir as _mybir
    from concourse.bass_utils import run_bass_kernel_spmd as _run

    nc = _bacc.Bacc("TRN2", target_bir_lowering=False, num_devices=1)
    arrays, aps = {}, {}
    for name in _INS:
        arr = _np.ascontiguousarray(inputs[name])
        arrays[f"in_{name}"] = arr
        aps[name] = nc.dram_tensor(f"in_{name}", arr.shape, _mybir.dt.from_np(arr.dtype), kind="ExternalInput").ap()
    out = nc.dram_tensor("out_0", (N, D), _mybir.dt.float32, kind="ExternalOutput").ap()
    gnn_ffn(nc, aps, out)
    return _run(nc, [arrays], core_ids=[0]).results[0]["out_0"]
```

```python
import concourse.bass as bass
from concourse import mybir
from contextlib import ExitStack

F32, BF16, I32, U32, U8 = (mybir.dt.float32, mybir.dt.bfloat16, mybir.dt.int32, mybir.dt.uint32, mybir.dt.uint8)
ALU = mybir.AluOpType
ACT = mybir.ActivationFunctionType
AX = mybir.AxisListType

P = 128
N = 3125
D = 256
DC = D // P
NT = -(-N // P)
NFULL = N // P
NTAIL = N - NFULL * P
NPAD = NT * P
EPS = 1e-5

E = 50000
WIN = 32
NW = -(-N // WIN)
ET = -(-E // P) + 1
EROWS = E // ET
EREST = E - EROWS * ET
STAGE = 14
BLOCKS = P * ET // P
KT = 488
KG = -(-KT // P)
WORDS = 4
RELS, BASES = 32, 8
QT = 4
KA = 416
RQ = 12
RS = -(-KT // RQ)
assert -(-E // P) + NT - 1 <= KA and -(-E // P) + NW - 1 <= KT <= RQ * RS <= KG * P and ET % (2 * STAGE) == 0 and EROWS == P - 1

GE = 32768
GT = GE // P
GKT = 280
GSTAGE = 8
GSPLIT = (4, 3, 5, 4)
assert sum(GSPLIT) * 2 * GSTAGE == GT
assert (GE + (P - 1) * NT) // P <= GKT
HEADS, EXPERTS = 4, 4
GW = HEADS * EXPERTS + HEADS


class Link:

    def __init__(self, sem):
        self.sem, self.count, self.base = sem, 0, 0

    def on(self, eng):
        self.eng = eng
        return self

    def __call__(self, ins):
        self.note(ins)
        self.eng.wait_ge(self.sem, self.base + self.count)

    def note(self, ins):
        self.count += 1
        ins.then_inc(self.sem, 1)

    def wait(self):
        self.eng.wait_ge(self.sem, self.base + self.count)

    def enter(self, i, per_step):
        self.kept, self.per_step = self.count, per_step
        self.base, self.count = i * per_step + self.kept, 0

    def leave(self, steps):
        assert self.count == self.per_step, (self.count, self.per_step)
        self.base, self.count = 0, self.kept + steps * self.per_step


class Common:

    def __init__(self, sem):
        self.paused = sem("paused")
        self.link = Link(sem("vector_steps"))
        self.var_ready, self.std_ready = sem("var_ready"), sem("std_ready")
        self.gathered = [sem(f"gathered{k}") for k in range(SETS)]
        self.summed = [sem(f"summed{k}") for k in range(SETS)]
        self.flushed = [sem(f"flushed{n}") for n in range(SET * SETS)]


def ds(start, size):
    return bass.ds(start, size)


def gnn_ffn(nc, a, out):
    scratch = lambda name, shape, dt: nc.dram_tensor(name, shape, dt, kind="Internal").ap()
    xn_dram = scratch("xn_table", (NPAD, D), F32)
    list_dram = scratch("edge_list", (P * ET, WORDS), F32)
    gpay_dram = scratch("attention_records", (P * GKT, 2), F32)
    with ExitStack() as whole:
        common = Common(lambda name: whole.enter_context(nc.semaphore(name)))
        sb = lambda name, shape, dt=F32: whole.enter_context(nc.sbuf_tensor(name, shape, dt))
        X = sb("X", [P, NT, D])
        iota = sb("iota", [P, P])
        ident = sb("ident", [P, P])
        ones = sb("ones", [P, P])
        fine = Slots(sb, "fine", NW, WIN, KT)
        coefs = sb("coefs", [P, RQ * RS, BASES])
        gslot = sb("gslot", [1, GKT], I32)
        gkeep = sb("gkeep", [P, GKT])
        glast = sb("glast", [1, NT], I32)
        y_dram = scratch("expert_rows", (EXPERTS * CHUNKS, P, CT, D), F32)
        adst_dram = scratch("a_dst", (P, NT, HEADS), F32)
        htab_dram = scratch("h_table", (P, NT, GW), F32)
        with ExitStack() as attention:
            sb = lambda name, shape, dt=F32: attention.enter_context(nc.sbuf_tensor(name, shape, dt))
            grecs = sb("grecs", [P, GKT + GSET * GSETS, 2])
            gall = sb("gall", [P, GKT, GW])
            tmax = sb("tmax", [P, HEADS, GKT + 2])
            with ExitStack() as early:
                sb = lambda name, shape, dt=F32: early.enter_context(nc.sbuf_tensor(name, shape, dt))
                grow = sb("grow", [P, GT], I32)
                gpay = sb("gpay", [P, GT, 2])
                with ExitStack() as first:
                    sb = lambda name, shape, dt=F32: first.enter_context(nc.sbuf_tensor(name, shape, dt))
                    coarse = Slots(sb, "coarse", NT, P, KA)
                    relf, norm = sb("relation", [P, RQ * RS]), sb("norm", [P, RQ * RS])
                    sort_edges(nc, common, a, X, iota, ident, ones, fine, coarse, relf, norm,
                               grow, gpay, gslot, gkeep, glast, xn_dram, list_dram, gpay_dram)
                    agg_dram = scratch("neighbour_sums", (NT, P, D + 1), F32)
                    sum_neighbours(nc, common, a, iota, ident, coarse, relf, norm, coefs, agg_dram, xn_dram)
                XNT = early.enter_context(nc.sbuf_tensor("XNT", [P, DC, NPAD], F32))
                table_dram = scratch("attention_table", (NPAD, GW), F32)
                first_update(nc, common, a, X, ident, agg_dram, grow, gpay, XNT, gpay_dram, table_dram, adst_dram, htab_dram)
                attention_maxima(nc, common, a, iota, ident, grow, gpay, grecs, gall, tmax, XNT, gpay_dram, table_dram, y_dram)
            second_update(nc, common, a, X, iota, ident, gslot, gkeep, glast, grecs, gall, tmax, adst_dram, htab_dram, y_dram, xn_dram)
        z_dram = scratch("basis_sums", (NT * P // WIN, P, DC * BASES * WIN), F32)
        sum_relations(nc, common, iota, fine, coefs, xn_dram, z_dram)
        third_update(nc, common, a, X, iota, ident, ones, z_dram, out)


def count_windows(dve, link, windows, unroll, T, win, iota, hot, count):
    with dve.Fori(0, windows // unroll) as i:
        link.enter(i, unroll)
        for u in range(unroll):
            w = i * unroll + u
            link.note(dve.tensor_scalar(hot[:, ds(w, 1), 0:T].rearrange("p o t -> p (o t)"), win[:, 0:T],
                                                   iota[:, ds(w, 1)], None, ALU.is_equal, ALU.add,
                                                   accum_out=count[:, ds(w, 1)]))
        link.leave(windows // unroll)
    link.wait()


def rank_edges(dve, link, windows, unroll, T, hot, start, rank, pos):
    with dve.Fori(0, windows // unroll) as i:
        link.enter(i, 3 * unroll)
        for u in range(unroll):
            w = i * unroll + u
            row = hot[:, ds(w, 1), 0:T].rearrange("p o t -> p (o t)")
            link(dve.tensor_tensor_scan(rank[:, 0:T], row, row, start[:, ds(w, 1)], ALU.add, ALU.max))
            link(dve.tensor_tensor(rank[:, 0:T], rank[:, 0:T], row, ALU.mult))
            link(dve.tensor_tensor(pos[:, 0:T], pos[:, 0:T], rank[:, 0:T], ALU.add))
        link.leave(windows // unroll)


def rows_of(dve, link, T, columns, pos, pos_i, rank, row_i):
    link(dve.tensor_scalar(pos_i[:, 0:T], pos[:, 0:T], -1.0, None, ALU.add))
    link(dve.tensor_scalar(row_i[:, 0:T], pos_i[:, 0:T], P - 1, None, ALU.bitwise_and))
    link(dve.tensor_copy(rank[:, 0:T], row_i[:, 0:T]))
    link(dve.tensor_scalar(row_i[:, 0:T], pos_i[:, 0:T], 7, None, ALU.arith_shift_right))
    link(dve.tensor_copy(pos[:, 0:T], row_i[:, 0:T]))
    link(dve.scalar_tensor_tensor(row_i[:, 0:T], rank[:, 0:T], float(columns), pos[:, 0:T], ALU.mult, ALU.add))


def inverse_root(dve, link, var, root, tmp, var_ready, std_ready, n):
    link(dve.tensor_scalar(var, var, EPS, None, ALU.add))
    dve.sem_inc(var_ready, 1)
    dve.wait_ge(std_ready, n)
    link(dve.reciprocal(root, root))
    link(dve.tensor_tensor(tmp, root, root, ALU.mult))
    link(dve.tensor_tensor(tmp, tmp, var, ALU.mult))
    link(dve.tensor_scalar(tmp, tmp, -0.5, 1.5, ALU.mult, ALU.add))
    link(dve.tensor_tensor(root, root, tmp, ALU.mult))


def measure(dve, link, X, stats, aggr, t):
    link(dve.bn_stats(stats[:, t, :], X[:, t, :]))
    link.note(dve.bn_aggr(aggr[:, t, :], stats[:, t, :]))


def normalise(dve, link, X, XN, stats, aggr, var, root, tmp, var_ready, std_ready, n, xn_ready, measured=False):
    if not measured:
        for t in range(NT):
            link.note(dve.bn_stats(stats[:, t, :], X[:, t, :]))
        link.wait()
        for t in range(NT):
            link.note(dve.bn_aggr(aggr[:, t, :], stats[:, t, :]))
    link.wait()
    link(dve.tensor_copy(var, aggr[:, :, 1]))
    inverse_root(dve, link, var, root, tmp, var_ready, std_ready, n)
    for t in range(NT):
        dve.tensor_scalar(XN[:, t, :], X[:, t, :], aggr[:, t, 0:1], root[:, t:t + 1],
                          ALU.subtract, ALU.mult).then_inc(xn_ready, 1)


def stage_columns(act, staged, cols, idx, rec, rows, pay):
    act.activation(rec[:, :, :], pay[:, cols, :], ACT.Copy).then_inc(staged, 1)
    act.activation(idx[:, :], rows[:, cols], ACT.Copy).then_inc(staged, 1)


def stage_first(act, staged, first, width, idx, rec, rows, pay):
    for k in range(2):
        stage_columns(act, staged, ds(first + k * width, width), idx[k], rec[k], rows, pay)


def stage_rest(act, staged, scattered, steps, first, width, idx, rec, rows, pay):
    with act.Fori(1, steps) as i:
        for k in range(2):
            act.wait_ge(scattered[k], i * (16 * width))
            stage_columns(act, staged, ds(i * (2 * width) + (first + k * width), width), idx[k], rec[k], rows, pay)


def scatter_staged(pool, paused, staged, scattered, steps, width, idx, rec, dram):
    with pool.Fori(0, steps) as i:
        for k in range(2):
            pool.wait_ge(staged, i * 4 + 2 * k + 2)
            pool.sem_inc(paused, 1)
            for t in range(width):
                pool.indirect_dma_start(dram, bass.IndirectOffsetOnAxis(ap=idx[k][:, t:t + 1].bitcast(U32), axis=0),
                                        rec[k][:, t, :], None).then_inc(scattered[k], 16)
    for k in range(2):
        pool.wait_ge(scattered[k], 16 * width * steps)


class Slots:

    def __init__(self, sb, name, groups, nodes, count):
        self.groups, self.nodes, self.count, self.wide = groups, nodes, count, -(-count // P)
        self.group = sb(name + "_group", [1, count], I32)
        self.last = sb(name + "_last", [1, count], I32)
        self.keep = sb(name + "_keep", [P, count])
        self.source = sb(name + "_source", [P, count], I32)
        self.target = sb(name + "_target", [P, count])

    def scratch(self, sb, name):
        n = self.groups
        self.start, self.end = sb(name + "_start", [P, n]), sb(name + "_end", [P, n])
        self.first_i, self.last_i = sb(name + "_first_i", [P, n], I32), sb(name + "_last_i", [P, n], I32)
        self.first, self.tiles, self.shift = sb(name + "_first", [P, n]), sb(name + "_tiles", [P, n]), sb(name + "_shift", [P, n])
        self.col, self.pair = sb(name + "_col", [P, 1]), sb(name + "_pair", [P, 2])
        self.full, self.ge = sb(name + "_full", [P, self.wide * P]), sb(name + "_ge", [P, self.wide * P])
        self.base, self.at = sb(name + "_base", [P, self.wide]), sb(name + "_at", [P, self.wide])
        self.block = sb(name + "_block", [P, self.wide], I32)


def place_slots(V, link, ident, slot_iota, z):
    n = z.groups
    link.note(V.tensor_copy(z.first_i[:, :], z.start[:, :]))
    link(V.tensor_scalar(z.last_i[:, :], z.end[:, :], float(P - 1), None, ALU.add))
    link.note(V.tensor_scalar(z.first_i[:, :], z.first_i[:, :], 7, None, ALU.arith_shift_right))
    link(V.tensor_scalar(z.last_i[:, :], z.last_i[:, :], 7, None, ALU.arith_shift_right))
    link.note(V.tensor_copy(z.first[:, :], z.first_i[:, :]))
    link(V.tensor_copy(z.tiles[:, :], z.last_i[:, :]))
    link(V.tensor_tensor(z.tiles[:, :], z.tiles[:, :], z.first[:, :], ALU.subtract))
    link(V.tensor_scalar(z.tiles[:, :], z.tiles[:, :], 1.0, None, ALU.max))
    link(V.tensor_tensor_scan(z.end[:, :], z.tiles[:, :], z.tiles[:, :], 0.0, ALU.add, ALU.max))
    link(V.tensor_tensor(z.shift[:, :], z.first[:, :], z.end[:, :], ALU.subtract))
    link(V.tensor_tensor(z.shift[:, :], z.shift[:, :], z.tiles[:, :], ALU.add))
    link.note(V.memset(z.first[:, n - 1:n], 0.0))
    link(V.tensor_tensor(z.first[:, 0:n - 1], z.shift[:, 1:n], z.shift[:, 0:n - 1], ALU.subtract))
    link(V.tensor_tensor(z.full[:, 0:n], ident[:, 0:n], z.end[:, :], ALU.mult))
    link(V.tensor_reduce(z.col[:, :], z.full[:, 0:n], AX.X, ALU.add))
    link(V.tensor_tensor(z.full[:, 0:n], ident[:, 0:n], z.first[:, :], ALU.mult))
    link.note(V.tensor_reduce(z.pair[:, 1:2], z.full[:, 0:n], AX.X, ALU.add))
    link.note(V.memset(z.pair[:, 0:1], 1.0))
    link(V.tensor_scalar(z.ge[:, :], slot_iota[:, 0:z.wide * P], z.col[:, :], None, ALU.is_ge))


def count_ends(pe, ones, z, end_ps, pair_ps):
    n = z.groups
    for j in range(z.wide):
        pe.matmul(pair_ps[:, j, :], z.ge[0:n, j * P:(j + 1) * P], z.pair[0:n, :], start=True, stop=True)
    return pe.matmul(end_ps[:, 0:z.wide * P], ones[0:n, :], z.ge[0:n, :], start=True, stop=True)


def describe_slots(V, link, slot_at, z, end_ps, pair_ps):
    K = z.count
    link(V.tensor_scalar(z.full[:, :], end_ps[:, 0:z.wide * P], float(z.groups - 1), None, ALU.min))
    link.note(V.tensor_copy(z.group[:, :], z.full[0:1, 0:K]))
    link.note(V.memset(z.keep[:, 0:1], 0.0))
    link.note(V.memset(z.last[:, K - 1:K], 1))
    link.note(V.tensor_tensor(z.keep[:, 1:K], z.full[:, 1:K], z.full[:, 0:K - 1], ALU.is_equal))
    link.note(V.tensor_tensor(z.last[:, 0:K - 1], z.full[0:1, 1:K], z.full[0:1, 0:K - 1], ALU.not_equal))
    link.note(V.tensor_scalar(z.base[:, :], pair_ps[:, :, 0], float(z.groups - 1), float(z.nodes), ALU.min, ALU.mult))
    link(V.tensor_tensor(z.at[:, :], pair_ps[:, :, 1], slot_at[:, 0:z.wide], ALU.add))
    link(V.tensor_scalar(z.block[:, :], z.at[:, :], float(BLOCKS - 1), None, ALU.min))


def sort_edges(nc, common, a, X, iota, ident, ones, fine, coarse, relf, norm,
               grow, gpay, gslot, gkeep, glast, xn_dram, list_dram, gpay_dram):
    paused, var_ready, std_ready = common.paused, common.var_ready, common.std_ready
    with ExitStack() as ctx:
        sb = lambda name, shape, dt=F32: ctx.enter_context(nc.sbuf_tensor(name, shape, dt))
        sem = lambda name: ctx.enter_context(nc.semaphore(name))
        W1 = NW + 1
        GBINS, UN = 5, 3
        stats, aggr, rstd = sb("stats0", [P, NT, 6]), sb("aggr0", [P, NT, 2]), sb("rstd0", [P, NT])
        var, tmp = sb("var0", [P, NT]), sb("tmp0", [P, NT])
        before = sb("before", [P, P])
        dst, nxt, src, rel = (sb(n, [P, ET], I32) for n in ("dst", "next_dst", "src", "rel"))
        norm_in = sb("norm_in", [P, ET])
        rec = sb("rec", [P, ET, WORDS])
        win = sb("win", [P, ET])
        count, start = sb("count", [P, W1 + 1]), sb("start", [P, W1])
        total, place_end = sb("total", [P, W1]), sb("place_end", [P, W1])
        kinds = (fine, coarse)
        for z, name in zip(kinds, ("fine", "coarse")):
            z.scratch(sb, name)
        rank, pos = sb("rank", [P, ET]), sb("pos", [P, ET])
        pos_i, row_i = sb("pos_i", [P, ET], I32), sb("row_i", [P, ET], I32)
        gdst, gsrc, gtmp, glow = (sb(n, [P, GT], I32) for n in ("gdst", "gsrc", "gtmp", "glow"))
        gwin, gcount, gstart = sb("gwin", [P, GT]), sb("gcount", [P, NT]), sb("gstart", [P, NT])
        gtotal, gtiles, gend = sb("gtotal", [P, NT], I32), sb("gtiles", [P, NT]), sb("gend", [P, NT])
        gpad = sb("gpad", [P, GKT * 2])
        unsorted = sb("unsorted", [1, 1], I32)
        slot_iota = sb("slot_iota", [P, KG * P])
        slot_at = sb("slot_at", [P, KG])
        tile_col = sb("tile_col", [P, 1])
        gidx = [sb(f"gidx0{k}", [P, GSTAGE], I32) for k in range(2)]
        grec = [sb(f"grec0{k}", [P, GSTAGE, 2]) for k in range(2)]
        idx_stage = [sb(f"idx_stage{k}", [P, STAGE], I32) for k in range(2)]
        rec_stage = [sb(f"rec_stage{k}", [P, STAGE, WORDS]) for k in range(2)]
        consts = sem("consts")
        x_in, list_in, glist_in = sem("x_in"), sem("list_in"), sem("glist_in")
        cleared, pads_out = sem("cleared"), sem("pads_out")
        gcount_ready, gprefix_ready, gend_ready, gend_done, grows_ready = (
            sem(n) for n in ("gcount_ready", "gprefix_ready", "gend_ready", "gend_done", "grows_ready"))
        count_ready, prefix_ready, end_ready, end_done = (sem(n) for n in ("count_ready", "prefix_ready", "end_ready", "end_done"))
        rec_ready, list_out = sem("rec_ready"), sem("list_out")
        gstaged, gscattered = [sem(f"gstaged{n}") for n in range(2)], [[sem(f"gscattered{n}{k}") for k in range(2)] for n in range(2)]
        vs, rows_ready, staged = sem("sort_steps"), sem("rows_ready"), sem("staged")
        scattered = [sem("scattered0"), sem("scattered1")]
        slots_in, offset, turned, slots_made = (sem(n) for n in ("slots_in", "offset", "turned", "slots_made"))
        xn_ready, xn_out = sem("xn_ready"), sem("xn_out")

        listing = ExitStack()
        hot = listing.enter_context(nc.sbuf_tensor("one_hot", [P, W1, ET], U8))
        with ExitStack() as counting, nc.Block() as block:
            pb = lambda name, shape: counting.enter_context(nc.psum_tensor(name, shape, F32))
            cnt_ps, gcnt_ps = pb("cnt_ps", [P, 2, 256]), pb("gcnt_ps", [P, 2, 256])
            gend_ps = pb("gend_ps", [P, 512])
            end_ps, pair_ps = [pb(f"end_ps{n}", [P, 512]) for n in range(2)], [pb(f"pair_ps{n}", [P, KG, 2]) for n in range(2)]

            @block.sync
            def _(sp):
                for tile, row in ((gsrc, 0), (gdst, 1)):
                    sp.dma_start(tile[:, :], a["L0_ffn_edge_index"][row, :].rearrange("(p t) -> p t", t=GT)).then_inc(glist_in, 16)
                sp.wait_ge(cleared, 8)
                for tile, name in ((dst, "dst"), (src, "src"), (rel, "edge_type_32"), (norm_in, "edge_weight1")):
                    flat = a[name].rearrange("e o -> (e o)") if name == "edge_weight1" else a[name]
                    sp.dma_start(tile[0:EROWS, :], flat[0:EROWS * ET].rearrange("(p t) -> p t", t=ET)).then_inc(list_in, 16)
                    sp.dma_start(tile[EROWS:P, 0:EREST], flat[EROWS * ET:E].rearrange("(p t) -> p t", p=1)).then_inc(list_in, 16)
                sp.dma_start(nxt[0:EROWS, :], a["dst"][1:EROWS * ET + 1].rearrange("(p t) -> p t", t=ET)).then_inc(list_in, 16)
                sp.dma_start(nxt[EROWS:P, 0:EREST - 1], a["dst"][EROWS * ET + 1:E].rearrange("(p t) -> p t", p=1)).then_inc(list_in, 16)
                sp.dma_start(gpay_dram.rearrange("(p k) w -> p (k w)", p=P), gpad[:, :]).then_inc(pads_out, 16)
                sp.dma_start(X[:, 0:NFULL, :], a["x"][0:NFULL * P, :].rearrange("(t p) d -> p t d", p=P)).then_inc(x_in, 16)
                sp.dma_start(X[0:NTAIL, NFULL, :], a["x"][NFULL * P:N, :]).then_inc(x_in, 16)
                sp.wait_ge(rec_ready, WORDS)
                sp.dma_start(list_dram.rearrange("(p t) w -> p t w", p=P), rec[:, :, :]).then_inc(list_out, 16)
                sp.wait_ge(list_out, 16)
                sp.wait_ge(x_in, 32)

            @block.gpsimd
            def _(pool):
                nc.gpsimd.iota(iota[:, :], [[1, P]], base=0, channel_multiplier=0, allow_small_or_imprecise_dtypes=True).then_inc(consts, 1)
                nc.gpsimd.iota(slot_iota[:, :], [[1, KG * P]], base=0, channel_multiplier=0, allow_small_or_imprecise_dtypes=True).then_inc(consts, 1)
                nc.gpsimd.iota(slot_at[:, :], [[P, KG]], base=0, channel_multiplier=1, allow_small_or_imprecise_dtypes=True).then_inc(consts, 1)
                nc.gpsimd.memset(ones[:, :], 1.0).then_inc(consts, 1)
                pool.wait_ge(consts, 4)
                nc.gpsimd.affine_select(out=ident[:, :], in_=ones[:, :], compare_op=ALU.is_equal, fill=0.0, base=0,
                                        pattern=[[-1, P]], channel_multiplier=1).then_inc(consts, 1)
                nc.gpsimd.affine_select(out=before[:, :], in_=ones[:, :], compare_op=ALU.is_gt, fill=0.0, base=0,
                                        pattern=[[1, P]], channel_multiplier=-1).then_inc(consts, 1)
                pool.wait_ge(pads_out, 16)
                scatter_staged(pool, paused, gstaged[0], gscattered[0], GSPLIT[0], GSTAGE, gidx, grec, gpay_dram)

            @block.scalar
            def _(act):
                act.wait_ge(list_in, 16 * 10)
                for w, tile in enumerate((src, dst, rel, norm_in)):
                    nc.scalar.activation(rec[:, :, w:w + 1], tile[:, :].unsqueeze(2), ACT.Copy).then_inc(rec_ready, 1)
                act.wait_ge(grows_ready, 1)
                stage_first(nc.scalar, gstaged[0], 0, GSTAGE, gidx, grec, grow, gpay)
                stage_rest(nc.scalar, gstaged[0], gscattered[0], GSPLIT[0], 0, GSTAGE, gidx, grec, grow, gpay)

            @block.tensor
            def _(pe):
                pe.wait_ge(consts, 6)
                pe.wait_ge(gcount_ready, 1)
                nc.tensor.matmul(gcnt_ps[:, 0, 0:NT], before[:, :], gcount[:, :], start=True, stop=True)
                nc.tensor.matmul(gcnt_ps[:, 1, 0:NT], ones[:, :], gcount[:, :], start=True, stop=True).then_inc(gprefix_ready, 1)
                pe.wait_ge(gend_ready, 1)
                nc.tensor.matmul(gend_ps[:, 0:GKT], ones[0:NT, :], fine.ge[0:NT, 0:GKT], start=True, stop=True).then_inc(gend_done, 1)
                pe.wait_ge(count_ready, 1)
                nc.tensor.matmul(cnt_ps[:, 0, 0:W1], before[:, :], count[:, 0:W1], start=True, stop=True)
                nc.tensor.matmul(cnt_ps[:, 1, 0:W1 + 1], ones[:, :], count[:, :], start=True, stop=True).then_inc(prefix_ready, 1)
                for n, z in enumerate(kinds):
                    pe.wait_ge(end_ready, n + 1)
                    count_ends(nc.tensor, ones, z, end_ps[n], pair_ps[n]).then_inc(end_done, 1)

            @block.vector
            def _(dve):
                link = common.link.on(dve)
                V = nc.vector
                V.memset(gpad[:, :], 0.0).then_inc(cleared, 1)
                dve.wait_ge(cleared, 1)
                V.memset(gpad[:, :].rearrange("p (k w) -> p k w", w=2)[:, :, 1:2], -1.0).then_inc(cleared, 1)
                for tile, fill in ((dst, NW * WIN), (nxt, NW * WIN), (src, 0), (rel, 0), (norm_in, 0.0), (X[:, NFULL, :], 0.0)):
                    V.memset(tile[:, :], fill).then_inc(cleared, 1)
                link(V.memset(pos[:, 0:GT], 0.0))
                dve.wait_ge(glist_in, 32)
                dve.wait_ge(consts, 6)
                link.note(V.tensor_scalar(gtmp[:, :], gdst[:, :], 7, None, ALU.arith_shift_right))
                link(V.tensor_scalar(glow[:, :], gdst[:, :], P - 1, None, ALU.bitwise_and))
                link.note(V.tensor_copy(gwin[:, :], gtmp[:, :]))
                link.note(V.tensor_copy(gpay[:, :, 0:1].bitcast(I32), gsrc[:, :].unsqueeze(2)))
                link(V.tensor_copy(gpay[:, :, 1:2], glow[:, :].unsqueeze(2)))
                count_windows(dve, link, NT, GBINS, GT, gwin, iota, hot, gcount)
                dve.sem_inc(gcount_ready, 1)
                dve.wait_ge(gprefix_ready, 1)
                link(V.tensor_scalar(gtotal[:, :], gcnt_ps[:, 1, 0:NT], float(P - 1), None, ALU.add))
                link(V.tensor_scalar(gtotal[:, :], gtotal[:, :], 7, None, ALU.arith_shift_right))
                link(V.tensor_copy(gtiles[:, :], gtotal[:, :]))
                link(V.tensor_tensor_scan(gend[:, :], gtiles[:, :], gtiles[:, :], 0.0, ALU.add, ALU.max))
                link(V.tensor_tensor(gstart[:, :], gend[:, :], gtiles[:, :], ALU.subtract))
                link(V.tensor_scalar(gstart[:, :], gstart[:, :], float(P), None, ALU.mult))
                link(V.tensor_tensor(gstart[:, :], gstart[:, :], gcnt_ps[:, 0, 0:NT], ALU.add))
                rank_edges(dve, link, NT, GBINS, GT, hot, gstart, rank, pos)
                rows_of(dve, link, GT, GKT, pos, pos_i, rank, grow)
                dve.sem_inc(grows_ready, 1)
                link(V.tensor_scalar(rank[:, 0:NT], gtiles[:, :], 0.5, float(GKT + 1), ALU.is_lt, ALU.mult))
                link(V.tensor_tensor(rank[:, 0:NT], rank[:, 0:NT], gend[:, :], ALU.max))
                link(V.tensor_scalar(glast[:, :], rank[0:1, 0:NT], -1.0, None, ALU.add))
                link(V.tensor_tensor(fine.full[:, 0:NT], ident[:, 0:NT], gend[:, :], ALU.mult))
                link(V.tensor_reduce(tile_col[:, :], fine.full[:, 0:NT], AX.X, ALU.add))
                link(V.tensor_scalar(fine.ge[:, 0:GKT], slot_iota[:, 0:GKT], tile_col[:, :], None, ALU.is_ge))
                dve.sem_inc(gend_ready, 1)
                dve.wait_ge(list_in, 16 * 10)
                link.note(V.tensor_scalar(row_i[:, :], dst[:, :], 5, None, ALU.arith_shift_right))
                link(V.tensor_scalar(pos_i[:, :], nxt[:, :], 5, None, ALU.arith_shift_right))
                link.note(V.tensor_copy(win[:, :], row_i[:, :]))
                link(V.tensor_tensor(rank[:, :], row_i[:, :], pos_i[:, :], ALU.is_gt))
                link(V.tensor_reduce(count[:, W1:W1 + 1], rank[:, :], AX.X, ALU.add))
                count_windows(dve, link, W1, UN, ET, win, iota, hot, count)
                dve.sem_inc(count_ready, 1)
                dve.wait_ge(gend_done, 1)
                link(V.tensor_scalar(fine.full[:, 0:GKT], gend_ps[:, 0:GKT], float(NT - 1), None, ALU.min))
                link.note(V.tensor_copy(gslot[:, :], fine.full[0:1, 0:GKT]))
                link.note(V.memset(gkeep[:, 0:1], 0.0))
                link(V.tensor_tensor(gkeep[:, 1:GKT], fine.full[:, 1:GKT], fine.full[:, 0:GKT - 1], ALU.is_equal))
                dve.wait_ge(prefix_ready, 1)
                link.note(V.tensor_scalar(unsorted[:, :], cnt_ps[0:1, 1, W1:W1 + 1], 1.0, None, ALU.min))
                link(V.tensor_copy(total[:, :], cnt_ps[:, 1, 0:W1]))
                link(V.tensor_tensor_scan(place_end[:, :], total[:, :], total[:, :], 0.0, ALU.add, ALU.max))
                link(V.tensor_tensor(start[:, :], place_end[:, :], total[:, :], ALU.subtract))
                link.note(V.tensor_copy(fine.start[:, :], start[:, 0:NW]))
                link.note(V.tensor_copy(fine.end[:, :], place_end[:, 0:NW]))
                ratio = coarse.nodes // fine.nodes
                link.note(V.tensor_copy(coarse.start[:, :], start[:, 0:NW:ratio]))
                link.note(V.tensor_copy(coarse.end[:, 0:NT - 1], start[:, ratio:NW:ratio]))
                link(V.memset(coarse.end[:, NT - 1:NT], float(E)))
                for z in kinds:
                    place_slots(V, link, ident, slot_iota, z)
                    dve.sem_inc(end_ready, 1)
                link(V.tensor_tensor(start[:, :], start[:, :], cnt_ps[:, 0, 0:W1], ALU.add))
                for n, z in enumerate(kinds):
                    dve.wait_ge(end_done, n + 1)
                    describe_slots(V, link, slot_at, z, end_ps[n], pair_ps[n])

        with nc.Block() as block:
            @block.vector
            def _(dve):
                wrong = nc.values_load(unsorted[0:1, 0:1], engines=[dve.engine], min_val=0, max_val=1)
                with dve.If(wrong > 0):
                    link = Link(vs).on(dve)
                    link(nc.vector.memset(pos[:, :], 0.0))
                    rank_edges(dve, link, W1, UN, ET, hot, start, rank, pos)
                    nc.vector.tensor_scalar(row_i[:, :], pos[:, :], -1.0, None, ALU.add).then_inc(rows_ready, 1)

            @block.scalar
            def _(act):
                wrong = nc.values_load(unsorted[0:1, 0:1], engines=[act.engine], min_val=0, max_val=1)
                with act.If(wrong > 0):
                    act.wait_ge(rows_ready, 1)
                    stage_first(nc.scalar, staged, 0, STAGE, idx_stage, rec_stage, row_i, rec)
                    stage_rest(nc.scalar, staged, scattered, ET // (2 * STAGE), 0, STAGE, idx_stage, rec_stage, row_i, rec)

            @block.gpsimd
            def _(pool):
                wrong = nc.values_load(unsorted[0:1, 0:1], engines=[pool.engine], min_val=0, max_val=1)
                with pool.If(wrong > 0):
                    scatter_staged(pool, paused, staged, scattered, ET // (2 * STAGE), STAGE, idx_stage, rec_stage, list_dram)

        listing.close()
        XN = sb("XN0", [P, NT, D])
        slot_rec = [sb(f"slot_rec{n}", [P, z.wide, P, WORDS]) for n, z in enumerate(kinds)]
        with ExitStack() as turn, nc.Block() as block:
            rec_ps = turn.enter_context(nc.psum_tensor("rec_ps", [P, 6, KG * P], F32))
            words = [(0, 0, fine.source), (0, 1, fine.target), (0, 2, relf), (0, 3, norm), (1, 0, coarse.source), (1, 1, coarse.target)]

            @block.sync
            def _(sp):
                sp.wait_ge(xn_ready, NT)
                sp.dma_start(xn_dram.rearrange("(t p) d -> p t d", p=P), XN[:, :, :]).then_inc(xn_out, 16)
                sp.wait_ge(xn_out, 16)

            @block.gpsimd
            def _(pool):
                blocks = list_dram.rearrange("(b e) w -> b (e w)", e=P)
                for n, z in enumerate(kinds):
                    for j in range(z.wide):
                        pool.indirect_dma_start(slot_rec[n][:, j, :, :].rearrange("p e w -> p (e w)"), None, blocks,
                                                bass.IndirectOffsetOnAxis(ap=z.block[:, j:j + 1].bitcast(U32), axis=0)
                                                ).then_inc(slots_in, 16)
                scatter_staged(pool, paused, gstaged[1], gscattered[1], GSPLIT[1], GSTAGE, gidx, grec, gpay_dram)

            @block.scalar
            def _(act):
                first_col = GSPLIT[0] * 2 * GSTAGE
                stage_first(nc.scalar, gstaged[1], first_col, GSTAGE, gidx, grec, grow, gpay)
                for m, (n, w, to) in enumerate(words):
                    act.wait_ge(turned, m + 1)
                    nc.scalar.activation(to[:, :], rec_ps[:, m, 0:to.shape[1]], ACT.Copy).then_inc(slots_made, 1)
                act.wait_ge(var_ready, 1)
                nc.scalar.activation(rstd[:, :], var[:, :], ACT.Sqrt).then_inc(std_ready, 1)
                stage_rest(nc.scalar, gstaged[1], gscattered[1], GSPLIT[1], first_col, GSTAGE, gidx, grec, grow, gpay)

            @block.tensor
            def _(pe):
                pe.wait_ge(offset, 1)
                for m, (n, w, to) in enumerate(words):
                    for j in range(kinds[n].wide):
                        mm = nc.tensor.transpose(rec_ps[:, m, j * P:(j + 1) * P], slot_rec[n][:, j, :, w], ident[:, :])
                    mm.then_inc(turned, 1)

            @block.vector
            def _(dve):
                link = common.link.on(dve)
                dve.wait_ge(slots_in, 16 * sum(z.wide for z in kinds))
                for n, z in enumerate(kinds):
                    for j in range(z.wide):
                        at = slot_rec[n][:, j, :, 1]
                        link.note(nc.vector.tensor_scalar(at, at, z.base[:, j:j + 1], None, ALU.subtract))
                link.wait()
                dve.sem_inc(offset, 1)
                normalise(dve, link, X, XN, stats, aggr, var[:, :], rstd[:, :], tmp[:, :], var_ready, std_ready, 1, xn_ready)


SET = 2
SETS = 4


def sum_neighbours(nc, common, a, iota, ident, coarse, relf, norm, coefs, agg_dram, table):
    paused, gathered, summed, flushed = common.paused, common.gathered, common.summed, common.flushed
    with ExitStack() as ctx:
        sb = lambda name, shape, dt=F32: ctx.enter_context(nc.sbuf_tensor(name, shape, dt))
        pb = lambda name, shape, dt=F32: ctx.enter_context(nc.psum_tensor(name, shape, dt))
        sem = lambda name: ctx.enter_context(nc.semaphore(name))
        PER = SET * SETS
        STEPS = KA // PER
        BANKS = 4
        rows = [sb(f"rows{k}", [P, SET, D + 1]) for k in range(SETS)]
        idx = [sb(f"idx{k}", [P, SET], I32) for k in range(SETS)]
        hot = [sb(f"hot{k}", [P, SET, P]) for k in range(SETS)]
        acc = [sb(f"tile_acc{n}", [P, D + 1]) for n in range(PER)]
        part = pb("part", [P, BANKS, 512])
        relhot = sb("relhot", [P, RQ, RELS])
        relhot_t = sb("relhot_t", [P, RQ // QT, P])
        wcomp = sb("wcomp", [P, QT, BASES])
        relt_ps, coef_ps = pb("relt_ps", [P, 512]), pb("coef_ps", [P, 512])
        idx_ready, hot_ready, added, cleared = (sem(n) for n in ("idx_ready", "hot_ready", "added", "cleared1"))
        wc_in, relhot_ready, relt_ready, relt_copied, coef_ready, coefs_made = (
            sem(n) for n in ("wc_in", "relhot_ready", "relt_ready", "relt_copied", "coef_ready", "coefs_made"))
        block = ctx.enter_context(nc.Block())
        parts = ((0, RS, True), (RS, STEPS, False))

        @block.sync
        def _(sp):
            sp.wait_ge(cleared, 2)
            for q in range(QT):
                sp.dma_start(wcomp[q * RELS:(q + 1) * RELS, q, :], a["L1_gnn_w_comp"]).then_inc(wc_in, 16)
            with sp.Fori(0, STEPS) as i:
                _, tiles = nc.values_load_multi_w_load_instructions(coarse.group[0:1, ds(i * PER, PER)], engines=[sp.engine],
                                                                    min_val=0, max_val=NT - 1)
                _, lasts = nc.values_load_multi_w_load_instructions(coarse.last[0:1, ds(i * PER, PER)], engines=[sp.engine],
                                                                    min_val=0, max_val=1)
                for n in range(PER):
                    sp.wait_ge(added, i * PER + (BANKS + n + 1))
                    sp.dma_start(agg_dram[ds(tiles[n], 1)].rearrange("o p d -> (o p) d"), acc[n][:, :],
                                 cond=lasts[n] > 0).then_inc(flushed[n], 16)
            for n in range(PER):
                sp.wait_ge(flushed[n], 16 * STEPS + 1)

        @block.scalar
        def _(act):
            for lo, hi, coefficients in parts:
                with act.Fori(lo, hi) as i:
                    for k in range(SETS):
                        act.wait_ge(summed[k], i + 1)
                        nc.scalar.activation(idx[k][:, :], coarse.source[:, ds(i * PER + k * SET, SET)], ACT.Copy).then_inc(idx_ready, 1)
                    if coefficients:
                        act.wait_ge(relt_ready, i + 1)
                        nc.scalar.activation(relhot_t[:, :, :].rearrange("p q e -> p (q e)"), relt_ps[:, 0:RQ // QT * P],
                                             ACT.Copy).then_inc(relt_copied, 1)

        @block.gpsimd
        def _(pool):
            pool.wait_ge(cleared, 2 + SETS)
            with pool.Fori(0, STEPS) as i:
                for k in range(SETS):
                    pool.wait_ge(idx_ready, i * SETS + k + 1)
                    pool.sem_inc(paused, 1)
                    for u in range(SET):
                        pool.indirect_dma_start(rows[k][:, u, 0:D], None, table,
                                                bass.IndirectOffsetOnAxis(ap=idx[k][:, u:u + 1].bitcast(U32), axis=0)
                                                ).then_inc(gathered[k], 16)

        @block.tensor
        def _(pe):
            pe.wait_ge(wc_in, 16 * QT)
            for lo, hi, coefficients in parts:
                with pe.Fori(lo, hi) as i:
                    for k in range(SETS):
                        if k == 1 and coefficients:
                            pe.wait_ge(relhot_ready, i + 1)
                            for q in range(RQ // QT):
                                mm = nc.tensor.transpose(relt_ps[:, q * P:(q + 1) * P],
                                                         relhot[:, q * QT:(q + 1) * QT, :].rearrange("p q r -> p (q r)"), ident[:, :])
                            mm.then_inc(relt_ready, 1)
                        pe.wait_ge(hot_ready, i * SETS + k + 1)
                        pe.wait_ge(gathered[k], (i + 1) * (16 * SET))
                        for u in range(SET):
                            n = k * SET + u
                            pe.wait_ge(added, i * PER + n + 1)
                            mm = nc.tensor.matmul(part[:, n % BANKS, 0:D + 1], hot[k][:, u, :], rows[k][:, u, :], start=True, stop=True)
                        mm.then_inc(summed[k], 1)
                    if coefficients:
                        pe.wait_ge(relt_copied, i + 1)
                        pe.wait_ge(coefs_made, i + 1)
                        for q in range(RQ // QT):
                            mm = nc.tensor.matmul(coef_ps[:, q * QT * BASES:(q + 1) * QT * BASES], relhot_t[:, q, :],
                                                  wcomp[:, :, :].rearrange("p q b -> p (q b)"), start=True, stop=True)
                        mm.then_inc(coef_ready, 1)

        @block.vector
        def _(dve):
            V = nc.vector
            dve.sem_inc(coefs_made, 1)
            for k in range(SETS):
                dve.sem_inc(summed[k], 1)
            for n in range(PER):
                dve.sem_inc(flushed[n], 1)
            V.memset(wcomp[:, :, :], 0.0).then_inc(cleared, 1)
            V.memset(acc[PER - 1][:, :], 0.0).then_inc(cleared, 1)
            for k in range(SETS):
                V.memset(rows[k][:, :, D:D + 1], 1.0).then_inc(cleared, 1)
            dve.wait_ge(cleared, 2 + SETS)
            dve.sem_inc(added, BANKS)

            def places(i, k):
                V.tensor_tensor(hot[k][:, :, :], coarse.target[:, ds(i * PER + k * SET, SET)].unsqueeze(2).to_broadcast([P, SET, P]),
                                iota[:, :].unsqueeze(1).to_broadcast([P, SET, P]), ALU.is_equal).then_inc(hot_ready, 1)

            def relations(i):
                V.tensor_tensor(relhot[:, :, :], relf[:, ds(i * RQ, RQ)].unsqueeze(2).to_broadcast([P, RQ, RELS]),
                                iota[:, 0:RELS].unsqueeze(1).to_broadcast([P, RQ, RELS]), ALU.is_equal).then_inc(relhot_ready, 1)

            def step(i, more, coefficients, more_coefficients):
                for k in range(SETS):
                    for u in range(SET):
                        n = k * SET + u
                        if u == 0:
                            dve.wait_ge(summed[k], i + 2)
                        dve.wait_ge(flushed[n], i * 16 + 1)
                        dve.wait_ge(added, i * PER + n + BANKS)
                        V.scalar_tensor_tensor(acc[n][:, :], acc[(n - 1) % PER][:, :], coarse.keep[:, ds(i * PER + n, 1)],
                                               part[:, n % BANKS, 0:D + 1], ALU.mult, ALU.add).then_inc(added, 1)
                        if more and u == 0:
                            places(i + 1, k)
                if coefficients:
                    dve.wait_ge(coef_ready, i + 1)
                    V.tensor_tensor(coefs[:, ds(i * RQ, RQ), :], coef_ps[:, 0:RQ * BASES].rearrange("p (t b) -> p t b", b=BASES),
                                    norm[:, ds(i * RQ, RQ)].unsqueeze(2).to_broadcast([P, RQ, BASES]), ALU.mult).then_inc(coefs_made, 1)
                if more_coefficients:
                    relations(i + 1)

            for k in range(SETS):
                places(0, k)
            relations(0)
            with dve.Fori(0, RS - 1) as i:
                step(i, True, True, True)
            step(RS - 1, True, True, False)
            with dve.Fori(RS, STEPS - 1) as i:
                step(i, True, False, False)
            step(STEPS - 1, False, False, False)


def transpose_nodes(pe, ident, XN, xnt_ps, psum_free, xnt_ready, first=0, loads=None, normalised=None):
    for n, (t, c) in enumerate((t, c) for t in range(NT) for c in range(DC)):
        g, q = divmod(n, 4)
        if loads and c == 0 and t in loads[0]:
            pe.wait_ge(loads[1][loads[0].index(t)], 16)
        if normalised and c == 0:
            pe.wait_ge(normalised, t + 1)
        if q == 0 and g >= 2:
            pe.wait_ge(psum_free, first + g - 1)
        mm = pe.transpose(xnt_ps[:, g % 2, q * P:(q + 1) * P], XN[:, t, c * P:(c + 1) * P], ident[:, :])
        if q == 3 or n == NT * DC - 1:
            mm.then_inc(xnt_ready, 1)


def copy_transposed(act, XNT, xnt_ps, psum_free, xnt_ready, first=0):
    groups = -(-NT * DC // 4)
    for g in range(groups):
        act.wait_ge(xnt_ready, first + g + 1)
        tiles = min(4, NT * DC - 4 * g) // DC
        act.activation(XNT[:, :, g * 2 * P:(g * 2 + tiles) * P].rearrange("p c (t n) -> p t c n", n=P),
                       xnt_ps[:, g % 2, 0:tiles * DC * P].rearrange("p (t c n) -> p t c n", c=DC, n=P),
                       ACT.Copy).then_inc(psum_free, 1)


def first_update(nc, common, a, X, ident, agg_dram, grow, gpay, XNT, gpay_dram, table_dram, adst_dram, htab_dram):
    paused, var_ready, std_ready = common.paused, common.var_ready, common.std_ready
    with ExitStack() as ctx:
        sb = lambda name, shape, dt=F32: ctx.enter_context(nc.sbuf_tensor(name, shape, dt))
        pb = lambda name, shape, dt=F32: ctx.enter_context(nc.psum_tensor(name, shape, dt))
        sem = lambda name: ctx.enter_context(nc.semaphore(name))
        W, b = sb("W_gnn", [P, DC, D]), sb("b_gnn", [P, D])
        wgat = sb("wgat", [P, DC, HEADS * EXPERTS])
        att = sb("att", [P, 2, HEADS * EXPERTS])
        inv, some = sb("inv", [P, NT]), sb("some", [P, NT])
        agg, aggT = sb("agg", [P, NT, D + 1]), sb("agg_transposed", [P, DC, NPAD])
        thirds = [0, 8, 16, NT]
        agg_in = [sem(f"agg_in{n}") for n in range(3)]
        XN = sb("XN1", [P, NT, D])
        stats, aggr = sb("stats1", [P, NT, 6]), sb("aggr1", [P, NT, 2])
        var, root, tmp = sb("var1", [P, NT]), sb("root1", [P, NT]), sb("tmp1", [P, NT])
        htab, ha, adst = sb("htab", [P, NT, GW]), sb("ha", [P, NT, HEADS * EXPERTS]), sb("adst", [P, NT, HEADS])
        gidx = [sb(f"gidx{k}", [P, GSTAGE], I32) for k in range(2)]
        grec = [sb(f"grec{k}", [P, GSTAGE, 2]) for k in range(2)]
        upd = [pb(f"upd{k}", [P, 512]) for k in range(2)]
        xnt_ps = pb("xnt_ps", [P, 2, 512])
        h_ps = pb("h_ps", [P, 512])
        w_in, updated, upd_used = (sem(n) for n in ("w_in", "updated", "upd_used"))
        xn_ready = sem("xn_ready1")
        psum_free, xnt_ready, h_ready, tables_ready, out_done = (
            sem(n) for n in ("psum_free", "xnt_ready", "h_ready", "tables_ready", "out_done"))
        staged = [sem("gstaged_a"), sem("gstaged_b")]
        scattered = [sem("gscattered0"), sem("gscattered1")]
        block = ctx.enter_context(nc.Block())
        GROUPS = -(-NT * DC // 4)

        @block.sync
        def _(sp):
            for n in range(3):
                tiles = slice(thirds[n], thirds[n + 1])
                sp.dma_start(agg[:, tiles, :], agg_dram[tiles].rearrange("t p d -> p t d")).then_inc(agg_in[n], 16)
            sp.dma_start(W[:, :, :], a["L0_gnn_weight"].rearrange("(c p) d -> p c d", p=P)).then_inc(w_in, 16)
            sp.dma_start(b[:, :], a["L0_gnn_bias"].partition_broadcast(P)).then_inc(w_in, 16)
            sp.dma_start(wgat[:, :, :], a["L0_ffn_W_gat"].rearrange("(c p) d -> p c d", p=P)).then_inc(w_in, 16)
            for n, name in enumerate(("L0_ffn_att_src", "L0_ffn_att_dst")):
                sp.dma_start(att[:, n, :], a[name].rearrange("h e -> (h e)").partition_broadcast(P)).then_inc(w_in, 16)
            first = sum(GSPLIT[0:2]) * 2 * GSTAGE

            def stage(i, k):
                cols = ds(i * (2 * GSTAGE) + (first + k * GSTAGE), GSTAGE)
                sp.dma_start(grec[k][:, :, :], gpay[:, cols, :]).then_inc(staged[k], 16)
                sp.dma_start(gidx[k][:, :], grow[:, cols]).then_inc(staged[k], 16)

            for k in range(2):
                stage(0, k)
            with sp.Fori(1, GSPLIT[2]) as i:
                for k in range(2):
                    sp.wait_ge(scattered[k], i * (16 * GSTAGE))
                    stage(i, k)

        @block.gpsimd
        def _(pool):
            with pool.Fori(0, GSPLIT[2]) as i:
                for k in range(2):
                    pool.wait_ge(staged[k], (i + 1) * 32)
                    pool.sem_inc(paused, 1)
                    for t in range(GSTAGE):
                        pool.indirect_dma_start(gpay_dram, bass.IndirectOffsetOnAxis(ap=gidx[k][:, t:t + 1].bitcast(U32), axis=0),
                                                grec[k][:, t, :], None).then_inc(scattered[k], 16)
            for k in range(2):
                pool.wait_ge(scattered[k], 16 * GSTAGE * GSPLIT[2])

        @block.scalar
        def _(act):
            copy_transposed(nc.scalar, aggT, xnt_ps, psum_free, xnt_ready)
            act.wait_ge(var_ready, 2)
            nc.scalar.activation(root[:, :], var[:, :], ACT.Sqrt).then_inc(std_ready, 1)
            copy_transposed(nc.scalar, XNT, xnt_ps, psum_free, xnt_ready, first=GROUPS)
            act.wait_ge(tables_ready, 1)
            act.dma_start(table_dram.rearrange("(t p) w -> p t w", p=P), htab[:, :, :]).then_inc(out_done, 16)
            act.dma_start(htab_dram, htab[:, :, :]).then_inc(out_done, 16)
            act.dma_start(adst_dram, adst[:, :, :]).then_inc(out_done, 16)
            act.wait_ge(out_done, 48)

        @block.tensor
        def _(pe):
            transpose_nodes(nc.tensor, ident, agg, xnt_ps, psum_free, xnt_ready, loads=(thirds, agg_in))
            pe.wait_ge(w_in, 80)
            for t in range(NT):
                pe.wait_ge(psum_free, t // 2 + 1)
                if t >= 2:
                    pe.wait_ge(upd_used, t - 1)
                for c in range(DC):
                    mm = nc.tensor.matmul(upd[t % 2][:, 0:D], aggT[:, c, t * P:(t + 1) * P], W[:, c, :], start=(c == 0), stop=(c == DC - 1))
                mm.then_inc(updated, 1)
            pe.wait_ge(xn_ready, NT)
            transpose_nodes(nc.tensor, ident, XN, xnt_ps, psum_free, xnt_ready, first=GROUPS)
            pe.wait_ge(psum_free, 2 * GROUPS)
            for t in range(NT):
                for c in range(DC):
                    mm = nc.tensor.matmul(h_ps[:, t * 16:(t + 1) * 16], XNT[:, c, t * P:(t + 1) * P], wgat[:, c, :],
                                          start=(c == 0), stop=(c == DC - 1))
            mm.then_inc(h_ready, 1)

        @block.vector
        def _(dve):
            link = common.link.on(dve)
            for n in range(3):
                dve.wait_ge(agg_in[n], 16)
            link.note(nc.vector.tensor_scalar(some[:, :], agg[:, :, D], 1.0, None, ALU.min))
            link(nc.vector.tensor_scalar(inv[:, :], agg[:, :, D], 1.0, None, ALU.max))
            link(nc.vector.reciprocal(inv[:, :], inv[:, :]))
            dve.wait_ge(w_in, 80)
            for t in range(NT):
                link.note(nc.vector.scalar_tensor_tensor(X[:, t, :], b[:, :], some[:, t:t + 1], X[:, t, :], ALU.mult, ALU.add))
            link.wait()
            for t in range(NT):
                dve.wait_ge(updated, t + 1)
                nc.vector.scalar_tensor_tensor(X[:, t, :], upd[t % 2][:, 0:D], inv[:, t:t + 1], X[:, t, :],
                                               ALU.mult, ALU.add).then_inc(upd_used, 1)
                dve.wait_ge(upd_used, t + 1)
                measure(dve, link, X, stats, aggr, t)
            normalise(dve, link, X, XN, stats, aggr, var[:, :], root[:, :], tmp[:, :], var_ready, std_ready, 2, xn_ready, measured=True)
            dve.wait_ge(h_ready, 1)
            hv = h_ps[:, 0:NT * 16].rearrange("p (t k) -> p t k", k=16)
            link.note(nc.vector.tensor_copy(htab[:, :, 0:16], hv))
            for n, to in ((0, htab[:, :, 16:20]), (1, adst[:, :, :])):
                link(nc.vector.tensor_tensor(ha[:, :, :], hv, att[:, n, :].unsqueeze(1).to_broadcast([P, NT, 16]), ALU.mult))
                link(nc.vector.tensor_reduce(to, ha[:, :, :].rearrange("p t (h e) -> p t h e", e=EXPERTS), AX.X, ALU.add))
            dve.sem_inc(tables_ready, 1)


CT = 5
CHUNKS = NT // CT
HALF = CT * P // 2
FE = 2 * D
FC = FE // P
GSET = 7
GSETS = 2
AHEAD = 4
GSTEPS = GKT // (GSET * GSETS)
BIG = 1e30
assert NT % CT == 0 and GSTEPS == EXPERTS * CHUNKS


def attention_maxima(nc, common, a, iota, ident, grow, gpay, grecs, gall, tmax, XNT, gpay_dram, table_dram, y_dram):
    paused = common.paused
    with ExitStack() as ctx:
        sb = lambda name, shape, dt=F32: ctx.enter_context(nc.sbuf_tensor(name, shape, dt))
        pb = lambda name, shape, dt=F32: ctx.enter_context(nc.psum_tensor(name, shape, dt))
        sem = lambda name: ctx.enter_context(nc.semaphore(name))
        PER = GSET * GSETS
        M = GSET * HEADS
        W1 = [sb(f"W1_{j}", [P, DC, FE]) for j in range(2)]
        W2 = sb("W2", [P, EXPERTS, FC, D])
        b1 = sb("b1", [P, EXPERTS, FC])
        hid = sb("hid", [P, FC, 2 * HALF])
        ys = sb("ys", [P, CT, D])
        rows = [sb(f"grows{k}", [P, GSET, GW]) for k in range(GSETS)]
        idx = [sb(f"gix{k}", [P, GSET], I32) for k in range(GSETS)]
        hot = [sb(f"ghot{k}", [P, GSET, P], BF16) for k in range(GSETS)]
        pen = [sb(f"pen{k}", [P, GSET, P], BF16) for k in range(GSETS)]
        rest = sb("rest", [P, M])
        split = [sb(f"split{k}", [P, 3, 32], BF16) for k in range(GSETS)]
        splt = [sb(f"splt{k}", [96, P], BF16) for k in range(GSETS)]
        identb = sb("identb", [P, P], BF16)
        pick = sb("pick", [96, M, P], BF16)
        hot_ps = pb("hot_ps", [P, GSET, P], BF16)
        splt_ps = pb("splt_ps", [96, P], BF16)
        val_ps = pb("val_ps", [P, 2, HEADS, P])
        h_ps, y_ps = pb("h_ps2", [P, 2, 512]), pb("y_ps", [P, 2, 512])

        b_in = sem("b_in")
        w_in, clear, pick_ready = sem("w_in2"), sem("clear2"), sem("pick_ready")
        idx_ready = sem("gix_ready")
        gathered = [sem(f"ggathered{k}") for k in range(GSETS)]
        kept, hot_ready, hott_ready, pen_ready = (sem(n) for n in ("kept", "ghot_ready", "ghott_ready", "pen_ready"))
        split_ready, splt_ready, splt_copied = sem("split_ready"), sem("splt_ready"), sem("splt_copied")
        val_ready, val_used = sem("val_ready"), sem("val_used")
        h_ready, h_used, y_ready, y_used = (sem(n) for n in ("h_ready2", "h_used", "y_ready", "y_used"))
        stored, up_in = sem("y_stored"), [sem("up_in0"), sem("up_in1")]
        gscattered, grecs_in = sem("gscattered3"), sem("grecs_in")
        first_col = sum(GSPLIT[0:3]) * 2 * GSTAGE
        block = ctx.enter_context(nc.Block())

        @block.sync
        def _(sp):
            def load_up(i, j):
                sp.dma_start(W1[j][:, :, :], a["L0_ffn_W1"][ds(i % EXPERTS, 1)].rearrange("o (c p) f -> p (o c) f", p=P)
                             ).then_inc(up_in[j], 16)

            load_up(0, 0)
            for e in range(EXPERTS):
                sp.dma_start(b1[:, e, :], a["L0_ffn_b1"][e].rearrange("(c p) -> p c", p=P),
                             allow_slow_non_contiguous=True).then_inc(b_in, 16)
            for e in range(EXPERTS):
                sp.dma_start(W2[:, e, :, :], a["L0_ffn_W2"][e].rearrange("(c p) f -> p c f", p=P)).then_inc(w_in, 16)
            load_up(1, 1)
            with sp.Fori(0, GSTEPS // 2) as ii:
                for j in range(2):
                    i = ii * 2 + j
                    sp.wait_ge(h_ready, (i + 1) * (2 * FC))
                    load_up(i + 2, j)
                    sp.wait_ge(y_used, (i + 1) * CT + 2)
                    sp.dma_start(y_dram[ds(i, 1)].rearrange("o p t d -> (o p) t d"), ys[:, :, :]).then_inc(stored, 16)
            for j in range(2):
                sp.wait_ge(up_in[j], 16 * (GSTEPS // 2 + 1))
            sp.wait_ge(stored, 16 * GSTEPS + 1)

        @block.gpsimd
        def _(pool):
            nc.gpsimd.memset(pick[:, :, :], 0.0).then_inc(pick_ready, 1)
            for j in range(3):
                pool.wait_ge(pick_ready, j + 1)
                view = pick[32 * j:32 * j + M, :, :]
                nc.gpsimd.affine_select(out=view, in_=view, compare_op=ALU.not_equal, fill=1.0, base=0,
                                        pattern=[[-1, M], [0, P]], channel_multiplier=1).then_inc(pick_ready, 1)
            pool.wait_ge(pick_ready, 4)
            for t in range(first_col, GT):
                pool.indirect_dma_start(gpay_dram, bass.IndirectOffsetOnAxis(ap=grow[:, t:t + 1].bitcast(U32), axis=0),
                                        gpay[:, t, :], None).then_inc(gscattered, 16)
            pool.wait_ge(gscattered, 16 * (GT - first_col))
            pool.dma_start(grecs[:, 0:GKT, :], gpay_dram.rearrange("(p k) w -> p k w", p=P)).then_inc(grecs_in, 16)
            with pool.Fori(0, GSTEPS // 2) as ii:
                for j in range(2):
                    i = ii * 2 + j
                    for k in range(GSETS):
                        pool.wait_ge(idx_ready, i * GSETS + k + 1)
                        pool.sem_inc(paused, 1)
                        pool.wait_ge(split_ready, i * GSETS + k + 1)
                        pool.sem_inc(paused, 1)
                        for u in range(GSET):
                            pool.indirect_dma_start(rows[k][:, u, :], None, table_dram,
                                                    bass.IndirectOffsetOnAxis(ap=idx[k][:, u:u + 1].bitcast(U32), axis=0)
                                                    ).then_inc(gathered[k], 16)

        UNITS = EXPERTS * CHUNKS
        LOOPED = (UNITS - AHEAD) // 2 - 1

        def run(engine, step):
            with engine.Fori(0, LOOPED) as ii:
                for j in range(2):
                    step(ii * 2 + j, ii, j, True, True, True)
            for i in range(2 * LOOPED, GSTEPS):
                step(i, i // 2, i % 2, i + AHEAD < UNITS, i + AHEAD + 1 < UNITS, i + 1 < GSTEPS)

        @block.scalar
        def _(act):
            def stage(i, k):
                nc.scalar.activation(idx[k][:, :].unsqueeze(2), grecs[:, ds(i * PER + k * GSET, GSET), 0:1].bitcast(I32),
                                     ACT.Copy).then_inc(idx_ready, 1)

            def keep_rows(i, k):
                act.wait_ge(gathered[k], (i + 1) * (16 * GSET))
                act.sem_inc(paused, 1)
                nc.scalar.activation(gall[:, ds(i * PER + k * GSET, GSET), :], rows[k][:, :, :], ACT.Copy).then_inc(kept, 1)
                act.wait_ge(kept, i * GSETS + k + 1)
                stage(i + 1, k)

            def turned(i, k, first=False):
                act.wait_ge(hott_ready, i * GSETS + k + 2)
                if not first:
                    act.wait_ge(val_ready, (i * GSETS + k - 1) * GSET + 1)
                nc.scalar.activation(pen[k][:, :, :], hot_ps[:, :, :], ACT.Copy, bias=-BIG, scale=BIG).then_inc(pen_ready, 1)
                act.wait_ge(splt_ready, i * GSETS + k + 2)
                nc.scalar.activation(splt[k][:, :], splt_ps[:, :], ACT.Copy).then_inc(splt_copied, 1)

            def hidden(m, n):
                half, f = divmod(n, FC)
                act.wait_ge(h_ready, m * (2 * FC) + n + 1)
                if n == 0:
                    act.wait_ge(y_ready, m * CT + 1)
                if not isinstance(m, int):
                    act.sem_inc(paused, 1)
                nc.scalar.activation(hid[:, f, half * HALF:(half + 1) * HALF], h_ps[:, n % 2, 0:HALF], ACT.Gelu,
                                     bias=b1[:, ds(m % EXPERTS, 1), f:f + 1].rearrange("p a b -> p (a b)")
                                     ).then_inc(h_used, 1)

            def rows_out(i, t):
                act.wait_ge(y_ready, i * CT + t + 2)
                nc.scalar.activation(ys[:, t, :], y_ps[:, t % 2, 0:D], ACT.Copy).then_inc(y_used, 1)

            def step(i, ii, j, second, first, following):
                m = i + AHEAD
                keep_rows(i, 1)
                if second:
                    act.wait_ge(stored, m * 16 + 1)
                    for t in range(3):
                        rows_out(m, t)
                turned(i, 1)
                if second:
                    for t in range(3, CT):
                        rows_out(m, t)
                if first:
                    for n in range(2):
                        hidden(m + 1, n)
                if following:
                    keep_rows(i + 1, 0)
                if first:
                    for n in range(2, 5):
                        hidden(m + 1, n)
                if following:
                    turned(i + 1, 0)
                if first:
                    for n in range(5, 2 * FC):
                        hidden(m + 1, n)

            act.wait_ge(b_in, 16 * EXPERTS)
            for m in range(AHEAD + 1):
                for n in range(2 * FC):
                    hidden(m, n)
                if m < AHEAD:
                    act.wait_ge(stored, m * 16 + 1)
                    for t in range(CT):
                        rows_out(m, t)
            act.wait_ge(grecs_in, 16)
            act.wait_ge(clear, 2)
            for k in range(GSETS):
                stage(0, k)
            keep_rows(0, 0)
            turned(0, 0, first=True)
            run(act, step)

        @block.tensor
        def _(pe):
            pe.sem_inc(h_used, 2)
            pe.sem_inc(y_used, 2)

            def transposes(i, k):
                pe.wait_ge(hot_ready, i * GSETS + k + 1)
                pe.wait_ge(pen_ready, i * GSETS + k + 1)
                for u in range(GSET):
                    mm = nc.tensor.transpose(hot_ps[:, u, :], hot[k][:, u, :], identb[:, :])
                mm.then_inc(hott_ready, 1)
                pe.wait_ge(split_ready, (i + 1) * GSETS + k + 1)
                pe.wait_ge(splt_copied, i * GSETS + k + 1)
                nc.tensor.transpose(splt_ps[:, :], split[k][:, :, :].rearrange("p j m -> p (j m)"), identb[:, :]).then_inc(splt_ready, 1)

            def values(i, s):
                k, u = divmod(s, GSET)
                if u == 0:
                    pe.wait_ge(pen_ready, i * GSETS + k + 2)
                    pe.wait_ge(splt_copied, i * GSETS + k + 2)
                pe.wait_ge(val_used, i * PER + s + 1)
                nc.tensor.matmul(val_ps[:, s % 2, :, :], identb[:, :],
                                 pen[k][:, u, :].unsqueeze(1).to_broadcast([P, HEADS, P]), start=True, stop=False)
                for h in range(HEADS):
                    mm = nc.tensor.matmul(val_ps[:, s % 2, h, :], pick[:, u * HEADS + h, :], splt[k][:, :],
                                          start=False, stop=(h == HEADS - 1))
                mm.then_inc(val_ready, 1)

            def first_layer(m, W, n):
                half, f = divmod(n, FC)
                pe.wait_ge(h_used, m * (2 * FC) + n + 1)
                for c in range(DC):
                    mm = nc.tensor.matmul(h_ps[:, n % 2, 0:HALF], W[:, c, f * P:(f + 1) * P],
                                          XNT[:, c, ds((m // EXPERTS) * (2 * HALF) + half * HALF, HALF)],
                                          start=(c == 0), stop=(c == DC - 1))
                mm.then_inc(h_ready, 1)

            def second_layer(i, t):
                if t == 0:
                    pe.wait_ge(h_used, i * (2 * FC) + 2 * FC + 2)
                pe.wait_ge(y_used, i * CT + t + 1)
                for f in range(FC):
                    mm = nc.tensor.matmul(y_ps[:, t % 2, 0:D], hid[:, f, t * P:(t + 1) * P],
                                          W2[:, ds(i % EXPERTS, 1), f, :].rearrange("p o d -> p (o d)"), start=(f == 0), stop=(f == FC - 1))
                mm.then_inc(y_ready, 1)

            def step(i, ii, j, second, first, following):
                m = i + AHEAD
                for s in range(PER):
                    if s == 3:
                        transposes(i, 1)
                    if s == 10 and following:
                        transposes(i + 1, 0)
                    values(i, s)
                    if s < CT and second:
                        second_layer(m, s)
                    elif CT <= s < CT + 2 * FC and first:
                        if s == CT:
                            pe.wait_ge(up_in[1 - j], (ii + (AHEAD // 2 + 1 + j)) * 16)
                        first_layer(m + 1, W1[1 - j], s - CT)

            for m in range(AHEAD + 1):
                pe.wait_ge(up_in[m % 2], (m // 2 + 1) * 16)
                for n in range(2 * FC):
                    first_layer(m, W1[m % 2], n)
                if m == 0:
                    pe.wait_ge(w_in, 16 * EXPERTS)
                if m < AHEAD:
                    for t in range(CT):
                        second_layer(m, t)
            pe.wait_ge(pick_ready, 4)
            pe.wait_ge(clear, 2)
            transposes(0, 0)
            run(pe, step)

        @block.vector
        def _(dve):
            link = common.link.on(dve)
            for one in (hott_ready, val_ready, y_ready, pen_ready, splt_copied, splt_ready, stored):
                dve.sem_inc(one, 1)
            nc.vector.memset(grecs[:, GKT:GKT + PER, :], 0.0).then_inc(clear, 1)
            nc.vector.tensor_copy(identb[:, :], ident[:, :]).then_inc(clear, 1)
            for k in range(GSETS):
                link(nc.vector.memset(split[k][:, :, :], 0.0))
            link(nc.vector.memset(tmax[:, :, GKT:GKT + 2], -BIG))
            dve.sem_inc(val_used, 2)
            dve.sem_inc(split_ready, GSETS)
            dve.wait_ge(grecs_in, 16)

            def prepare(i, k, first=False):
                if not first:
                    dve.wait_ge(hott_ready, i * GSETS + k)
                nc.vector.tensor_tensor(hot[k][:, :, :], grecs[:, ds(i * PER + k * GSET, GSET), 1:2].to_broadcast([P, GSET, P]),
                                        iota[:, :].unsqueeze(1).to_broadcast([P, GSET, P]), ALU.is_equal).then_inc(hot_ready, 1)
                dve.wait_ge(gathered[k], (i + 1) * (16 * GSET))
                if not first:
                    dve.wait_ge(splt_ready, i * GSETS + k)
                value = rows[k][:, :, 16:20]
                part = lambda q: split[k][:, q, 0:M].rearrange("p (u h) -> p u h", h=HEADS)
                left = rest[:, :].rearrange("p (u h) -> p u h", h=HEADS)
                link(nc.vector.tensor_copy(part(0), value))
                link(nc.vector.tensor_tensor(left, value, part(0), ALU.subtract))
                link(nc.vector.tensor_copy(part(1), left))
                link(nc.vector.tensor_tensor(left, left, part(1), ALU.subtract))
                nc.vector.tensor_copy(part(2), left).then_inc(split_ready, 1)

            def step(i, ii, j, second, first, following):
                if j == 0 and not isinstance(i, int):
                    link.enter(ii, 2 * 4 * GSETS)
                for s in range(PER):
                    if s == 1:
                        prepare(i, 1)
                    if s == 8 and following:
                        prepare(i + 1, 0)
                    dve.wait_ge(val_ready, i * PER + s + 2)
                    nc.vector.tensor_reduce(tmax[:, :, ds(i * PER + s, 1)].rearrange("p h o -> p (h o)"),
                                            val_ps[:, s % 2, :, :], AX.X, ALU.max).then_inc(val_used, 1)
                if j == 1 and not isinstance(i, int):
                    link.leave(LOOPED)

            prepare(0, 0, first=True)
            run(dve, step)


def block_ends(nc, eng, copy, link, glast, to, values, first, count, step=5):
    with eng.Fori(0, count // step) as i:
        link.enter(i, step)
        _, ends = nc.values_load_multi_w_load_instructions(glast[0:1, ds(i * step + first, step)], engines=[eng.engine],
                                                           min_val=0, max_val=GKT)
        for u in range(step):
            link.note(copy(to[:, ds(i * step + first + u, 1), :].rearrange("p o c -> p c o"),
                           values[:, :, ds(ends[u], 1)]))
        link.leave(count // step)
    link.wait()


def second_update(nc, common, a, X, iota, ident, gslot, gkeep, glast, grecs, gall, tmax, adst_dram, htab_dram, y_dram, xn_dram):
    paused, var_ready, std_ready = common.paused, common.var_ready, common.std_ready
    with ExitStack() as ctx:
        sb = lambda name, shape, dt=F32: ctx.enter_context(nc.sbuf_tensor(name, shape, dt))
        pb = lambda name, shape, dt=F32: ctx.enter_context(nc.psum_tensor(name, shape, dt))
        sem = lambda name: ctx.enter_context(nc.semaphore(name))
        H, C16 = HEADS, HEADS * EXPERTS
        PER = GSET * GSETS
        adst, htab = sb("adst2", [P, NT, H]), sb("htab2", [P, NT, GW])
        reset = sb("reset", [P, GKT])
        own = sb("own", [P, NT, 2 * H])
        rest, own3 = sb("rest2", [P, NT, 2 * H]), sb("own3", [P, NT, 3, 2 * H], BF16)
        selfw = sb("selfw", [P, NT, H])
        identb = sb("identb2", [P, P], BF16)
        hotb = [sb(f"hotb{k}", [P, GSET, P], BF16) for k in range(GSETS)]
        hott = [sb(f"hott{k}", [P, GSET, P], BF16) for k in range(GSETS)]
        POOLED = 9
        ownq = sb("own_of_slots", [P, PER, 24], BF16)
        pool_staged, act_staged = sem("pool_staged"), sem("act_staged")
        look = sb("look", [P, GKT, 2 * H])
        weight = sb("weight", [P, GKT, H])
        hotf = [sb(f"hotf{k}", [P, GSET, P]) for k in range(GSETS)]
        assert GW * (GKT + 2) <= NT * D
        space = sb("sums_then_normalised", [P, NT * D])
        sums = space[:, 0:GW * (GKT + 2)].rearrange("p (c k) -> p c k", c=GW)
        XN = space[:, :].rearrange("p (t d) -> p t d", t=NT)
        acc = sb("acc", [P, NT, GW])
        sq, mean, var, root, tmp = (sb("sq", [P, NT, C16]), *(sb(f"{n}3", [P, NT]) for n in ("mean", "var", "root", "tmp")))
        bg = sb("bg", [P, 3, C16])
        den = sb("den", [P, NT, H])
        score, gate, rank = (sb(n, [P, NT, EXPERTS]) for n in ("score", "gate", "rank2"))
        cmp = sb("cmp", [P, NT, EXPERTS, EXPERTS])
        gatet, b2 = sb("gatet", [EXPERTS, NPAD]), sb("b2", [EXPERTS, D])
        yt = [sb(f"yt{k}", [P, EXPERTS, D]) for k in range(SET * SETS)]
        AHEAD_Y = len(yt)
        PE_EXPERTS = 2
        diag = [sb(f"diag{k}", [P, PE_EXPERTS, P]) for k in range(2)]
        diag_ready = sem("diag_ready")
        stats, aggr = sb("stats2", [P, NT, 6]), sb("aggr2", [P, NT, 2])
        hot_ps = pb("hot_ps2", [P, 2, 1024], BF16)
        look_ps = pb("look_ps", [P, 2, 512])
        gt_ps, b_ps = pb("gt_ps", [EXPERTS, 2, 512]), pb("b_ps", [P, 2, 512])

        w_in = sem("w_in3")
        hot_ready, hott_ready, hott_copied, look_ready, look_used = (
            sem(n) for n in ("hotb_ready", "hott_ready2", "hott_copied", "look_ready", "look_used"))
        hotf_ready, sum_ready, sum_used, own_ready, arg_ready, exp_done = (
            sem(n) for n in ("hotf_ready", "sum_ready", "sum_used", "own_ready", "arg_ready", "exp_done"))
        xn_ready, xn_out = sem("xn_ready3"), sem("xn_out3")
        gt_ready, gt_copied, b_ready, x_added = (
            sem(n) for n in ("gt_ready", "gt_copied", "b_ready", "x_added"))
        y_in, LEFT = common.flushed, KA // len(yt) * 16 + 1
        msg_ready = sem("msg_ready")
        SHARES = {"dve": (0, 10), "pool": (10, 10), "act": (20, NT - 20)}
        ends_asked, ends_pool, ends_act = (sem(n) for n in ("ends_asked", "ends_pool", "ends_act"))
        block = ctx.enter_context(nc.Block())
        GG = -(-NT // 4)

        @block.sync
        def _(sp):
            sp.dma_start(adst[:, :, :], adst_dram).then_inc(w_in, 16)
            sp.dma_start(htab[:, :, :], htab_dram).then_inc(w_in, 16)
            for n, name in enumerate(("L0_ffn_b_gat", "L0_ffn_ln_gamma", "L0_ffn_ln_beta")):
                sp.dma_start(bg[:, n, :], a[name].partition_broadcast(P)).then_inc(w_in, 16)
            sp.dma_start(b2[:, :], a["L0_ffn_b2"]).then_inc(w_in, 16)
            for t in range(NT):
                if t >= AHEAD_Y:
                    sp.wait_ge(x_added, t - AHEAD_Y + 1)
                chunk, tt = divmod(t, CT)
                sp.dma_start(yt[t % AHEAD_Y][:, :, :], y_dram[chunk * EXPERTS:(chunk + 1) * EXPERTS, :, tt, :]
                             .rearrange("e p d -> p e d")).then_inc(y_in[t % AHEAD_Y], 16)
            cuts = [0, 8, 16, 22, NT]
            for lo, hi in zip(cuts, cuts[1:]):
                sp.wait_ge(xn_ready, hi)
                sp.dma_start(xn_dram.rearrange("(t p) d -> p t d", p=P)[:, lo:hi, :], XN[:, lo:hi, :]).then_inc(xn_out, 16)
            sp.wait_ge(xn_out, 16 * (len(cuts) - 1))

        @block.gpsimd
        def _(pool):
            link = Link(ends_pool).on(pool)
            pool.wait_ge(ends_asked, 1)
            block_ends(nc, pool, nc.gpsimd.tensor_copy, link, glast, den, tmax, *SHARES["pool"])
            pool.wait_ge(own_ready, 1)
            with pool.Fori(0, GSTEPS) as i:
                _, blocks = nc.values_load_multi_w_load_instructions(gslot[0:1, ds(i * PER, POOLED)], engines=[pool.engine],
                                                                     min_val=0, max_val=NT - 1)
                pool.wait_ge(look_ready, i * GSETS + 1)
                pool.sem_inc(paused, 1)
                for n in range(POOLED):
                    nc.gpsimd.tensor_copy(ownq[:, n, :], own3[:, ds(blocks[n], 1), :, :].rearrange("p o j c -> p (o j c)")
                                          ).then_inc(pool_staged, 1)
            pool.wait_ge(ends_asked, 2)
            block_ends(nc, pool, nc.gpsimd.tensor_copy, link, glast, acc, sums, *SHARES["pool"])

        @block.scalar
        def _(act):
            link = Link(ends_act).on(act)
            copy = lambda to, values: nc.scalar.activation(to, values, ACT.Copy)
            act.wait_ge(ends_asked, 1)
            block_ends(nc, act, copy, link, glast, den, tmax, *SHARES["act"])
            act.wait_ge(own_ready, 1)
            with act.Fori(0, GSTEPS) as i:
                _, blocks = nc.values_load_multi_w_load_instructions(gslot[0:1, ds(i * PER + POOLED, PER - POOLED)],
                                                                     engines=[act.engine], min_val=0, max_val=NT - 1)
                act.wait_ge(look_ready, i * GSETS + 1)
                act.sem_inc(paused, 1)
                for n in range(PER - POOLED):
                    nc.scalar.activation(ownq[:, POOLED + n, :], own3[:, ds(blocks[n], 1), :, :].rearrange("p o j c -> p (o j c)"),
                                         ACT.Copy).then_inc(act_staged, 1)
                for k in range(GSETS):
                    act.wait_ge(hott_ready, i * GSETS + k + 2)
                    nc.scalar.activation(hott[k][:, :, :].rearrange("p u d -> p (u d)"), hot_ps[:, k, 0:GSET * P],
                                         ACT.Copy).then_inc(hott_copied, 1)
            act.wait_ge(arg_ready, 1)
            nc.scalar.activation(weight[:, :, :], weight[:, :, :], ACT.Exp).then_inc(exp_done, 1)
            nc.scalar.activation(selfw[:, :, :], selfw[:, :, :], ACT.Exp).then_inc(exp_done, 1)
            with act.Fori(0, GSTEPS) as i:
                for k in range(GSETS):
                    act.wait_ge(sum_ready, i * GSETS + k + 2)
                    act.sem_inc(paused, 1)
                    nc.scalar.activation(sums[:, :, ds(i * PER + k * GSET, GSET)].rearrange("p c u -> p u c"),
                                         look_ps[:, k, 0:GSET * GW].rearrange("p (u c) -> p u c", c=GW), ACT.Copy).then_inc(sum_used, 1)
            act.wait_ge(ends_asked, 2)
            block_ends(nc, act, copy, link, glast, acc, sums, *SHARES["act"])
            act.wait_ge(var_ready, 3)
            nc.scalar.activation(root[:, :], var[:, :], ACT.Sqrt).then_inc(std_ready, 1)
            act.wait_ge(arg_ready, 2)
            nc.scalar.activation(gate[:, :, :], gate[:, :, :], ACT.Exp).then_inc(exp_done, 1)
            for g in range(GG):
                act.wait_ge(gt_ready, g + 1)
                n = min(4, NT - 4 * g) * P
                nc.scalar.activation(gatet[:, g * 4 * P:g * 4 * P + n], gt_ps[:, g % 2, 0:n], ACT.Copy).then_inc(gt_copied, 1)
            act.wait_ge(arg_ready, 3)
            for t in range(NT):
                if t >= 2:
                    act.wait_ge(b_ready, t - 1)
                for e in range(PE_EXPERTS):
                    nc.scalar.activation(diag[t % 2][:, e, :], ident[:, :], ACT.Copy, scale=gate[:, t, e:e + 1]).then_inc(diag_ready, 1)
            act.wait_ge(var_ready, 4)
            nc.scalar.activation(root[:, :], var[:, :], ACT.Sqrt).then_inc(std_ready, 1)

        @block.tensor
        def _(pe):
            pe.wait_ge(own_ready, 1)
            with pe.Fori(0, GSTEPS) as i:
                for k in range(GSETS):
                    pe.wait_ge(hot_ready, i * GSETS + k + 1)
                    pe.wait_ge(hott_copied, i * GSETS + 1)
                    for u in range(GSET):
                        mm = nc.tensor.transpose(hot_ps[:, k, u * P:(u + 1) * P], hotb[k][:, u, :], identb[:, :])
                    mm.then_inc(hott_ready, 1)
                for k in range(GSETS):
                    pe.wait_ge(hott_copied, i * GSETS + k + 2)
                    pe.wait_ge(look_used, i * GSETS + 1)
                    pe.wait_ge(pool_staged, (i + 1) * POOLED)
                    if k:
                        pe.wait_ge(act_staged, (i + 1) * (PER - POOLED))
                    for u in range(GSET):
                        mm = nc.tensor.matmul(look_ps[:, k, u * 24:(u + 1) * 24], hott[k][:, u, :],
                                              ownq[:, k * GSET + u, :],
                                              start=True, stop=True)
                    mm.then_inc(look_ready, 1)
            pe.wait_ge(msg_ready, 1)
            with pe.Fori(0, GSTEPS) as i:
                for k in range(GSETS):
                    pe.wait_ge(hotf_ready, i * GSETS + k + 1)
                    pe.wait_ge(sum_used, i * GSETS + k + 1)
                    for u in range(GSET):
                        mm = nc.tensor.matmul(look_ps[:, k, u * GW:(u + 1) * GW], hotf[k][:, u, :],
                                              gall[:, ds(i * PER + k * GSET + u, 1), :].rearrange("p o c -> p (o c)"),
                                              start=True, stop=True)
                    mm.then_inc(sum_ready, 1)
            pe.wait_ge(arg_ready, 3)
            for g in range(GG):
                if g >= 2:
                    pe.wait_ge(gt_copied, g - 1)
                for t in range(4 * g, min(4 * g + 4, NT)):
                    mm = nc.tensor.transpose(gt_ps[:, g % 2, (t % 4) * P:(t % 4 + 1) * P], gate[:, t, :], ident[:, :])
                mm.then_inc(gt_ready, 1)
            pe.wait_ge(gt_copied, GG)
            for t in range(NT):
                if t >= 2:
                    pe.wait_ge(x_added, t - 1)
                nc.tensor.matmul(b_ps[:, t % 2, 0:D], gatet[:, t * P:(t + 1) * P], b2[:, :], start=True, stop=False)
                pe.wait_ge(diag_ready, PE_EXPERTS * (t + 1))
                pe.wait_ge(y_in[t % AHEAD_Y], LEFT + 16 * (t // AHEAD_Y + 1))
                for e in range(PE_EXPERTS):
                    mm = nc.tensor.matmul(b_ps[:, t % 2, 0:D], diag[t % 2][:, e, :], yt[t % AHEAD_Y][:, e, :], start=False, stop=(e == PE_EXPERTS - 1))
                mm.then_inc(b_ready, 1)

        @block.vector
        def _(dve):
            link = common.link.on(dve)
            dve.sem_inc(hott_ready, 1)
            dve.sem_inc(look_ready, 1)
            dve.sem_inc(hott_copied, 1)
            dve.sem_inc(look_used, 1)
            dve.sem_inc(sum_ready, 1)
            dve.sem_inc(sum_used, 2)
            V = nc.vector

            def leaky(x):
                link(V.scalar_tensor_tensor(x, x, 0.2, x, ALU.mult, ALU.max))

            link.note(V.tensor_copy(identb[:, :], ident[:, :]))
            link.note(V.memset(sums[:, :, GKT:GKT + 2], 0.0))
            link(V.tensor_scalar(reset[:, :], gkeep[:, :], -1.0, BIG, ALU.add, ALU.mult))
            for h in range(H):
                link.note(V.tensor_tensor_scan(tmax[:, h, 0:GKT], reset[:, :], tmax[:, h, 0:GKT], -BIG, ALU.add, ALU.max))
            link.wait()
            dve.sem_inc(ends_asked, 1)
            block_ends(nc, dve, V.tensor_copy, link, glast, den, tmax, *SHARES["dve"])
            dve.wait_ge(ends_pool, SHARES["pool"][1])
            dve.wait_ge(ends_act, SHARES["act"][1])
            dve.wait_ge(w_in, 96)
            asrc, hown = htab[:, :, 16:20], htab[:, :, 0:16]
            link(V.tensor_tensor(den[:, :, :], den[:, :, :], asrc, ALU.max))
            link(V.tensor_tensor(own[:, :, H:2 * H], den[:, :, :], adst[:, :, :], ALU.add))
            leaky(own[:, :, H:2 * H])
            link(V.tensor_copy(own[:, :, 0:H], adst[:, :, :]))
            link(V.tensor_tensor(selfw[:, :, :], asrc, adst[:, :, :], ALU.add))
            leaky(selfw[:, :, :])
            link(V.tensor_tensor(selfw[:, :, :], selfw[:, :, :], own[:, :, H:2 * H], ALU.subtract))
            link(V.tensor_copy(own3[:, :, 0, :], own[:, :, :]))
            link(V.tensor_tensor(rest[:, :, :], own[:, :, :], own3[:, :, 0, :], ALU.subtract))
            link(V.tensor_copy(own3[:, :, 1, :], rest[:, :, :]))
            link(V.tensor_tensor(rest[:, :, :], rest[:, :, :], own3[:, :, 1, :], ALU.subtract))
            link(V.tensor_copy(own3[:, :, 2, :], rest[:, :, :]))
            dve.sem_inc(own_ready, 1)
            def targets(i, k, to, ready):
                V.tensor_tensor(to[k][:, :, :], grecs[:, ds(i * PER + k * GSET, GSET), 1:2].to_broadcast([P, GSET, P]),
                                iota[:, :].unsqueeze(1).to_broadcast([P, GSET, P]), ALU.is_equal).then_inc(ready, 1)

            for k in range(GSETS):
                targets(0, k, hotb, hot_ready)
            with dve.Fori(0, GSTEPS) as i:
                for k in range(GSETS):
                    dve.wait_ge(hott_ready, i * GSETS + k + 2)
                    targets(i + 1, k, hotb, hot_ready)
                for k in range(GSETS):
                    dve.wait_ge(look_ready, i * GSETS + k + 2)
                    V.tensor_reduce(look[:, ds(i * PER + k * GSET, GSET), :],
                                    look_ps[:, k, 0:GSET * 24].rearrange("p (u j c) -> p u c j", j=3, c=2 * H),
                                    AX.X, ALU.add).then_inc(look_used, 1)
            for k in range(GSETS):
                targets(0, k, hotf, hotf_ready)
            dve.wait_ge(look_used, GSTEPS * GSETS + 1)
            link(V.tensor_tensor(weight[:, :, :], gall[:, :, 16:20], look[:, :, 0:H], ALU.add))
            leaky(weight[:, :, :])
            link(V.tensor_tensor(weight[:, :, :], weight[:, :, :], look[:, :, H:2 * H], ALU.subtract))
            link(V.tensor_scalar(weight[:, :, :], weight[:, :, :], 0.0, None, ALU.min))
            dve.sem_inc(arg_ready, 1)
            dve.wait_ge(exp_done, 2)
            g4 = gall[:, :, 0:16].rearrange("p k (h e) -> p k h e", e=EXPERTS)
            for h in range(H):
                link.note(V.tensor_tensor(gall[:, :, h * EXPERTS:(h + 1) * EXPERTS], gall[:, :, h * EXPERTS:(h + 1) * EXPERTS],
                                          weight[:, :, h:h + 1].to_broadcast([P, GKT, EXPERTS]), ALU.mult))
            link.note(V.tensor_copy(gall[:, :, 16:20], weight[:, :, :]))
            link.wait()
            dve.sem_inc(msg_ready, 1)
            with dve.Fori(0, GSTEPS - 1) as i:
                for k in range(GSETS):
                    dve.wait_ge(sum_ready, i * GSETS + k + 2)
                    targets(i + 1, k, hotf, hotf_ready)
            dve.wait_ge(sum_used, GSTEPS * GSETS + 2)
            for c in range(GW):
                link.note(V.tensor_tensor_scan(sums[:, c, 0:GKT], gkeep[:, :], sums[:, c, 0:GKT], 0.0, ALU.mult, ALU.add))
            link.wait()
            dve.sem_inc(ends_asked, 1)
            block_ends(nc, dve, V.tensor_copy, link, glast, acc, sums, *SHARES["dve"])
            dve.wait_ge(ends_pool, 2 * SHARES["pool"][1])
            dve.wait_ge(ends_act, 2 * SHARES["act"][1])
            a3 = lambda x: x.rearrange("p t (h e) -> p t h e", e=EXPERTS)
            for h in range(H):
                part = slice(h * EXPERTS, (h + 1) * EXPERTS)
                link.note(V.tensor_tensor(sq[:, :, part], hown[:, :, part], selfw[:, :, h:h + 1].to_broadcast([P, NT, EXPERTS]), ALU.mult))
            link.wait()
            link(V.tensor_tensor(acc[:, :, 0:16], acc[:, :, 0:16], sq[:, :, :], ALU.add))
            link(V.tensor_tensor(den[:, :, :], acc[:, :, 16:20], selfw[:, :, :], ALU.add))
            link(V.tensor_scalar(den[:, :, :], den[:, :, :], 1e-16, None, ALU.add))
            link(V.reciprocal(den[:, :, :], den[:, :, :]))
            for h in range(H):
                part = slice(h * EXPERTS, (h + 1) * EXPERTS)
                link.note(V.tensor_tensor(acc[:, :, part], acc[:, :, part], den[:, :, h:h + 1].to_broadcast([P, NT, EXPERTS]), ALU.mult))
            link.wait()
            agg = acc[:, :, 0:16]
            spread = lambda n: bg[:, n, :].unsqueeze(1).to_broadcast([P, NT, C16])
            over = lambda x: x.unsqueeze(2).to_broadcast([P, NT, C16])
            link(V.tensor_tensor(agg, agg, spread(0), ALU.add))
            link(V.tensor_reduce(mean[:, :], agg, AX.X, ALU.add))
            link(V.tensor_scalar(mean[:, :], mean[:, :], 1.0 / C16, None, ALU.mult))
            link(V.tensor_tensor(agg, agg, over(mean[:, :]), ALU.subtract))
            link(V.tensor_tensor(sq[:, :, :], agg, agg, ALU.mult))
            link(V.tensor_reduce(var[:, :], sq[:, :, :], AX.X, ALU.add))
            link(V.tensor_scalar(var[:, :], var[:, :], 1.0 / C16, None, ALU.mult))
            inverse_root(dve, link, var[:, :], root[:, :], tmp[:, :], var_ready, std_ready, 3)
            link(V.tensor_tensor(agg, agg, over(root[:, :]), ALU.mult))
            link(V.tensor_tensor(agg, agg, spread(1), ALU.mult))
            link(V.tensor_tensor(agg, agg, spread(2), ALU.add))
            link(V.tensor_reduce(score[:, :, :], agg.rearrange("p t (h e) -> p t e h", e=EXPERTS), AX.X, ALU.add))
            link(V.tensor_scalar(score[:, :, :], score[:, :, :], 1.0 / H, None, ALU.mult))
            for o in range(EXPERTS):
                for lo, hi, before in ((0, o + 1, ALU.is_gt), (o + 1, EXPERTS, ALU.is_ge)):
                    if lo < hi:
                        link.note(V.tensor_tensor(cmp[:, :, lo:hi, o], score[:, :, o:o + 1].to_broadcast([P, NT, hi - lo]),
                                                  score[:, :, lo:hi], before))
            link.wait()
            link(V.tensor_reduce(rank[:, :, :], cmp[:, :, :, :], AX.X, ALU.add))
            link(V.tensor_scalar(rank[:, :, :], rank[:, :, :], 1.5, None, ALU.is_lt))
            link(V.tensor_reduce(tmp[:, :], score[:, :, :], AX.X, ALU.max))
            link(V.tensor_tensor(gate[:, :, :], score[:, :, :], tmp[:, :].unsqueeze(2).to_broadcast([P, NT, EXPERTS]), ALU.subtract))
            dve.sem_inc(arg_ready, 1)
            dve.wait_ge(exp_done, 3)
            link(V.tensor_tensor(gate[:, :, :], gate[:, :, :], rank[:, :, :], ALU.mult))
            link(V.tensor_reduce(tmp[:, :], gate[:, :, :], AX.X, ALU.add))
            link(V.reciprocal(tmp[:, :], tmp[:, :]))
            link(V.tensor_tensor(gate[:, :, :], gate[:, :, :], tmp[:, :].unsqueeze(2).to_broadcast([P, NT, EXPERTS]), ALU.mult))
            dve.sem_inc(arg_ready, 1)
            def from_dve(t, e):
                link.note(V.scalar_tensor_tensor(X[:, t, :], yt[t % AHEAD_Y][:, e, :], gate[:, t, e:e + 1], X[:, t, :], ALU.mult, ALU.add))

            for t0 in range(0, NT, 2):
                tiles = range(t0, min(t0 + 2, NT))
                for t in tiles:
                    dve.wait_ge(y_in[t % AHEAD_Y], LEFT + 16 * (t // AHEAD_Y + 1))
                    from_dve(t, PE_EXPERTS)
                link.wait()
                for e in range(PE_EXPERTS + 1, EXPERTS):
                    for t in tiles:
                        from_dve(t, e)
                    link.wait()
                for t in tiles:
                    dve.wait_ge(b_ready, t + 1)
                    V.tensor_tensor(X[:, t, :], X[:, t, :], b_ps[:, t % 2, 0:D], ALU.add).then_inc(x_added, 1)
                for t in tiles:
                    dve.wait_ge(x_added, t + 1)
                    measure(dve, link, X, stats, aggr, t)
            normalise(dve, link, X, XN, stats, aggr, var[:, :], root[:, :], tmp[:, :], var_ready, std_ready, 4, xn_ready, measured=True)


def sum_relations(nc, common, iota, fine, coefs, table, z_dram):
    paused = common.paused
    with ExitStack() as ctx:
        sb = lambda name, shape, dt=F32: ctx.enter_context(nc.sbuf_tensor(name, shape, dt))
        pb = lambda name, shape, dt=F32: ctx.enter_context(nc.psum_tensor(name, shape, dt))
        sem = lambda name: ctx.enter_context(nc.semaphore(name))
        PER = SET * SETS
        STEPS = KT // PER
        BW = BASES * WIN
        rows = [sb(f"rrows{k}", [P, SET, D]) for k in range(SETS)]
        idx = [sb(f"ridx{k}", [P, SET], I32) for k in range(SETS)]
        hot = [sb(f"rhot{k}", [P, SET, WIN]) for k in range(SETS)]
        coef = [sb(f"coef{k}", [P, SET, BASES, WIN]) for k in range(SETS)]
        acc = [sb(f"acc{n}", [P, DC * BW]) for n in range(PER)]
        zero = sb("zero", [P, DC * BW])
        part = pb("part5", [P, PER, 512])
        idx_ready, coef_ready, added = (
            sem(n) for n in ("ridx_ready", "coef_ready5", "added5"))
        gathered, summed, flushed = common.gathered, common.summed, common.flushed
        DONE = KA // PER
        GATHERED, SUMMED = DONE * (16 * SET), DONE + 1
        FLUSHED = [DONE * 16 + 1 + 16 * len(range(n, NT, PER)) for n in range(PER)]
        zero_ready, zero_out = sem("zero_ready"), sem("zero_out")
        block = ctx.enter_context(nc.Block())

        @block.sync
        def _(sp):
            sp.wait_ge(zero_ready, 1)
            for w in range(NW, NT * P // WIN):
                sp.dma_start(z_dram[w], zero[:, :]).then_inc(zero_out, 16)
            with sp.Fori(0, STEPS) as i:
                _, wins = nc.values_load_multi_w_load_instructions(fine.group[0:1, ds(i * PER, PER)], engines=[sp.engine],
                                                                   min_val=0, max_val=NW - 1)
                _, lasts = nc.values_load_multi_w_load_instructions(fine.last[0:1, ds(i * PER, PER)], engines=[sp.engine],
                                                                    min_val=0, max_val=1)
                for n in range(PER):
                    sp.wait_ge(added, (i + 1) * PER + n + 1)
                    sp.dma_start(z_dram[ds(wins[n], 1)].rearrange("o p w -> (o p) w"), acc[n][:, :],
                                 cond=lasts[n] > 0).then_inc(flushed[n], 16)
            sp.wait_ge(zero_out, 16 * (NT * P // WIN - NW))
            for n in range(PER):
                sp.wait_ge(flushed[n], FLUSHED[n] + 16 * STEPS)

        @block.scalar
        def _(act):
            with act.Fori(0, STEPS) as i:
                for k in range(SETS):
                    act.wait_ge(summed[k], i + SUMMED)
                    nc.scalar.activation(idx[k][:, :], fine.source[:, ds(i * PER + k * SET, SET)], ACT.Copy).then_inc(idx_ready, 1)

        @block.gpsimd
        def _(pool):
            with pool.Fori(0, STEPS) as i:
                for k in range(SETS):
                    pool.wait_ge(idx_ready, i * SETS + k + 1)
                    pool.sem_inc(paused, 1)
                    for u in range(SET):
                        pool.indirect_dma_start(rows[k][:, u, :], None, table,
                                                bass.IndirectOffsetOnAxis(ap=idx[k][:, u:u + 1].bitcast(U32), axis=0)
                                                ).then_inc(gathered[k], 16)

        @block.tensor
        def _(pe):
            with pe.Fori(0, STEPS) as i:
                for k in range(SETS):
                    pe.wait_ge(coef_ready, i * SETS + k + 1)
                    pe.wait_ge(added, i * PER + (k + 1) * SET)
                    pe.wait_ge(gathered[k], i * (16 * SET) + (GATHERED + 16 * SET))
                    for u in range(SET):
                        for c in range(DC):
                            mm = nc.tensor.matmul(part[:, k * SET + u, c * BW:(c + 1) * BW], rows[k][:, u, c * P:(c + 1) * P],
                                                  coef[k][:, u, :, :].rearrange("p b w -> p (b w)"), start=True, stop=True)
                    mm.then_inc(summed[k], 1)

        @block.vector
        def _(dve):
            link = common.link.on(dve)
            V = nc.vector
            V.memset(zero[:, :], 0.0).then_inc(zero_ready, 1)
            link(V.memset(acc[PER - 1][:, :], 0.0))

            def places(i, k):
                link.note(V.tensor_tensor(hot[k][:, :, :], fine.target[:, ds(i * PER + k * SET, SET)].unsqueeze(2).to_broadcast([P, SET, WIN]),
                                          iota[:, 0:WIN].unsqueeze(1).to_broadcast([P, SET, WIN]), ALU.is_equal))

            def weights(i, k):
                link.wait()
                V.tensor_tensor(coef[k][:, :, :, :], hot[k][:, :, :].unsqueeze(2).to_broadcast([P, SET, BASES, WIN]),
                                coefs[:, ds(i * PER + k * SET, SET), :].unsqueeze(3).to_broadcast([P, SET, BASES, WIN]),
                                ALU.mult).then_inc(coef_ready, 1)

            def step(i, more):
                for k in range(SETS):
                    dve.wait_ge(summed[k], i + (SUMMED + 1))
                    if more:
                        places(i + 1, k)
                    for u in range(SET):
                        n = k * SET + u
                        dve.wait_ge(flushed[n], i * 16 + FLUSHED[n])
                        dve.wait_ge(added, i * PER + n + PER)
                        V.scalar_tensor_tensor(acc[n][:, :], acc[(n - 1) % PER][:, :], fine.keep[:, ds(i * PER + n, 1)],
                                               part[:, n, :], ALU.mult, ALU.add).then_inc(added, 1)
                        if more and u == 0:
                            weights(i + 1, k)

            dve.sem_inc(added, PER)
            for k in range(SETS):
                places(0, k)
                weights(0, k)
            with dve.Fori(0, STEPS - 1) as i:
                link.enter(i, SETS)
                step(i, True)
                link.leave(STEPS - 1)
            step(STEPS - 1, False)


def third_update(nc, common, a, X, iota, ident, ones, z_dram, out):
    var_ready, std_ready = common.var_ready, common.std_ready
    with ExitStack() as ctx:
        sb = lambda name, shape, dt=F32: ctx.enter_context(nc.sbuf_tensor(name, shape, dt))
        pb = lambda name, shape, dt=F32: ctx.enter_context(nc.psum_tensor(name, shape, dt))
        sem = lambda name: ctx.enter_context(nc.semaphore(name))
        BW, WT = BASES * WIN, P // WIN
        E8, K2 = 8, 2
        CAPACITY = float(-(-N * 5 // (4 * E8)))
        bases = sb("bases", [P, BASES, DC, D])
        z = [sb(f"z{k}", [P, WT, DC * BW]) for k in range(2)]
        zn = [sb(f"zn{k}", [P, DC * BASES, WT, WIN]) for k in range(2)]
        assert N % NT == 0
        parts, total = sb("node_parts", [P, DC, NT]), sb("node_sum", [P, DC])
        XN, XNT = sb("XN6", [P, NT, D]), sb("XNT6", [P, DC, NPAD])
        stats, aggr = sb("stats6", [P, NT, 6]), sb("aggr6", [P, NT, 2])
        var, root, tmp = sb("var6", [P, NT]), sb("root6", [P, NT]), sb("tmp6", [P, NT])
        wr, br = sb("wr", [P, DC, E8]), sb("br", [P, E8])
        mean = sb("mean6", [P, DC, P])
        lg, r1, r2, top, sm = (sb(n, [P, E8]) for n in ("lg", "r1", "r2", "top", "sm"))
        larger, equal, earlier = (sb(n, [P, E8, E8]) for n in ("larger", "equal", "earlier"))
        which = sb("which", [P, K2], I32)
        wgt = sb("wgt", [P, K2])
        W1 = [sb(f"V1_{k}", [P, DC, FE]) for k in range(K2)]
        W2 = [sb(f"V2_{k}", [P, FC, D]) for k in range(K2)]
        b1, b2 = sb("b1_6", [P, K2, FC]), sb("b2_6", [P, K2, D])
        gam, bet, bias = sb("gam", [P, D]), sb("bet", [P, D]), sb("bias6", [P, D])
        hid = [sb(f"hid6_{k}", [P, FC, 2 * HALF]) for k in range(1)]
        z_ps = pb("z_ps", [P, 2, 512])
        xnt_ps = pb("xnt_ps6", [P, 2, 512])
        h_ps, y_ps = pb("h_ps6", [P, 2, 512]), pb("y_ps6", [P, 2, 512])
        w_in, e_in = sem("w_in6"), sem("experts_in")
        z_in = [sem("z_in0"), sem("z_in1")]
        z_ready, z_added, z_turned = sem("z_ready"), sem("z_added"), sem("z_turned")
        xn_ready = sem("xn_ready6")
        psum_free, xnt_ready = sem("psum_free6"), sem("xnt_ready6")
        mean_ready, mean_copied, logits_ready, arg_ready, exp_done, picked = (
            sem(n) for n in ("mean_ready", "mean_copied", "logits_ready", "arg_ready6", "exp_done6", "picked"))
        h_ready, h_used, y_ready, y_used = (sem(n) for n in ("h_ready6", "h_used6", "y_ready6", "y_used6"))
        out_ready, out_done = sem("out_ready"), sem("out_done6")
        block = ctx.enter_context(nc.Block())
        GROUPS = -(-NT * DC // 4)

        @block.sync
        def _(sp):
            sp.dma_start(bases[:, :, :, :], a["L1_gnn_bases"].rearrange("b (c p) d -> p b c d", p=P)).then_inc(w_in, 16)
            sp.dma_start(wr[:, :, :], a["L1_ffn_Wr"].rearrange("(c p) e -> p c e", p=P)).then_inc(w_in, 16)
            sp.dma_start(br[:, :], a["L1_ffn_br"].partition_broadcast(P)).then_inc(w_in, 16)
            sp.dma_start(gam[:, :], a["L1_ffn_gamma"].partition_broadcast(P)).then_inc(w_in, 16)
            sp.dma_start(bet[:, :], a["L1_ffn_beta"].partition_broadcast(P)).then_inc(w_in, 16)
            for t in range(NT):
                if t >= 2:
                    sp.wait_ge(z_turned, t - 1)
                sp.dma_start(z[t % 2][:, :, :], z_dram[t * WT:(t + 1) * WT].rearrange("w p x -> p w x")).then_inc(z_in[t % 2], 16)
            sp.wait_ge(picked, 1)
            _, chosen = nc.values_load_multi_w_load_instructions(which[0:1, :], engines=[sp.engine],
                                                                 min_val=0, max_val=E8 - 1, bass_reorder=False)
            for k in range(K2):
                e = ds(chosen[k], 1)
                sp.dma_start(W1[k][:, :, :], a["L1_ffn_W1"][e].rearrange("o (c p) f -> p (o c) f", p=P)).then_inc(e_in, 16)
                sp.dma_start(W2[k][:, :, :], a["L1_ffn_W2"][e].rearrange("o (c p) f -> p (o c) f", p=P)).then_inc(e_in, 16)
                sp.dma_start(b1[:, k, :], a["L1_ffn_b1"][e].rearrange("o (c p) -> p (o c)", p=P),
                             allow_slow_non_contiguous=True).then_inc(e_in, 16)
                sp.dma_start(b2[:, k, :], a["L1_ffn_b2"][e].rearrange("o d -> (o d)").partition_broadcast(P)).then_inc(e_in, 16)
            cuts = [0, 7, 14, 20, NFULL]
            for lo, hi in zip(cuts, cuts[1:]):
                sp.wait_ge(out_ready, hi)
                sp.dma_start(out[lo * P:hi * P, :].rearrange("(t p) d -> p t d", p=P), XN[:, lo:hi, :]).then_inc(out_done, 16)
            sp.wait_ge(out_ready, NT)
            sp.dma_start(out[NFULL * P:N, :], XN[0:NTAIL, NFULL, :]).then_inc(out_done, 16)
            sp.wait_ge(out_done, 16 * len(cuts))

        @block.scalar
        def _(act):
            for t in range(NT):
                act.wait_ge(z_in[t % 2], 16 * (t // 2 + 1))
                if t >= 2:
                    act.wait_ge(z_ready, t - 1)
                nc.scalar.activation(zn[t % 2][:, :, :, :], z[t % 2][:, :, :].rearrange("p w (k d) -> p k w d", d=WIN),
                                     ACT.Copy).then_inc(z_turned, 1)
            act.wait_ge(var_ready, 5)
            nc.scalar.activation(root[:, :], var[:, :], ACT.Sqrt).then_inc(std_ready, 1)
            copy_transposed(nc.scalar, XNT, xnt_ps, psum_free, xnt_ready)
            act.wait_ge(mean_ready, 1)
            for c in range(DC):
                nc.scalar.activation(mean[:, c, :], total[:, c:c + 1].to_broadcast([P, P]), ACT.Copy, scale=1.0 / N).then_inc(mean_copied, 1)
            for n in range(3):
                act.wait_ge(arg_ready, n + 1)
                x = sm[:, 0:1] if n == 2 else sm[:, :]
                nc.scalar.activation(x, x, ACT.Exp).then_inc(exp_done, 1)
            act.wait_ge(e_in, 16 * 4 * K2)
            for unit in range(CHUNKS * K2):
                for n in range(2 * FC):
                    half, f = divmod(n, FC)
                    act.wait_ge(h_ready, unit * 2 * FC + n + 1)
                    if n == 0 and unit:
                        act.wait_ge(y_ready, unit * CT)
                    nc.scalar.activation(hid[0][:, f, half * HALF:(half + 1) * HALF], h_ps[:, n % 2, 0:HALF], ACT.Gelu,
                                         bias=b1[:, unit % K2, f:f + 1]).then_inc(h_used, 1)
            act.wait_ge(var_ready, 6)
            nc.scalar.activation(root[:, :], var[:, :], ACT.Sqrt).then_inc(std_ready, 1)

        @block.tensor
        def _(pe):
            pe.wait_ge(w_in, 16 * 5)
            for t in range(NT):
                pe.wait_ge(z_turned, t + 1)
                if t >= 2:
                    pe.wait_ge(z_added, t - 1)
                for n, (c, b) in enumerate((c, b) for c in range(DC) for b in range(BASES)):
                    mm = nc.tensor.matmul(z_ps[:, t % 2, 0:D], zn[t % 2][:, c * BASES + b, :, :].rearrange("p w d -> p (w d)"), bases[:, b, c, :],
                                          start=(n == 0), stop=(n == DC * BASES - 1))
                mm.then_inc(z_ready, 1)
            transpose_nodes(nc.tensor, ident, XN, xnt_ps, psum_free, xnt_ready, normalised=xn_ready)
            pe.wait_ge(mean_copied, DC)
            for c in range(DC):
                mm = nc.tensor.matmul(y_ps[:, 0, 0:E8], mean[:, c, :], wr[:, c, :], start=(c == 0), stop=(c == DC - 1))
            mm.then_inc(logits_ready, 1)
            pe.wait_ge(psum_free, GROUPS)
            pe.wait_ge(e_in, 16 * 4 * K2)
            for unit in range(CHUNKS * K2):
                chunk, k = divmod(unit, K2)
                for n in range(2 * FC):
                    half, f = divmod(n, FC)
                    if unit * 2 * FC + n >= 2:
                        pe.wait_ge(h_used, unit * 2 * FC + n - 1)
                    lo = chunk * 2 * HALF + half * HALF
                    for c in range(DC):
                        mm = nc.tensor.matmul(h_ps[:, n % 2, 0:HALF], W1[k][:, c, f * P:(f + 1) * P], XNT[:, c, lo:lo + HALF],
                                              start=(c == 0), stop=(c == DC - 1))
                    mm.then_inc(h_ready, 1)
                pe.wait_ge(h_used, (unit + 1) * 2 * FC)
                for t in range(CT):
                    if unit * CT + t >= 2:
                        pe.wait_ge(y_used, unit * CT + t - 1)
                    for f in range(FC):
                        mm = nc.tensor.matmul(y_ps[:, (unit * CT + t) % 2, 0:D], hid[0][:, f, t * P:(t + 1) * P], W2[k][:, f, :],
                                              start=(f == 0), stop=(f == FC - 1))
                    mm.then_inc(y_ready, 1)

        @block.vector
        def _(dve):
            link = common.link.on(dve)
            V = nc.vector
            for t in range(NT):
                dve.wait_ge(z_ready, t + 1)
                V.scalar_tensor_tensor(X[:, t, :], z_ps[:, t % 2, 0:D], 0.0, X[:, t, :], ALU.max, ALU.add).then_inc(z_added, 1)
                dve.wait_ge(z_added, t + 1)
                measure(dve, link, X, stats, aggr, t)
            normalise(dve, link, X, XN, stats, aggr, var[:, :], root[:, :], tmp[:, :], var_ready, std_ready, 5, xn_ready, measured=True)

            dve.wait_ge(psum_free, GROUPS)
            link(V.tensor_reduce(parts[:, :, :], XNT[:, :, 0:N].rearrange("p c (t n) -> p c t n", t=NT), AX.X, ALU.add))
            link(V.tensor_reduce(total[:, :], parts[:, :, :], AX.X, ALU.add))
            dve.sem_inc(mean_ready, 1)

            def softmax(x, n):
                link(V.tensor_reduce(tmp[:, 0:1], x, AX.X, ALU.max))
                link(V.tensor_scalar(sm[:, :], x, tmp[:, 0:1], None, ALU.subtract))
                dve.sem_inc(arg_ready, 1)
                dve.wait_ge(exp_done, n)
                link(V.tensor_reduce(tmp[:, 0:1], sm[:, :], AX.X, ALU.add))
                link(V.reciprocal(tmp[:, 0:1], tmp[:, 0:1]))
                link(V.tensor_scalar(x, sm[:, :], tmp[:, 0:1], None, ALU.mult))

            dve.wait_ge(logits_ready, 1)
            link(V.tensor_tensor(lg[:, :], y_ps[:, 0, 0:E8], br[:, :], ALU.add))
            softmax(lg[:, :], 1)
            link(V.tensor_scalar(r1[:, :], lg[:, :], float(N), None, ALU.mult))
            link(V.tensor_scalar(r2[:, :], r1[:, :], CAPACITY, None, ALU.max))
            link(V.reciprocal(r2[:, :], r2[:, :]))
            link(V.tensor_scalar(r2[:, :], r2[:, :], CAPACITY, None, ALU.mult))
            link(V.tensor_scalar(r1[:, :], r1[:, :], CAPACITY, None, ALU.is_gt))
            link(V.scalar_tensor_tensor(r2[:, :], r2[:, :], -1.0, r1[:, :], ALU.add, ALU.mult))
            link(V.tensor_scalar(r2[:, :], r2[:, :], 1.0, None, ALU.add))
            link(V.tensor_tensor(lg[:, :], lg[:, :], r2[:, :], ALU.mult))
            softmax(lg[:, :], 2)
            e_of = lambda x: x.unsqueeze(2).to_broadcast([P, E8, E8])
            o_of = lambda x: x.unsqueeze(1).to_broadcast([P, E8, E8])
            link.note(V.tensor_tensor(larger[:, :, :], o_of(lg[:, :]), e_of(lg[:, :]), ALU.is_gt))
            link.note(V.tensor_tensor(equal[:, :, :], o_of(lg[:, :]), e_of(lg[:, :]), ALU.is_equal))
            link(V.tensor_tensor(earlier[:, :, :], o_of(iota[:, 0:E8]), e_of(iota[:, 0:E8]), ALU.is_lt))
            link(V.tensor_tensor(equal[:, :, :], equal[:, :, :], earlier[:, :, :], ALU.mult))
            link(V.tensor_tensor(larger[:, :, :], larger[:, :, :], equal[:, :, :], ALU.add))
            link(V.tensor_reduce(r1[:, :], larger[:, :, :], AX.X, ALU.add))
            for k in range(K2):
                link(V.tensor_scalar(r2[:, :], r1[:, :], float(k), None, ALU.is_equal))
                link(V.tensor_tensor(sm[:, :], r2[:, :], iota[:, 0:E8], ALU.mult))
                link(V.tensor_reduce(tmp[:, 0:1], sm[:, :], AX.X, ALU.add))
                link(V.tensor_copy(which[:, k:k + 1], tmp[:, 0:1]))
                link(V.tensor_tensor(sm[:, :], r2[:, :], lg[:, :], ALU.mult))
                link(V.tensor_reduce(top[:, k:k + 1], sm[:, :], AX.X, ALU.add))
            dve.sem_inc(picked, 1)
            link(V.tensor_tensor(sm[:, 0:1], top[:, 1:2], top[:, 0:1], ALU.subtract))
            dve.sem_inc(arg_ready, 1)
            dve.wait_ge(exp_done, 3)
            link(V.tensor_scalar(tmp[:, 0:1], sm[:, 0:1], 1.0, None, ALU.add))
            link(V.reciprocal(wgt[:, 0:1], tmp[:, 0:1]))
            link(V.tensor_tensor(wgt[:, 1:2], wgt[:, 0:1], sm[:, 0:1], ALU.mult))
            for t in range(NT):
                link.note(V.tensor_tensor(X[:, t, :], X[:, t, :], bet[:, :], ALU.add))
            dve.wait_ge(e_in, 16 * 4 * K2)
            link(V.tensor_scalar(bias[:, :], b2[:, 0, :], wgt[:, 0:1], None, ALU.mult))
            link(V.scalar_tensor_tensor(bias[:, :], b2[:, 1, :], wgt[:, 1:2], bias[:, :], ALU.mult, ALU.add))
            for t in range(NT):
                link.note(V.tensor_tensor(XN[:, t, :], XN[:, t, :], bias[:, :], ALU.add))
            link.wait()
            for unit in range(CHUNKS * K2):
                chunk, k = divmod(unit, K2)
                for t in range(CT):
                    node = chunk * CT + t
                    if k:
                        dve.wait_ge(y_used, (unit - 1) * CT + t + 1)
                    dve.wait_ge(y_ready, unit * CT + t + 1)
                    V.scalar_tensor_tensor(XN[:, node, :], y_ps[:, (unit * CT + t) % 2, 0:D], wgt[:, k:k + 1], XN[:, node, :],
                                           ALU.mult, ALU.add).then_inc(y_used, 1)
                    if k == K2 - 1:
                        dve.wait_ge(y_used, unit * CT + t + 1)
                        measure(dve, link, XN, stats, aggr, node)
                        link.wait()
                        link.note(V.scalar_tensor_tensor(XN[:, node, :], XN[:, node, :], aggr[:, node, 0:1], gam[:, :],
                                                         ALU.subtract, ALU.mult))
            link.wait()
            link(V.tensor_copy(var[:, :], aggr[:, :, 1]))
            inverse_root(dve, link, var[:, :], root[:, :], tmp[:, :], var_ready, std_ready, 6)
            for t in range(NT):
                V.scalar_tensor_tensor(XN[:, t, :], XN[:, t, :], root[:, t:t + 1], X[:, t, :],
                                       ALU.mult, ALU.add).then_inc(out_ready, 1)


_INS = ["x", "src", "dst", "edge_type_32", "edge_weight1", "L0_gnn_weight", "L0_gnn_bias", "L0_ffn_W_gat",
        "L0_ffn_att_src", "L0_ffn_att_dst", "L0_ffn_b_gat", "L0_ffn_ln_gamma", "L0_ffn_ln_beta", "L0_ffn_W1",
        "L0_ffn_b1", "L0_ffn_W2", "L0_ffn_b2", "L0_ffn_edge_index", "L1_gnn_bases", "L1_gnn_w_comp", "L1_ffn_Wr",
        "L1_ffn_br", "L1_ffn_W1", "L1_ffn_b1", "L1_ffn_W2", "L1_ffn_b2", "L1_ffn_gamma", "L1_ffn_beta"]


def kernel(**inputs):
    import numpy as _np
    import concourse.bacc as _bacc
    from concourse import mybir as _mybir
    from concourse.bass_utils import run_bass_kernel_spmd as _run

    nc = _bacc.Bacc("TRN2", target_bir_lowering=False, num_devices=1)
    arrays, aps = {}, {}
    for name in _INS:
        arr = _np.ascontiguousarray(inputs[name])
        arrays[f"in_{name}"] = arr
        aps[name] = nc.dram_tensor(f"in_{name}", arr.shape, _mybir.dt.from_np(arr.dtype), kind="ExternalInput").ap()
    out = nc.dram_tensor("out_0", (N, D), _mybir.dt.float32, kind="ExternalOutput").ap()
    gnn_ffn(nc, aps, out)
    return _run(nc, [arrays], core_ids=[0]).results[0]["out_0"]
```
